# Optimizing a Trainium2 kernel written in Bass

```python
import numpy as np
import jax
import jax.numpy as jnp

def _softmax(x, axis=-1):
    return jax.nn.softmax(x, axis=axis)

def _gelu(x):
    return jax.nn.gelu(x, approximate=True)

def _silu(x):
    return jax.nn.silu(x)

def _sigmoid(x):
    return jax.nn.sigmoid(x)

def _layernorm(x, axis=-1, eps=1e-05):
    m = jnp.mean(x, axis=axis, keepdims=True)
    v = jnp.var(x, axis=axis, keepdims=True)
    return (x - m) / jnp.sqrt(v + eps)

def _scatter_add(tgt, idx, src, axis=0):
    return tgt.at[idx].add(src)

def _segment_sum(src, seg, n):
    return jax.ops.segment_sum(src, seg, n)
kernel_name = 'mk_gps_d1_gnn_r32_bd249a'

def setup_inputs(seed: int=0):
    np.random.seed(seed)
    _w = jnp.asarray

    def _rec_inputs():
        import jax
        import jax.numpy as jnp
        _gk = jax.random.key(seed)
        x = -0.0002117 + 1 * jax.random.normal(jax.random.fold_in(_gk, 1), (3125, 256), jnp.float32)
        src = jax.random.randint(jax.random.fold_in(_gk, 2), (50000,), 0, 3125, jnp.int32)
        dst = jnp.minimum((3125 * jax.random.uniform(jax.random.fold_in(_gk, 3), (50000,)) ** 2.0).astype(jnp.int32), 99999)
        _o = jnp.argsort(dst, stable=True)
        src = src[_o]
        dst = dst[_o]
        edge_weight = jax.random.uniform(jax.random.fold_in(_gk, 12), (50000,), jnp.float32, 0.0, 1)
        return (x, src, dst, edge_weight)
    x, src, dst, edge_weight = _rec_inputs()

    def _L0_gnn_setup():
        import jax, jax.numpy as jnp
        import numpy as np
        N_NODES = 3125
        N_EDGES = 100000
        N_IN = 256
        N_OUT = 256
        key = jax.random.key(seed)
        k1, k2, k3, k4, k5 = jax.random.split(key, 5)
        x = jax.random.normal(k1, (N_NODES, N_IN), dtype=jnp.float32)
        W = jax.random.normal(k2, (N_IN, N_OUT), dtype=jnp.float32) * (1.0 / np.sqrt(N_IN))
        edge_row = jax.random.randint(k3, (N_EDGES,), 0, N_NODES, dtype=jnp.int32)
        edge_col = jax.random.randint(k4, (N_EDGES,), 0, N_NODES, dtype=jnp.int32)
        edge_val = jax.random.uniform(k5, (N_EDGES,), dtype=jnp.float32)
        return {'x': x, 'W': W, 'edge_row': edge_row, 'edge_col': edge_col, 'edge_val': edge_val}
    _L0_gnn_all = _L0_gnn_setup()
    _L0_gnn_in = {k: v for k, v in _L0_gnn_all.items() if k in ('W',)}
    del _L0_gnn_all

    def _L0_mix_setup():
        import jax, jax.numpy as jnp
        import numpy as np
        EMB, HEADS, DEPTH, SEQ, BATCH = (256, 8, 4, 256, 4)
        DH = EMB // HEADS
        FF = 4 * EMB
        EPS = 1e-05

        def _layernorm(x, g, b):
            mu = x.mean(-1, keepdims=True)
            var = ((x - mu) ** 2).mean(-1, keepdims=True)
            return (x - mu) * jax.lax.rsqrt(var + EPS) * g + b

        def _linear_attn(x, Wq, Wk, Wv, Wo, bo):
            b, n, dm = x.shape
            split = lambda t: t.reshape(b, n, HEADS, DH).transpose(0, 2, 1, 3)
            scale = DH ** (-0.25)
            q = jax.nn.softmax(split(x @ Wq) * scale, axis=-1)
            k = jax.nn.softmax(split(x @ Wk) * scale, axis=-2)
            v = split(x @ Wv)
            context = jnp.einsum('bhnd,bhne->bhde', k, v)
            out = jnp.einsum('bhnd,bhde->bhne', q, context)
            out = out.transpose(0, 2, 1, 3).reshape(b, n, dm)
            return out @ Wo + bo

        def _forward(x, Wq, Wk, Wv, Wo, bo, ln1_g, ln1_b, W1, b1, W2, b2, ln2_g, ln2_b):
            for i in range(DEPTH):
                h = _layernorm(x, ln1_g[i], ln1_b[i])
                x = x + _linear_attn(h, Wq[i], Wk[i], Wv[i], Wo[i], bo[i])
                h = _layernorm(x, ln2_g[i], ln2_b[i])
                x = x + (jax.nn.gelu(h @ W1[i] + b1[i], approximate=False) @ W2[i] + b2[i])
            return x
        key = jax.random.key(seed)
        ks = jax.random.split(key, 8)
        w = lambda k, shape: jax.random.normal(k, shape, dtype=jnp.float32) * 0.02
        D = DEPTH
        return {'x': jax.random.normal(ks[0], (BATCH, SEQ, EMB), dtype=jnp.float32), 'Wq': w(ks[1], (D, EMB, EMB)), 'Wk': w(ks[2], (D, EMB, EMB)), 'Wv': w(ks[3], (D, EMB, EMB)), 'Wo': w(ks[4], (D, EMB, EMB)), 'bo': jnp.zeros((D, EMB), jnp.float32), 'ln1_g': jnp.ones((D, EMB), jnp.float32), 'ln1_b': jnp.zeros((D, EMB), jnp.float32), 'W1': w(ks[5], (D, EMB, FF)), 'b1': jnp.zeros((D, FF), jnp.float32), 'W2': w(ks[6], (D, FF, EMB)), 'b2': jnp.zeros((D, EMB), jnp.float32), 'ln2_g': jnp.ones((D, EMB), jnp.float32), 'ln2_b': jnp.zeros((D, EMB), jnp.float32)}
    _L0_mix_all = _L0_mix_setup()
    _L0_mix_in = {k: v for k, v in _L0_mix_all.items() if k in ('Wq', 'Wk', 'Wv', 'Wo', 'bo', 'ln1_g', 'ln1_b', 'W1', 'b1', 'W2', 'b2', 'ln2_g', 'ln2_b')}
    del _L0_mix_all

    def _L0_ffn_setup():
        import jax, jax.numpy as jnp
        import numpy as np
        DIM = 256
        H = 8
        D = 64
        G = 64
        INNER = H * D
        SCALE = D ** (-0.5)
        key = jax.random.key(seed)
        ks = jax.random.split(key, 12)
        B, N = (4, 512)
        x = jax.random.normal(ks[0], (B, N, DIM), dtype=jnp.float32)
        s = lambda fan_in: 1.0 / np.sqrt(fan_in)
        W_fx = jax.random.normal(ks[1], (DIM, INNER), dtype=jnp.float32) * s(DIM)
        b_fx = jnp.zeros((INNER,), dtype=jnp.float32)
        W_x = jax.random.normal(ks[2], (DIM, INNER), dtype=jnp.float32) * s(DIM)
        b_x = jnp.zeros((INNER,), dtype=jnp.float32)
        A = jax.random.normal(ks[3], (G, D), dtype=jnp.float32)
        Q, _ = jnp.linalg.qr(A.T)
        W_slice = Q[:, :G].astype(jnp.float32)
        b_slice = jnp.zeros((G,), dtype=jnp.float32)
        W_q = jax.random.normal(ks[4], (D, D), dtype=jnp.float32) * s(D)
        W_k = jax.random.normal(ks[5], (D, D), dtype=jnp.float32) * s(D)
        W_v = jax.random.normal(ks[6], (D, D), dtype=jnp.float32) * s(D)
        W_out = jax.random.normal(ks[7], (INNER, DIM), dtype=jnp.float32) * s(INNER)
        b_out = jnp.zeros((DIM,), dtype=jnp.float32)
        temperature = jnp.ones((1, H, 1, 1), dtype=jnp.float32) * 0.5
        return {'x': x, 'W_fx': W_fx, 'b_fx': b_fx, 'W_x': W_x, 'b_x': b_x, 'W_slice': W_slice, 'b_slice': b_slice, 'W_q': W_q, 'W_k': W_k, 'W_v': W_v, 'W_out': W_out, 'b_out': b_out, 'temperature': temperature}
    _L0_ffn_all = _L0_ffn_setup()
    _L0_ffn_in = {k: v for k, v in _L0_ffn_all.items() if k in ('W_fx', 'b_fx', 'W_x', 'b_x', 'W_slice', 'b_slice', 'W_q', 'W_k', 'W_v', 'W_out', 'b_out', 'temperature')}
    del _L0_ffn_all
    return {'x': x, 'src': src, 'dst': dst, 'edge_weight': edge_weight, 'L0_gnn_W': _L0_gnn_in['W'], 'L0_mix_Wq': _L0_mix_in['Wq'], 'L0_mix_Wk': _L0_mix_in['Wk'], 'L0_mix_Wv': _L0_mix_in['Wv'], 'L0_mix_Wo': _L0_mix_in['Wo'], 'L0_mix_bo': _L0_mix_in['bo'], 'L0_mix_ln1_g': _L0_mix_in['ln1_g'], 'L0_mix_ln1_b': _L0_mix_in['ln1_b'], 'L0_mix_W1': _L0_mix_in['W1'], 'L0_mix_b1': _L0_mix_in['b1'], 'L0_mix_W2': _L0_mix_in['W2'], 'L0_mix_b2': _L0_mix_in['b2'], 'L0_mix_ln2_g': _L0_mix_in['ln2_g'], 'L0_mix_ln2_b': _L0_mix_in['ln2_b'], 'L0_ffn_W_fx': _L0_ffn_in['W_fx'], 'L0_ffn_b_fx': _L0_ffn_in['b_fx'], 'L0_ffn_W_x': _L0_ffn_in['W_x'], 'L0_ffn_b_x': _L0_ffn_in['b_x'], 'L0_ffn_W_slice': _L0_ffn_in['W_slice'], 'L0_ffn_b_slice': _L0_ffn_in['b_slice'], 'L0_ffn_W_q': _L0_ffn_in['W_q'], 'L0_ffn_W_k': _L0_ffn_in['W_k'], 'L0_ffn_W_v': _L0_ffn_in['W_v'], 'L0_ffn_W_out': _L0_ffn_in['W_out'], 'L0_ffn_b_out': _L0_ffn_in['b_out'], 'L0_ffn_temperature': _L0_ffn_in['temperature']}

def reference(x, src, dst, edge_weight, L0_gnn_W, L0_mix_Wq, L0_mix_Wk, L0_mix_Wv, L0_mix_Wo, L0_mix_bo, L0_mix_ln1_g, L0_mix_ln1_b, L0_mix_W1, L0_mix_b1, L0_mix_W2, L0_mix_b2, L0_mix_ln2_g, L0_mix_ln2_b, L0_ffn_W_fx, L0_ffn_b_fx, L0_ffn_W_x, L0_ffn_b_x, L0_ffn_W_slice, L0_ffn_b_slice, L0_ffn_W_q, L0_ffn_W_k, L0_ffn_W_v, L0_ffn_W_out, L0_ffn_b_out, L0_ffn_temperature):
    import jax
    import jax.numpy as jnp

    def _L0_gnn_ref(x, W, edge_row, edge_col, edge_val):
        import jax, jax.numpy as jnp
        import numpy as np
        N_NODES = 3125
        N_EDGES = 100000
        N_IN = 256
        N_OUT = 256
        support = jnp.matmul(x, W)
        msgs = support[edge_col] * edge_val[:, None]
        out = jax.ops.segment_sum(msgs, edge_row, num_segments=N_NODES)
        return out

    def _L0_mix_ref(x, Wq, Wk, Wv, Wo, bo, ln1_g, ln1_b, W1, b1, W2, b2, ln2_g, ln2_b):
        import jax, jax.numpy as jnp
        import numpy as np
        EMB, HEADS, DEPTH, SEQ, BATCH = (256, 8, 4, 256, 4)
        DH = EMB // HEADS
        FF = 4 * EMB
        EPS = 1e-05

        def _layernorm(x, g, b):
            mu = x.mean(-1, keepdims=True)
            var = ((x - mu) ** 2).mean(-1, keepdims=True)
            return (x - mu) * jax.lax.rsqrt(var + EPS) * g + b

        def _linear_attn(x, Wq, Wk, Wv, Wo, bo):
            b, n, dm = x.shape
            split = lambda t: t.reshape(b, n, HEADS, DH).transpose(0, 2, 1, 3)
            scale = DH ** (-0.25)
            q = jax.nn.softmax(split(x @ Wq) * scale, axis=-1)
            k = jax.nn.softmax(split(x @ Wk) * scale, axis=-2)
            v = split(x @ Wv)
            context = jnp.einsum('bhnd,bhne->bhde', k, v)
            out = jnp.einsum('bhnd,bhde->bhne', q, context)
            out = out.transpose(0, 2, 1, 3).reshape(b, n, dm)
            return out @ Wo + bo

        def _forward(x, Wq, Wk, Wv, Wo, bo, ln1_g, ln1_b, W1, b1, W2, b2, ln2_g, ln2_b):
            for i in range(DEPTH):
                h = _layernorm(x, ln1_g[i], ln1_b[i])
                x = x + _linear_attn(h, Wq[i], Wk[i], Wv[i], Wo[i], bo[i])
                h = _layernorm(x, ln2_g[i], ln2_b[i])
                x = x + (jax.nn.gelu(h @ W1[i] + b1[i], approximate=False) @ W2[i] + b2[i])
            return x
        return _forward(x, Wq, Wk, Wv, Wo, bo, ln1_g, ln1_b, W1, b1, W2, b2, ln2_g, ln2_b)

    def _L0_ffn_ref(x, W_fx, b_fx, W_x, b_x, W_slice, b_slice, W_q, W_k, W_v, W_out, b_out, temperature):
        import jax, jax.numpy as jnp
        import numpy as np
        DIM = 256
        H = 8
        D = 64
        G = 64
        INNER = H * D
        SCALE = D ** (-0.5)
        B, N, _ = x.shape
        fx_mid = (x @ W_fx + b_fx).reshape(B, N, H, D).transpose(0, 2, 1, 3)
        x_mid = (x @ W_x + b_x).reshape(B, N, H, D).transpose(0, 2, 1, 3)
        temp = jnp.clip(temperature, 0.1, 5.0)
        slice_weights = jax.nn.softmax((x_mid @ W_slice + b_slice) / temp, axis=-1)
        slice_norm = slice_weights.sum(axis=2)
        slice_token = jnp.einsum('bhnc,bhng->bhgc', fx_mid, slice_weights)
        slice_token = slice_token / (slice_norm[..., None] + 1e-05)
        q = slice_token @ W_q
        k = slice_token @ W_k
        v = slice_token @ W_v
        attn = jax.nn.softmax(jnp.einsum('bhgc,bhkc->bhgk', q, k) * SCALE, axis=-1)
        out_slice = jnp.einsum('bhgk,bhkc->bhgc', attn, v)
        out_x = jnp.einsum('bhgc,bhng->bhnc', out_slice, slice_weights)
        out_x = out_x.transpose(0, 2, 1, 3).reshape(B, N, INNER)
        return out_x @ W_out + b_out
    xn = _layernorm(x, axis=-1)
    x = x + _L0_gnn_ref(xn, L0_gnn_W, src, dst, edge_weight) + _L0_mix_ref(xn[None], L0_mix_Wq, L0_mix_Wk, L0_mix_Wv, L0_mix_Wo, L0_mix_bo, L0_mix_ln1_g, L0_mix_ln1_b, L0_mix_W1, L0_mix_b1, L0_mix_W2, L0_mix_b2, L0_mix_ln2_g, L0_mix_ln2_b)[0]
    x = x + _L0_ffn_ref(_layernorm(x, axis=-1)[None], L0_ffn_W_fx, L0_ffn_b_fx, L0_ffn_W_x, L0_ffn_b_x, L0_ffn_W_slice, L0_ffn_b_slice, L0_ffn_W_q, L0_ffn_W_k, L0_ffn_W_v, L0_ffn_W_out, L0_ffn_b_out, L0_ffn_temperature)[0]
    return x

_drawn_inputs = setup_inputs


def setup_inputs(seed=0):
    import zlib

    import numpy as np

    out = dict(_drawn_inputs(seed))
    spreads = {'L0_mix_bo': (0.0, 0.1),
     'L0_mix_ln1_g': (1.0, 0.6),
     'L0_mix_ln1_b': (0.0, 0.8),
     'L0_mix_b1': (0.0, 0.313),
     'L0_mix_b2': (0.0, 0.1),
     'L0_mix_ln2_g': (1.0, 0.6),
     'L0_mix_ln2_b': (0.0, 0.8),
     'L0_ffn_b_fx': (0.0, 0.285),
     'L0_ffn_b_x': (0.0, 0.8),
     'L0_ffn_b_slice': (0.0, 2.0),
     'L0_ffn_b_out': (0.0, 0.433),
     'L0_ffn_temperature': (0.5, 0.6)}
    factors = {'L0_mix_Wq': 8.0,
     'L0_mix_Wk': 8.0,
     'L0_mix_Wv': 4.185,
     'L0_mix_Wo': 3.892,
     'L0_ffn_W_x': 8.0,
     'L0_ffn_W_slice': 8.0,
     'L0_ffn_W_q': 8.0,
     'L0_ffn_W_k': 8.0}
    for name, (base, spread) in spreads.items():
        noise = np.random.default_rng([zlib.crc32(name.encode()), seed]).standard_normal(out[name].shape)
        drawn = base * np.exp(spread * noise) if base else spread * noise
        out[name] = jnp.asarray(drawn.astype(out[name].dtype))
    for name, factor in factors.items():
        out[name] = (out[name] * factor).astype(out[name].dtype)
    return out
```

```python
from contextlib import ExitStack, contextmanager

import concourse.bass as bass
from concourse import mybir

F32 = mybir.dt.float32
I32 = mybir.dt.int32
ALU = mybir.AluOpType
ACT = mybir.ActivationFunctionType
AX_X = mybir.AxisListType.X

N = 3125
D = 256
T = 125
NT = N // T
G = 5
NG = NT // G
GW = G * T
KC = D // 128
LAYERS = 4
HEADS, DH = 8, 32
FF = 4 * D
FB = FF // 128
EPS = 1e-5
QSCALE = DH ** -0.25
E = 50000
UNIT = 8
EC = -(-E // (128 * UNIT)) * UNIT
NCH = -(-(E + NT * 127) // (128 * UNIT)) * UNIT
RC = NCH + 2
SET = UNIT // 2
FH, FD, FG = 8, 64, 64
INNER = FH * FD
HALF = [(0, 3), (3, 2)]
MAGIC = float(0x5F3759DF)

COUNTS = {
    "norm_in": {"xh_ready": G, "xt_ready": G, "xt_done": G, "dve_step": 15},
    "norm_a": {"xh_ready": G, "xt_ready": G, "xt_done": G, "dve_step": 15},
    "norm_c": {"xh_ready": G, "xt_ready": G, "xt_done": G, "dve_step": 16},
    "norm_f": {"xh_ready": G, "xt_ready": G, "xt_done": G, "dve_step": 16},
    "support": {"row_ready": G, "row_done": G, "sup_stored": 16},
    "keys": {"wide_ready": 2 * KC, "wide_done": 2 * KC, "dve_step": 1},
    "queries": {"row_ready": G, "row_done": G, "qz_ready": 1, "qe_ready": 1, "qn_ready": 1, "dve_step": 3},
    "turn_q": {"qt_ready": G, "qt_done": G},
    "kmax": {"kmax_ready": 1, "dve_step": 1},
    "context": {"kexp": KC, "bxh_ready": G, "kt_ready": G, "kt_done": G, "g_acc": G},
    "fold": {"g_closed": 1, "gs_ready": 1, "cm_ready": 1, "cm_done": 1, "m_ready": 1, "ms_done": 1, "dve_step": 2},
    "attend": {"qs_ready": 1, "row_ready": G, "row_done": G},
    "up0": {"wide_ready": FB, "wide_done": FB},
    "up1": {"wide_ready": FB, "wide_done": FB},
    "down0": {"row_ready": HALF[0][1], "row_done": HALF[0][1]},
    "down1": {"row_ready": HALF[1][1], "row_done": HALF[1][1]},
    "prep_qk": {"w_qk": 16, "lb_ready": 1, "bqk_ready": 1, "qk_ready": 1},
    "prep_rest": {"w_rest": 80, "bv_ready": 1, "bvm_ready": 1, "b2m_ready": 1, "rest_ready": 1, "dve_step": 1},
    "edges": {"hot_ready": UNIT, "agg_ready": UNIT, "agg_done": UNIT},
    "logits": {"row_ready": G, "row_done": G, "sz_ready": G, "se_ready": G, "s_ready": G, "tok": G, "s_summed": G,
               "dve_step": 3 * G},
    "finish": {"sc_ready": G, "st_ready": G, "st_done": G, "row_ready": G, "row_done": G, "out_done": 16,
               "dve_step": 1},
}


class Count:

    def __init__(self, start=0):
        self.base, self.own = {}, {sem: start for stage in COUNTS.values() for sem in stage}

    def __call__(self, sem):
        b, o = self.base.get(sem, 0), self.own.get(sem, 0)
        return o if isinstance(b, int) and b == 0 else b + o

    def over(self, *stages):
        for stage in stages:
            for sem, n in COUNTS[stage].items():
                self.own[sem] = self.own.get(sem, 0) + n

    def rest(self, stage):
        for sem, n in COUNTS[stage].items():
            if sem != "dve_step":
                self.own[sem] = self.own.get(sem, 0) + n

    @contextmanager
    def loop(self, eng, lo, hi, stages):
        per = Count()
        per.over(*stages)
        per.own = {sem: n for sem, n in per.own.items() if n}
        base, own = dict(self.base), dict(self.own)
        with eng.Fori(lo, hi) as r:
            turn = r if lo == 0 else r - lo
            for sem, n in per.own.items():
                self.base[sem] = turn * n + self(sem)
                self.own[sem] = 0
            yield r
        for sem in per.own:
            assert self.own[sem] == per.own[sem], (sem, self.own[sem], per.own[sem])
        self.base, self.own = base, own
        for sem, n in per.own.items():
            self.own[sem] = own.get(sem, 0) + n * (hi - lo)


def wait(eng, sem, value):
    if not isinstance(value, int) or value > 1:
        eng.wait_ge(sem, value)


def apart(eng, sem):
    eng.sem_inc(sem, 1)


A_STAGES = ["norm_a", "keys", "queries", "turn_q"]
FRONT = ["attend", "norm_c"]
FFN_STAGES = ["up0", "up1", "down0", "down1"]
MIX = ["prep_rest"] + ["context"] * NG + ["fold"]
LAYER_STAGES = MIX + ["prep_qk"] + (FRONT + FFN_STAGES + A_STAGES) * NG + ["kmax"]


def layers(eng, c, stage):
    def turn(l, g, front, back):
        stage["up"](l, g, 0)
        if back:
            stage["norm_a"](g - 1)
        stage["up"](l, g, 1)
        if back:
            stage["keys"](g - 1)
            stage["queries"](g - 1)
        stage["down"](g, 0)
        if front:
            stage["attend"](g + 1)
        stage["down"](g, 1)
        if back:
            stage["turn_q"](g - 1)
        if front:
            stage["norm_c"](g + 1)

    def layer(l, more):
        stage["prep_rest"](l)
        with c.loop(eng, 0, NG, ["context"]) as g:
            stage["context"](g)
        stage["fold"]()
        if more:
            stage["prep_qk"](l + 1)
        stage["attend"](0)
        stage["norm_c"](0)
        turn(l, 0, True, False)
        with c.loop(eng, 1, NG - 1, FFN_STAGES + FRONT + A_STAGES * more) as g:
            turn(l, g, True, more)
        turn(l, NG - 1, False, more)
        if more:
            stage["norm_a"](NG - 1)
            stage["keys"](NG - 1)
            stage["queries"](NG - 1)
            stage["turn_q"](NG - 1)
            stage["kmax"]()

    stage["prep_qk"](0)
    with c.loop(eng, 0, NG, ["norm_in", "support"]) as g:
        stage["norm_in"](g)
        stage["support"](g)
    with c.loop(eng, 0, NG, A_STAGES) as g:
        stage["norm_a"](g)
        stage["keys"](g)
        stage["queries"](g)
        stage["turn_q"](g)
    stage["kmax"]()
    with c.loop(eng, 0, LAYERS - 1, LAYER_STAGES) as l:
        layer(l, True)
    layer(LAYERS - 1, False)


def gps_layer(nc, x, src, dst, ew, w_gnn, w_qk, w_vo, w_1, w_2, cols, b_o, b_2, w_fx, w_xt, w_slice,
              b_slice, b_fx, b_x, w_q, w_k, w_v, w_out, b_out, temp, out):
    x_t = x.rearrange("(t p) c -> p t c", p=T)
    out_t = out.rearrange("(t p) c -> p t c", p=T)
    sup_d = nc.dram_tensor("support_rows", (N, D), F32).ap()
    rec_d = nc.dram_tensor("edge_records", (128 * RC, 4), F32).ap()
    sup_t = sup_d.rearrange("(t p) c -> p t c", p=T)

    with ExitStack() as ctx:
        def sb(name, shape, dt=F32):
            return ctx.enter_context(nc.sbuf_tensor(name, shape, dt))

        X = sb("X", [T, NT, D])
        AGG = sb("AGG", [T, NT, D])
        big = sb("big", [128, NT * INNER])
        KX = big[:, 0:KC * N].rearrange("p (k n) -> p k n", k=KC)
        QT = big[:, KC * N:2 * KC * N].rearrange("p (k n) -> p k n", k=KC)
        S = big[0:T, :].rearrange("p (t s) -> p t s", t=NT)
        W1 = sb("W1", [128, KC, FF])
        W2 = sb("W2", [128, FB, D])
        UT = [sb(f"UT{h}", [128, FB, n * T]) for h, (_, n) in enumerate(HALF)]
        WQK = sb("WQK", [128, KC, 2 * D])
        WVO = sb("WVO", [128, KC, 2 * D])
        WG = sb("WG", [128, KC, D])
        COLS = sb("COLS", [128, LAYERS * 16])
        XH = sb("XH", [T, G, D])
        XT = sb("XT", [128, KC, GW])
        QS = sb("QS", [128, KC, GW])
        KE = QS
        QZ = sb("QZ", [T, G, D])
        KT = sb("KT", [T, 2, D])
        GS = sb("GS", [128, KC, D])
        CM = sb("CM", [128, D])
        MS = sb("MS", [128, KC, D])
        B2M = sb("B2M", [128, KC, D])
        BVM = sb("BVM", [128, D])
        LB = sb("LB", [128, KC, T])
        BQ = sb("BQ", [T, D])
        BK = sb("BK", [128, KC])
        BV = sb("BV", [128, KC])
        B1 = sb("B1", [128, FB])
        BB2 = sb("BB2", [T, D])
        BO = sb("BO", [1, D])
        MASK = sb("MASK", [128, D])
        ident = sb("ident", [128, 128])
        ones = sb("ones", [128, 128])
        eighth = sb("eighth", [1, 128])
        ST = sb("ST", [T, G, 6])
        MV = sb("MV", [T, G, 2])
        NW = sb("NW", [T, 3, G])
        RSTD = sb("RSTD", [T, NT])
        NMR = sb("NMR", [T, NT])
        QM = sb("QM", [T, G * HEADS])
        MX = sb("MX", [128, KC, NG])
        KB = sb("KB", [128, KC])
        KS = sb("KS", [128, KC, NG])
        RS = sb("RS", [128, 2, KC])
        REC = sb("REC", [128, RC * 4])
        REC3 = REC[:, :].rearrange("p (c r) -> p c r", r=4)
        MSG = sb("MSG", [128, UNIT, D])
        IDS = sb("IDS", [128, UNIT], I32)
        HOT = sb("HOT", [128, 2, T])
        SLOT = sb("SLOT", [128, 2, SET, 4])
        AT = sb("AT", [128, 2, SET], I32)
        POSI = sb("POSI", [128, EC], I32)
        IOTA = sb("IOTA", [128, 512])
        BLK = sb("BLK", [1, NCH], I32)

        TRI = CM[:, 0:128]
        ENDC = sb("ENDC", [32, 4])
        NB = NT + 1
        BT = sb("BT", [128, NB])
        zeros = sb("zeros", [1, INNER])

        u0 = UT[0][:, :, :].rearrange("p a b -> p (a b)")
        u1 = UT[1][:, :, :].rearrange("p a b -> p (a b)")
        SRC, DST, EW = u0[:, 0:EC].bitcast(I32), u0[:, 400:400 + EC].bitcast(I32), u0[:, 800:800 + EC]
        SRCF, LOC, BKT = u0[:, 1200:1200 + EC], u0[:, 1600:1600 + EC], u0[:, 2000:2000 + EC]
        CNT, OFF, TOT = u0[:, 2400:2432], u0[:, 2440:2472], u0[:, 2480:2512]
        END, BASE = u0[:, 2520:2552], u0[:, 2560:2592]
        TOTI = u0[:, 2600:2632].bitcast(I32)
        HIT, SCAN, RANK = u1[:, 0:EC], u1[:, 400:400 + EC], u1[:, 800:800 + EC]
        POS, LANE = u1[:, 1200:1200 + EC].bitcast(I32), u1[:, 1600:1600 + EC].bitcast(I32)
        PAST = KX[0:32, 0, 0:NCH]
        REC0 = REC[:, 0:EC * 4].rearrange("p (c r) -> p c r", r=4)

        WXT = QS[:, :, :].rearrange("p k n -> p (k n)")[:, 0:4 * D].rearrange("p (j c) -> p j c", j=4)
        WXS = W1[:, :, 0:INNER]
        WFX = W1[:, :, INNER:2 * INNER]
        M2 = W2[:, 0:4, :]
        BOUT = W2[0:T, 4, :]
        BD = W2[:, 5, 0:128]
        TEMP = W2[:, 5, 128:136]
        TI = W2[:, 5, 136:144]
        BXC = W2[:, 5, 144:148]
        LBX = W2[:, 6:8, :].rearrange("p a b -> p (a b)")[:, 0:4 * T].rearrange("p (j t) -> p j t", j=4)
        LBI = u1[0:T, 0:INNER]
        BSL = u1[0:T, INNER:INNER + FG]
        SZ = [u1[0:T, 600:600 + INNER], u1[0:T, 1200:1200 + INNER]]
        SMX = QM[:, 0:FH]
        SSUM = GS[0:T, :, :].rearrange("p k n -> p (k n)")
        SC = [QZ[:, 0:2, :].rearrange("p a b -> p (a b)"), QZ[:, 2:4, :].rearrange("p a b -> p (a b)")]
        STT = [u0[:, 0:4 * T].rearrange("p (j t) -> p j t", j=4), u0[:, 512:512 + 4 * T].rearrange("p (j t) -> p j t", j=4)]
        YT = WVO[:, :, :]
        w8 = lambda a: a.rearrange("p (h c) -> p h c", h=FH)
        qk_ = WQK[0:FG, :, :].rearrange("p k n -> p (k n)")
        TK, TKT = qk_[:, 0:INNER], qk_[:, INNER:2 * INNER]
        gx = XT[0:FG, :, :].rearrange("p k n -> p (k n)")
        BFX, FQT = u0[0:FG, 2104:2104 + INNER], gx[:, INNER:2 * INNER]
        qx = QS[0:FG, :, :].rearrange("p k n -> p (k n)")
        FKT, FV = qx[:, 0:INNER], qx[:, INNER:2 * INNER]
        gs_ = GS[0:FG, :, :].rearrange("p k n -> p (k n)")
        AW = gs_[:, 0:INNER]
        ms_ = MS[0:FG, :, :].rearrange("p k n -> p (k n)")
        AWT = ms_[:, 0:INNER]
        OP = u0[0:FG, 1040:1040 + FH * 128].rearrange("p (h a) -> p h a", h=FH)
        WOUT = MSG[0:FG, :, :]
        WQKV = B2M[0:FG, :, :].rearrange("p k n -> p (k n)")[:, 0:3 * FD]
        DEN, AMX = sb("DEN", [FG, FH]), sb("AMX", [FG, FH])
        SDEN = QM[:, FH:2 * FH]
        NRM = sb("NRM", [FG, FH])

        P = [ctx.enter_context(nc.psum_tensor(f"P{i}", [128, 512], F32)) for i in range(8)]
        WIDE, ROW, TP, QP, ACC = [P[0], P[1]], [P[2], P[3]], P[4], P[5], [P[6], P[7]]

        def turned(bank):
            return bank[:, 0:256].rearrange("p (k t) -> p k t", k=KC)[:, :, 0:T]

        names = sorted({n for cs in COUNTS.values() for n in cs} | {
            "consts", "x_in", "w_g", "cols_in", "edges_in", "dve_step", "pool_step", "pe_step", "e_records", "e_counted",
            "e_offset", "e_placed", "e_ends", "e_past", "e_passed", "e_blocks", "e_zero", "e_zeroed", "e_back",
            "f_in", "f_bd", "f_lbx", "f_fold", "f_ready", "f_gone", "y_ready", "n_ready", "tk_ready", "tk_done",
            "tkt_ready", "tkt_done", "qkv_ready", "qkv_done", "aw_ready", "az_ready", "ae_ready", "aw_done",
            "awt_ready", "awt_done", "o_ready", "o_done", "m2_ready", "m2_done", "ssum_zero", "slots", "ids_ready",
            "e_bucketed", "e_rank", "dve_waited", "pool_waited"})
        sem = {n: ctx.enter_context(nc.semaphore(n)) for n in names}
        msg_in = [ctx.enter_context(nc.semaphore(f"msg_in{i}")) for i in range(UNIT)]
        sent = [ctx.enter_context(nc.semaphore(f"sent{i}")) for i in range(2)]
        block = ctx.enter_context(nc.Block())

        def span(at, n):
            return slice(at, at + n) if isinstance(at, int) else bass.ds(at, n)

        @block.sync
        def _(sp):
            for n in sorted({n for stage in COUNTS.values() for n in stage}):
                sp.sem_inc(sem[n], 1)
            sp.sem_inc(sem["e_rank"], 1)
            c = Count(1)
            sp.dma_start(SRC, src).then_inc(sem["edges_in"], 16)
            sp.dma_start(DST, dst).then_inc(sem["edges_in"], 16)
            sp.dma_start(EW, ew).then_inc(sem["edges_in"], 16)
            sp.dma_start(AGG[:, :, :], x_t).then_inc(sem["x_in"], 16)
            sp.dma_start(WG[:, :, :], w_gnn).then_inc(sem["w_g"], 16)
            sp.dma_start(COLS[:, :], cols).then_inc(sem["cols_in"], 16)
            sp.wait_ge(sem["e_zero"], 1)
            sp.dma_start(rec_d.rearrange("(p c) r -> p (c r)", p=128), REC[:, :]).then_inc(sem["e_zeroed"], 16)

            def prep_qk(l):
                wait(sp, sem["row_done"], c("row_done"))
                sp.dma_start(WQK[:, :, :], w_qk[span(l, 1)].rearrange("l p k n -> p (l k) n")).then_inc(sem["w_qk"], 16)
                c.over("prep_qk")

            def prep_rest(l):
                wait(sp, sem["row_done"], c("row_done"))
                for buf, w in ((WVO, w_vo), (W1, w_1), (W2, w_2)):
                    sp.dma_start(buf[:, :, :], w[span(l, 1)].rearrange("l p k n -> p (l k) n")).then_inc(sem["w_rest"], 16)
                sp.dma_start(BO[:, :], b_o[span(l, 1), :]).then_inc(sem["w_rest"], 16)
                sp.dma_start(BB2[:, :], b_2[span(l, 1), :].broadcast_to([T, D])).then_inc(sem["w_rest"], 16)
                c.over("prep_rest")

            def support(g):
                sp.wait_ge(sem["row_done"], c("row_done") + G)
                sp.dma_start(sup_t[:, span(g * G, G), :], QZ[:, :, :]).then_inc(sem["sup_stored"], 16)
                c.over("support")

            def nothing(*names_):
                return lambda *a: c.over(*names_)

            layers(sp, c, {
                "prep_qk": prep_qk, "prep_rest": prep_rest, "support": support, "norm_in": nothing("norm_in"),
                "norm_a": nothing("norm_a"), "norm_c": nothing("norm_c"), "keys": nothing("keys"),
                "queries": nothing("queries"), "turn_q": nothing("turn_q"), "kmax": nothing("kmax"),
                "context": nothing("context"), "fold": nothing("fold"), "attend": nothing("attend"),
                "up": lambda l, g, h: c.over(f"up{h}"), "down": lambda g, h: c.over(f"down{h}")})

            for i in range(2):
                sp.wait_ge(sent[i], 16 * EC // 2)
            sp.dma_start(REC[:, :], rec_d.rearrange("(p c) r -> p (c r)", p=128)).then_inc(sem["e_back"], 16)

            sp.wait_ge(sem["row_done"], c("row_done"))
            sp.wait_ge(sem["agg_done"], NCH + 1)
            for a, b in ((WXT, w_xt), (WFX, w_fx), (BOUT, b_out.broadcast_to([T, D])), (TEMP, temp.broadcast_to([128, FH])),
                         (BXC, b_x), (BSL, b_slice.broadcast_to([T, FG])), (WOUT, w_out),
                         (BFX, b_fx.broadcast_to([FG, INNER])),
                         (WQKV[:, 0:FD], w_q), (WQKV[:, FD:2 * FD], w_k), (WQKV[:, 2 * FD:3 * FD], w_v)):
                sp.dma_start(a, b).then_inc(sem["f_in"], 16)
            sp.wait_ge(sem["f_bd"], 1)
            for i in range(2):
                sp.dma_start(BD[FD * i:FD * (i + 1), FG * i:FG * (i + 1)], w_slice).then_inc(sem["f_in"], 16)
            c.over(*["norm_f", "logits"] * NG)
            with c.loop(sp, 0, NG, ["finish"]) as g:
                sp.wait_ge(sem["row_done"], c("row_done") + G)
                sp.dma_start(out_t[:, span(g * G, G), :], X[:, span(g * G, G), :]).then_inc(sem["out_done"], 16)
                c.over("finish")
            sp.wait_ge(sem["out_done"], 16 * NG + 1)

        F_LOADS = 13 * 16
        MIXER = ["prep_qk"] + ["norm_in", "support"] * NG + A_STAGES * NG + ["kmax"] + LAYER_STAGES * (LAYERS - 1) + MIX + (FRONT + FFN_STAGES) * NG

        @block.gpsimd
        def _(pool):
            done = [0]

            def step(ins):
                done[0] += 1
                ins.then_inc(sem["pool_step"], 1)
                pool.wait_ge(sem["pool_step"], done[0])

            pool.memset(REC[:, :], 0.0).then_inc(sem["e_zero"], 1)
            step(pool.memset(ones[:, :], 1.0))
            step(pool.memset(MASK[:, :], 1.0))
            step(pool.memset(eighth[:, :], 1.0 / HEADS))
            step(pool.iota(IOTA[:, :], pattern=[[1, 512]], base=0, channel_multiplier=0,
                           allow_small_or_imprecise_dtypes=True))
            step(pool.affine_select(out=ident[:, :], in_=ones[:, :], compare_op=ALU.is_equal, fill=0.0,
                                    base=0, pattern=[[-1, 128]], channel_multiplier=1))
            step(pool.affine_select(out=TRI[:, :], in_=ones[:, :], compare_op=ALU.is_gt, fill=0.0,
                                    base=0, pattern=[[1, 128]], channel_multiplier=-1))
            for k in range(KC):
                mk = MASK[:, k * 128:(k + 1) * 128].rearrange("p (h d) -> p h d", d=DH)
                step(pool.affine_select(out=mk, in_=mk, compare_op=ALU.is_ge, fill=0.0, base=0,
                                        pattern=[[-DH, 128 // DH], [0, DH]], channel_multiplier=1))
                step(pool.affine_select(out=mk, in_=mk, compare_op=ALU.is_ge, fill=0.0, base=DH - 1,
                                        pattern=[[DH, 128 // DH], [0, DH]], channel_multiplier=-1))
            pool.memset(zeros[:, :], 0.0).then_inc(sem["consts"], 1)
            pool.wait_ge(sem["edges_in"], 48)
            step(pool.tensor_copy(SRCF, SRC))
            step(pool.tensor_scalar(LOC.bitcast(I32), SRCF, 1.0 / T, -(T - 1) / (2.0 * T), ALU.mult, ALU.add))
            step(pool.tensor_copy(BKT, LOC.bitcast(I32)))
            step(pool.tensor_scalar(BKT, BKT, float(T), None, ALU.mult))
            step(pool.tensor_tensor(LOC, SRCF, BKT, ALU.subtract))
            pool.iota(BT[:, :], pattern=[[T, NB]], base=0, channel_multiplier=0,
                      allow_small_or_imprecise_dtypes=True).then_inc(sem["e_bucketed"], 1)
            pool.wait_ge(sem["e_zeroed"], 16)
            step(pool.tensor_copy(REC0[:, :, 0].bitcast(I32), DST))
            step(pool.tensor_copy(REC0[:, :, 1], LOC))
            pool.tensor_copy(REC0[:, :, 2], EW).then_inc(sem["e_records"], 1)

            pool.wait_ge(sem["e_placed"], 1)
            pool.wait_ge(sem["e_records"], 1)
            def scatter(r):
                for i in range(2):
                    if not isinstance(r, int):
                        pool.wait_ge(sent[i], r * (16 * SET))
                    pool.tensor_copy(AT[:, i, :], POSI[:, span(r * UNIT + i * SET, SET)]).then_inc(sem["slots"], 1)
                    pool.tensor_copy(SLOT[:, i, :, :], REC0[:, span(r * UNIT + i * SET, SET), :]).then_inc(sem["slots"], 1)
                    pool.wait_ge(sem["slots"], r * 4 + 2 * i + 2)
                    apart(pool, sem["pool_waited"])
                    for j in range(SET):
                        pool.indirect_dma_start(rec_d, bass.IndirectOffsetOnAxis(ap=AT[:, i, j:j + 1], axis=0),
                                                SLOT[:, i, j, :], None).then_inc(sent[i], 16)
            scatter(0)
            with pool.Fori(1, EC // UNIT) as r:
                scatter(r)

            pool.wait_ge(sem["e_back"], 16)
            pool.wait_ge(sem["sup_stored"], 16 * NG + 1)
            with pool.Fori(0, NCH // UNIT) as r:
                pool.wait_ge(sem["agg_ready"], r * UNIT + 1)
                pool.tensor_copy(IDS[:, :], REC3[:, bass.ds(r * UNIT, UNIT), 0].bitcast(I32)).then_inc(sem["ids_ready"], 1)
                pool.wait_ge(sem["ids_ready"], r + 1)
                apart(pool, sem["pool_waited"])
                for i in range(UNIT):
                    pool.indirect_dma_start(MSG[:, i, :], None, sup_d,
                                            bass.IndirectOffsetOnAxis(ap=IDS[:, i:i + 1], axis=0)).then_inc(msg_in[i], 16)

            c = Count(1)
            c.over(*MIXER)
            pool.memset(SSUM, 0.0).then_inc(sem["ssum_zero"], 1)
            pool.wait_ge(sem["ssum_zero"], 1)
            with c.loop(pool, 0, NG, ["norm_f", "logits"]) as g:
                for i in range(G):
                    pool.wait_ge(sem["s_ready"], c("s_ready") + i + 1)
                    pool.wait_ge(sem["s_summed"], c("s_summed") + i)
                    pool.tensor_tensor(SSUM, SSUM, S[:, span(g * G + i, 1), :].rearrange("p a s -> p (a s)"),
                                       ALU.add).then_inc(sem["s_summed"], 1)
                c.over("norm_f", "logits")
            with c.loop(pool, 0, NG, ["finish"]) as g:
                for i in range(G):
                    pool.wait_ge(sem["st_ready"], c("st_ready") + max(i - 1, 0))
                    pool.tensor_copy(SC[i % 2], S[:, span(g * G + i, 1), :].rearrange("p a s -> p (a s)")).then_inc(sem["sc_ready"], 1)
                c.over("finish")

        @block.tensor
        def _(pe):
            c = Count(1)

            def row_free(i):
                if i == 0:
                    wait(pe, sem["row_done"], c("row_done"))
                elif i >= 2:
                    pe.wait_ge(sem["row_done"], c("row_done") + i - 1)

            def wide_free(i):
                if i == 0:
                    wait(pe, sem["wide_done"], c("wide_done"))
                elif i >= 2:
                    pe.wait_ge(sem["wide_done"], c("wide_done") + i - 1)

            def norm(name):
                for i in range(G):
                    pe.wait_ge(sem["xh_ready"], c("xh_ready") + i + 1)
                    wait(pe, sem["xt_done"], c("xt_done") + i)
                    for k in range(KC):
                        mm = pe.transpose(turned(TP)[:, k, :], XH[:, i, k * 128:(k + 1) * 128], ident[0:T, 0:T])
                    mm.then_inc(sem["xt_ready"], 1)
                c.over(name)

            def rows(lhs, rhs):
                for i in range(G):
                    row_free(i)
                    for k in range(KC):
                        mm = pe.matmul(ROW[i % 2][0:T, 0:D], lhs(k, i), rhs(k), start=(k == 0), stop=(k == KC - 1))
                    mm.then_inc(sem["row_ready"], 1)

            def support(g):
                pe.wait_ge(sem["xt_done"], c("xt_done"))
                rows(lambda k, i: XT[:, k, i * T:(i + 1) * T], lambda k: WG[:, k, :])
                c.over("support")

            def prep_qk(l):
                pe.wait_ge(sem["w_qk"], c("w_qk") + 16)
                pe.wait_ge(sem["lb_ready"], c("lb_ready") + 1)
                wait(pe, sem["row_done"], c("row_done"))
                for k in range(KC):
                    pe.matmul(ROW[0][0:T, 0:D], LB[:, k, :], WQK[:, k, 0:D], start=(k == 0), stop=(k == KC - 1))
                for m in range(KC):
                    for k in range(KC):
                        mm = pe.matmul(ROW[1][:, m:m + 1], WQK[:, k, D + m * 128:D + (m + 1) * 128], LB[:, k, 0:1],
                                       start=(k == 0), stop=(k == KC - 1))
                mm.then_inc(sem["bqk_ready"], 1)
                pe.wait_ge(sem["qk_ready"], c("qk_ready") + 1)
                c.over("prep_qk")

            def keys(g):
                n = 0
                for off, tiles in HALF:
                    pe.wait_ge(sem["xt_done"], c("xt_done") - G + off + tiles)
                    for m in range(KC):
                        wide_free(n)
                        for k in range(KC):
                            mm = pe.matmul(WIDE[n % 2][:, 0:tiles * T], WQK[:, k, D + m * 128:D + (m + 1) * 128],
                                           XT[:, k, off * T:(off + tiles) * T], start=(k == 0), stop=(k == KC - 1))
                        mm.then_inc(sem["wide_ready"], 1)
                        n += 1
                c.over("keys")

            def queries(g):
                rows(lambda k, i: XT[:, k, i * T:(i + 1) * T], lambda k: WQK[:, k, 0:D])
                c.over("queries")

            def turn_q(g):
                pe.wait_ge(sem["qn_ready"], c("qn_ready"))
                for i in range(G):
                    wait(pe, sem["qt_done"], c("qt_done") + i)
                    for k in range(KC):
                        mm = pe.transpose(turned(QP)[:, k, :], QZ[:, i, k * 128:(k + 1) * 128], ident[0:T, 0:T])
                    mm.then_inc(sem["qt_ready"], 1)
                c.over("turn_q")

            def prep_rest(l):
                pe.wait_ge(sem["w_rest"], c("w_rest") + 80)
                wait(pe, sem["row_done"], c("row_done"))
                ps = ROW[0]
                for j in range(KC):
                    for k in range(KC):
                        pe.matmul(ps[:, j:j + 1], WVO[:, k, j * 128:(j + 1) * 128], COLS[:, span(l * 16 + 2 + k, 1)],
                                  start=(k == 0), stop=(k == KC - 1))
                for j in range(FB):
                    for k in range(KC):
                        mm = pe.matmul(ps[:, 8 + j:9 + j], W1[:, k, j * 128:(j + 1) * 128], COLS[:, span(l * 16 + 6 + k, 1)],
                                       start=(k == 0), stop=(k == KC - 1))
                mm.then_inc(sem["bv_ready"], 1)
                pe.wait_ge(sem["bvm_ready"], c("bvm_ready") + 1)
                for j in range(KC):
                    pe.matmul(ROW[1][:, j * D:(j + 1) * D], BVM[:, j * 128:(j + 1) * 128], WVO[:, j, D:2 * D],
                              start=True, stop=False)
                    mm = pe.matmul(ROW[1][:, j * D:(j + 1) * D], eighth[:, :], BO[:, :], start=False, stop=True)
                mm.then_inc(sem["b2m_ready"], 1)
                pe.wait_ge(sem["rest_ready"], c("rest_ready") + 1)
                for m in range(KC):
                    pe.matmul(ACC[m][:, 0:D], zeros[:, 0:128], zeros[:, 0:D], start=True, stop=False,
                              skip_group_check=True)
                c.over("prep_rest")

            def context(g):
                def turn(i):
                    pe.wait_ge(sem["kexp"], c("kexp") + KC)
                    if i == 0:
                        wait(pe, sem["kt_done"], c("kt_done"))
                    elif i >= 2:
                        pe.wait_ge(sem["kt_done"], c("kt_done") + i - 1)
                    bank = [TP, QP][i % 2]
                    for k in range(KC):
                        mm = pe.transpose(bank[0:T, k * 128:(k + 1) * 128], KE[:, k, i * T:(i + 1) * T], ident[:, :])
                    mm.then_inc(sem["kt_ready"], 1)

                def add(i):
                    pe.wait_ge(sem["kt_done"], c("kt_done") + i + 1)
                    pe.wait_ge(sem["bxh_ready"], c("bxh_ready") + i + 1)
                    for m in range(KC):
                        mm = pe.matmul(ACC[m][:, 0:D], XH[:, i, m * 128:(m + 1) * 128], KT[:, i % 2, :],
                                       start=False, stop=False, skip_group_check=True)
                    mm.then_inc(sem["g_acc"], 1)
                turn(0)
                for i in range(1, G):
                    turn(i)
                    add(i - 1)
                add(G - 1)
                c.over("context")


            def fold():
                for m in range(KC):
                    mm = pe.matmul(ACC[m][:, 0:D], zeros[:, 0:128], zeros[:, 0:D], start=False, stop=True,
                                   skip_group_check=True)
                mm.then_inc(sem["g_closed"], 1)
                pe.wait_ge(sem["gs_ready"], c("gs_ready") + 1)
                wait(pe, sem["kt_done"], c("kt_done"))
                for j in range(KC):
                    cols_ = slice(j * 128, (j + 1) * 128)
                    for k in range(KC):
                        mm = pe.matmul(TP[:, cols_], WVO[:, k, cols_], GS[:, k, cols_], start=(k == 0), stop=(k == KC - 1))
                mm.then_inc(sem["cm_ready"], 1)
                pe.wait_ge(sem["cm_done"], c("cm_done") + 1)
                for j in range(KC):
                    mm = pe.matmul(ROW[j][:, 0:D], CM[:, j * 128:(j + 1) * 128], WVO[:, j, D:2 * D], start=True, stop=True)
                mm.then_inc(sem["m_ready"], 1)
                pe.wait_ge(sem["ms_done"], c("ms_done") + 1)
                c.over("fold")

            def attend(g):
                pe.wait_ge(sem["qs_ready"], c("qs_ready") + 1)
                rows(lambda k, i: QS[:, k, i * T:(i + 1) * T], lambda k: MS[:, k, :])
                c.over("attend")

            def up(l, g, h):
                off, tiles = HALF[h]
                if h == 0:
                    pe.wait_ge(sem["xt_done"], c("xt_done"))
                for j in range(FB):
                    wide_free(j)
                    for k in range(KC):
                        mm = pe.matmul(WIDE[j % 2][:, 0:tiles * T], W1[:, k, j * 128:(j + 1) * 128],
                                       KX[:, k, span(g * GW + off * T, tiles * T)], start=(k == 0), stop=(k == KC - 1))
                    mm.then_inc(sem["wide_ready"], 1)
                c.over(f"up{h}")

            def down(g, h):
                off, tiles = HALF[h]
                pe.wait_ge(sem["wide_done"], c("wide_done"))
                for i in range(tiles):
                    row_free(i)
                    for j in range(FB):
                        mm = pe.matmul(ROW[i % 2][0:T, 0:D], UT[h][:, j, i * T:(i + 1) * T], W2[:, j, :],
                                       start=(j == 0), stop=(j == FB - 1))
                    mm.then_inc(sem["row_ready"], 1)
                c.over(f"down{h}")

            pe.wait_ge(sem["consts"], 1)
            pe.wait_ge(sem["e_counted"], 1)
            pe.matmul(P[6][:, 0:NB], TRI[:, :], CNT[:, 0:NB], start=True, stop=True)
            pe.matmul(P[6][:, 32:32 + NB], ones[:, :], CNT[:, 0:NB], start=True, stop=True).then_inc(sem["e_offset"], 1)
            pe.wait_ge(sem["e_ends"], 1)
            pe.matmul(P[7][0:NT, 0:1], END[0:1, 0:NT], ones[0:1, 0:1], start=True, stop=True).then_inc(sem["e_past"], 1)
            pe.wait_ge(sem["e_passed"], 1)
            pe.matmul(P[7][0:1, 0:NCH], ones[0:NT, 0:1], PAST[0:NT, :], start=True, stop=True).then_inc(sem["e_blocks"], 1)
            pe.wait_ge(sem["w_g"], 16)
            pe.wait_ge(sem["cols_in"], 16)

            layers(pe, c, {
                "prep_qk": prep_qk, "prep_rest": prep_rest, "support": support, "norm_in": lambda g: norm("norm_in"),
                "norm_a": lambda g: norm("norm_a"), "norm_c": lambda g: norm("norm_c"), "keys": keys,
                "queries": queries, "turn_q": turn_q, "kmax": lambda: c.over("kmax"),
                "context": context, "fold": fold, "attend": attend, "up": up, "down": down})

            with c.loop(pe, 0, NCH // UNIT, ["edges"]) as r:
                for i in range(UNIT):
                    pe.wait_ge(sem["hot_ready"], c("hot_ready") + i + 1)
                    pe.wait_ge(msg_in[i], r * 16 + 16)
                    pe.wait_ge(sem["agg_done"], c("agg_done") + max(i - 1, 0))
                    pe.matmul(ACC[i % 2][0:T, 0:D], HOT[:, i % 2, :], MSG[:, i, :], start=True,
                              stop=True).then_inc(sem["agg_ready"], 1)
                c.over("edges")

            pe.wait_ge(sem["f_in"], F_LOADS)
            pe.wait_ge(sem["f_lbx"], 1)
            pe.wait_ge(sem["agg_done"], NCH + 1)
            for j in range(4):
                js = slice(j * 128, (j + 1) * 128)
                for m in range(KC):
                    pe.matmul(ACC[m][:, js], WXT[:, j, m * 128:(m + 1) * 128], BD, start=True, stop=True)
                mm = pe.matmul(ROW[0][0:T, js], LBX[:, j, :], BD, start=True, stop=True)
            mm.then_inc(sem["f_fold"], 1)
            pe.wait_ge(sem["f_ready"], 1)
            for m in range(KC):
                pe.matmul(ACC[m][:, :], zeros[:, 0:128], zeros[:, :], start=True, stop=False, skip_group_check=True)
            with c.loop(pe, 0, NG, ["norm_f", "logits"]) as g:
                norm("norm_f")

                def logit(i):
                    row_free(i)
                    pe.wait_ge(sem["xt_done"], c("xt_done") - G + i + 1)
                    for k in range(KC):
                        mm = pe.matmul(ROW[i % 2][0:T, :], XT[:, k, i * T:(i + 1) * T], WXS[:, k, :],
                                       start=(k == 0), stop=(k == KC - 1))
                    mm.then_inc(sem["row_ready"], 1)

                def token(i):
                    pe.wait_ge(sem["s_ready"], c("s_ready") + i + 1)
                    for m in range(KC):
                        mm = pe.matmul(ACC[m][:, :], XH[:, i, m * 128:(m + 1) * 128],
                                       S[:, span(g * G + i, 1), :].rearrange("p a s -> p (a s)"),
                                       start=False, stop=False, skip_group_check=True)
                    mm.then_inc(sem["tok"], 1)
                logit(0)
                for i in range(1, G):
                    logit(i)
                    token(i - 1)
                token(G - 1)
                c.over("logits")
            for m in range(KC):
                mm = pe.matmul(ACC[m][:, :], zeros[:, 0:128], zeros[:, :], start=False, stop=True, skip_group_check=True)
            mm.then_inc(sem["y_ready"], 1)
            pe.wait_ge(sem["s_summed"], NT + 1)
            wait(pe, sem["row_done"], c("row_done"))
            for h in range(FH):
                mm = pe.matmul(TP[0:FG, h:h + 1], SSUM[:, h * FG:(h + 1) * FG], ones[0:T, 0:1], start=True, stop=True)
            mm.then_inc(sem["n_ready"], 1)
            pe.wait_ge(sem["y_ready"], 2)
            for h in range(FH):
                for k in range(KC):
                    mm = pe.matmul(ROW[0][0:FG, h * FD:(h + 1) * FD], YT[:, k, h * FG:(h + 1) * FG],
                                   WFX[:, k, h * FD:(h + 1) * FD], start=(k == 0), stop=(k == KC - 1))
            mm.then_inc(sem["tk_ready"], 1)
            pe.wait_ge(sem["tk_done"], 1)
            for h in range(FH):
                mm = pe.transpose(QP[0:FD, h * FG:(h + 1) * FG], TK[:, h * FD:(h + 1) * FD], ident[0:FG, 0:FG])
            mm.then_inc(sem["tkt_ready"], 1)
            pe.wait_ge(sem["tkt_done"], 1)
            pe.matmul(WIDE[0][0:FD, :], WQKV[:, 0:FD], TKT, start=True, stop=True)
            pe.matmul(WIDE[1][0:FD, :], WQKV[:, FD:2 * FD], TKT, start=True, stop=True)
            for h in range(FH):
                mm = pe.matmul(ROW[1][0:FG, h * FD:(h + 1) * FD], TKT[:, h * FG:(h + 1) * FG], WQKV[:, 2 * FD:3 * FD],
                               start=True, stop=True)
            mm.then_inc(sem["qkv_ready"], 1)
            pe.wait_ge(sem["qkv_done"], 1)
            for h in range(FH):
                hs = slice(h * FG, (h + 1) * FG)
                mm = pe.matmul(ROW[0][0:FG, hs], FQT[:, hs], FKT[:, hs], start=True, stop=True)
            mm.then_inc(sem["aw_ready"], 1)
            pe.wait_ge(sem["aw_done"], 1)
            for h in range(FH):
                hs = slice(h * FG, (h + 1) * FG)
                mm = pe.transpose(QP[0:FG, hs], AW[:, hs], ident[0:FG, 0:FG])
            mm.then_inc(sem["awt_ready"], 1)
            pe.wait_ge(sem["awt_done"], 1)
            for h in range(FH):
                hs = slice(h * FG, (h + 1) * FG)
                mm = pe.matmul(ROW[1][0:FD, hs], FV[:, h * FD:(h + 1) * FD], AWT[:, hs], start=True, stop=True)
            mm.then_inc(sem["o_ready"], 1)
            pe.wait_ge(sem["o_done"], 1)
            for j in range(4):
                for a in range(2):
                    mm = pe.matmul(ACC[j // 2][:, (j % 2) * D:(j % 2 + 1) * D], OP[:, 2 * j + a, :], WOUT[:, 2 * j + a, :],
                                   start=(a == 0), stop=(a == 1))
            mm.then_inc(sem["m2_ready"], 1)
            pe.wait_ge(sem["m2_done"], 1)
            with c.loop(pe, 0, NG, ["finish"]) as g:
                def turn(i):
                    pe.wait_ge(sem["sc_ready"], c("sc_ready") + i + 1)
                    pe.wait_ge(sem["st_done"], c("st_done") + i)
                    for j in range(4):
                        mm = pe.transpose(TP[:, j * T:(j + 1) * T], SC[i % 2][:, j * 128:(j + 1) * 128], ident[0:T, 0:T])
                    mm.then_inc(sem["st_ready"], 1)

                def put(i):
                    pe.wait_ge(sem["st_done"], c("st_done") + i + 1)
                    row_free(i)
                    for j in range(4):
                        mm = pe.matmul(ROW[i % 2][0:T, 0:D], STT[i % 2][:, j, :], M2[:, j, :], start=(j == 0), stop=(j == 3))
                    mm.then_inc(sem["row_ready"], 1)
                turn(0)
                for i in range(1, G):
                    turn(i)
                    put(i - 1)
                put(G - 1)
                c.over("finish")

        @block.scalar
        def _(act):
            c = Count(1)

            def norm(name, g, out_, readers):
                for sem_ in readers:
                    wait(act, sem[sem_], c(sem_))
                for i in range(G):
                    act.wait_ge(sem["xt_ready"], c("xt_ready") + i + 1)
                    act.activation(out_(g, i), turned(TP), ACT.Copy).then_inc(sem["xt_done"], 1)
                c.over(name)

            def to_xt(g, i):
                return XT[:, :, i * T:(i + 1) * T]

            def to_kx(g, i):
                return KX[:, :, span(g * GW + i * T, T)]

            def keys(g):
                n = 0
                for off, tiles in HALF:
                    for m in range(KC):
                        act.wait_ge(sem["wide_ready"], c("wide_ready") + n + 1)
                        act.activation(KX[:, m, span(g * GW + off * T, tiles * T)], WIDE[n % 2][:, 0:tiles * T],
                                       ACT.Identity, bias=BK[:, m:m + 1]).then_inc(sem["wide_done"], 1)
                        n += 1
                c.over("keys")

            def queries(g):
                act.wait_ge(sem["qz_ready"], c("qz_ready") + 1)
                act.activation(QZ[:, :, :], QZ[:, :, :], ACT.Exp, scale=QSCALE).then_inc(sem["qe_ready"], 1)
                c.over("queries")

            def turn_q(g):
                wait(act, sem["qs_ready"], c("qs_ready"))
                for i in range(G):
                    act.wait_ge(sem["qt_ready"], c("qt_ready") + i + 1)
                    act.activation(QT[:, :, span(g * GW + i * T, T)], turned(QP), ACT.Copy).then_inc(sem["qt_done"], 1)
                c.over("turn_q")

            def context(g):
                act.wait_ge(sem["kmax_ready"], c("kmax_ready"))
                wait(act, sem["kt_ready"], c("kt_ready"))
                for k in range(KC):
                    act.activation(KE[:, k, :], KX[:, k, span(g * GW, GW)], ACT.Exp, bias=KB[:, k:k + 1], scale=QSCALE,
                                   accum_out=KS[:, k, span(g, 1)]).then_inc(sem["kexp"], 1)
                for i in range(G):
                    act.wait_ge(sem["kt_ready"], c("kt_ready") + i + 1)
                    if i != 1:
                        wait(act, sem["g_acc"], c("g_acc") + max(i - 1, 0))
                    act.activation(KT[:, i % 2, :], [TP, QP][i % 2][0:T, 0:D], ACT.Copy).then_inc(sem["kt_done"], 1)
                c.over("context")

            def up(l, g, h):
                off, tiles = HALF[h]
                for j in range(FB):
                    act.wait_ge(sem["wide_ready"], c("wide_ready") + j + 1)
                    act.activation(UT[h][:, j, :], WIDE[j % 2][:, 0:tiles * T], ACT.Gelu,
                                   bias=B1[:, j:j + 1]).then_inc(sem["wide_done"], 1)
                c.over(f"up{h}")

            def nothing(*names_):
                return lambda *a: c.over(*names_)

            layers(act, c, {
                "prep_qk": nothing("prep_qk"), "prep_rest": nothing("prep_rest"), "support": nothing("support"),
                "norm_in": lambda g: norm("norm_in", g, to_xt, ["row_ready"]),
                "norm_a": lambda g: norm("norm_a", g, to_xt, ["row_ready", "wide_ready"]),
                "norm_c": lambda g: norm("norm_c", g, to_kx, ["kt_ready"]),
                "keys": keys, "queries": queries, "turn_q": turn_q, "kmax": nothing("kmax"), "context": context,
                "fold": nothing("fold"), "attend": nothing("attend"), "up": up, "down": lambda g, h: c.over(f"down{h}")})

            with c.loop(act, 0, NG, ["norm_f", "logits"]) as g:
                norm("norm_f", g, to_xt, ["row_ready"])
                for i in range(G):
                    act.wait_ge(sem["sz_ready"], c("sz_ready") + i + 1)
                    act.activation(SZ[i % 2], SZ[i % 2], ACT.Exp).then_inc(sem["se_ready"], 1)
                c.over("logits")
            act.wait_ge(sem["az_ready"], 1)
            act.activation(AW, AW, ACT.Exp, scale=FD ** -0.5).then_inc(sem["ae_ready"], 1)
            with c.loop(act, 0, NG, ["finish"]) as g:
                for i in range(G):
                    act.wait_ge(sem["st_ready"], c("st_ready") + i + 1)
                    wait(act, sem["row_ready"], c("row_ready") + max(i - 1, 0))
                    act.activation(STT[i % 2], TP[:, 0:4 * T].rearrange("p (j t) -> p j t", j=4),
                                   ACT.Copy).then_inc(sem["st_done"], 1)
                c.over("finish")

        @block.vector
        def _(dve):
            c = Count(1)

            def step(ins):
                ins.then_inc(sem["dve_step"], 1)
                c.own["dve_step"] += 1
                dve.wait_ge(sem["dve_step"], c("dve_step"))

            def tiles_of(buf, g):
                return buf[:, span(g * G, G), :]

            def norm(name, g, src_, keep=False, bias=None):
                wait(dve, sem["row_done"], c("row_done"))
                apart(dve, sem["dve_waited"])
                for i in range(G):
                    ins = dve.bn_stats(ST[:, i, :], src_[:, span(g * G + i, 1), :].rearrange("p a d -> p (a d)"))
                step(ins)
                apart(dve, sem["dve_waited"])
                for i in range(G):
                    ins = dve.bn_aggr(MV[:, i, :], ST[:, i, :])
                step(ins)
                rs, nm = RSTD[:, span(g * G, G)], NMR[:, span(g * G, G)]
                v, y, z = NW[:, 0, :], NW[:, 1, :], NW[:, 2, :]
                step(dve.tensor_scalar_add(v, MV[:, :, 1], EPS))
                step(dve.tensor_single_scalar(z.bitcast(I32), v.bitcast(I32), 1, ALU.logical_shift_right))
                step(dve.tensor_scalar(y.bitcast(I32), z.bitcast(I32), -1.0, MAGIC, ALU.mult, ALU.add))
                for n in range(3):
                    step(dve.scalar_tensor_tensor(z, y, -0.5, y, ALU.mult, ALU.mult))
                    step(dve.tensor_tensor(z, z, v, ALU.mult))
                    step(dve.scalar_tensor_tensor(rs if n == 2 else y, z, 1.5, y, ALU.add, ALU.mult))
                step(dve.scalar_tensor_tensor(nm, MV[:, :, 0], -1.0, rs, ALU.mult, ALU.mult))
                wait(dve, sem["xt_done"], c("xt_done"))
                wait(dve, sem["g_acc"], c("g_acc"))
                wait(dve, sem["tok"], c("tok"))
                for i in range(G):
                    t = span(g * G + i, 1)
                    dve.tensor_scalar(XH[:, i, :], src_[:, t, :].rearrange("p a d -> p (a d)"), RSTD[:, t], NMR[:, t],
                                      ALU.mult, ALU.add).then_inc(sem["xh_ready"], 1)
                    if keep:
                        dve.tensor_scalar(X[:, t, :].rearrange("p a d -> p (a d)"), src_[:, t, :].rearrange("p a d -> p (a d)"),
                                          RSTD[:, t], NMR[:, t], ALU.mult, ALU.add)
                if bias is not None:
                    dve.wait_ge(sem["xh_ready"], c("xh_ready") + G)
                    step(dve.tensor_tensor(tiles_of(X, g), tiles_of(X, g), bias.unsqueeze(1).broadcast_to([T, G, D]), ALU.add))
                    apart(dve, sem["dve_waited"])
                c.rest(name)

            def add_rows(g, off, tiles):
                for i in range(tiles):
                    t = span(g * G + off + i, 1)
                    x_ = X[:, t, :].rearrange("p a d -> p (a d)")
                    dve.wait_ge(sem["row_ready"], c("row_ready") + i + 1)
                    dve.tensor_tensor(x_, ROW[i % 2][0:T, 0:D], x_, ALU.add).then_inc(sem["row_done"], 1)

            def support(g):
                wait(dve, sem["sup_stored"], c("sup_stored"))
                for i in range(G):
                    dve.wait_ge(sem["row_ready"], c("row_ready") + i + 1)
                    dve.tensor_copy(QZ[:, i, :], ROW[i % 2][0:T, 0:D]).then_inc(sem["row_done"], 1)
                c.rest("support")

            def prep_qk(l):
                for k in range(KC):
                    ins = dve.tensor_scalar(LB[:, k, :], ones[:, 0:T], COLS[:, span(l * 16 + 2 + k, 1)], None, ALU.mult)
                ins.then_inc(sem["lb_ready"], 1)
                dve.wait_ge(sem["bqk_ready"], c("bqk_ready") + 1)
                wait(dve, sem["wide_done"], c("wide_done"))
                dve.tensor_copy(BQ[:, :], ROW[0][0:T, 0:D])
                dve.tensor_copy(BK[:, :], ROW[1][:, 0:KC])
                for k in range(KC):
                    ins = dve.tensor_scalar(WQK[:, k, :], WQK[:, k, :], COLS[:, span(l * 16 + k, 1)], None, ALU.mult)
                ins.then_inc(sem["qk_ready"], 1)
                c.rest("prep_qk")

            def keys(g):
                dve.wait_ge(sem["wide_done"], c("wide_done") + 2 * KC)
                step(dve.tensor_reduce(MX[:, :, span(g, 1)], KX[:, :, span(g * GW, GW)], axis=AX_X, op=ALU.max))
                c.rest("keys")

            def queries(g):
                wait(dve, sem["qt_ready"], c("qt_ready"))
                wait(dve, sem["sup_stored"], c("sup_stored"))
                for i in range(G):
                    dve.wait_ge(sem["row_ready"], c("row_ready") + i + 1)
                    dve.tensor_tensor(QZ[:, i, :], ROW[i % 2][0:T, 0:D], BQ[:, :], ALU.add).then_inc(sem["row_done"], 1)
                z = QZ[:, :, :].rearrange("p g (h d) -> p (g h) d", d=DH)
                m = QM[:, :].unsqueeze(2).broadcast_to([T, G * HEADS, DH])
                dve.wait_ge(sem["row_done"], c("row_done") + G)
                step(dve.tensor_reduce(QM[:, :], z, axis=AX_X, op=ALU.max))
                dve.tensor_tensor(z, z, m, ALU.subtract).then_inc(sem["qz_ready"], 1)
                dve.wait_ge(sem["qe_ready"], c("qe_ready") + 1)
                step(dve.tensor_reduce(QM[:, :], z, axis=AX_X, op=ALU.add))
                step(dve.reciprocal(QM[:, :], QM[:, :]))
                dve.tensor_tensor(z, z, m, ALU.mult).then_inc(sem["qn_ready"], 1)
                c.rest("queries")

            def kmax():
                wait(dve, sem["kexp"], c("kexp"))
                step(dve.tensor_reduce(KB[:, :], MX[:, :, :], axis=AX_X, op=ALU.max))
                dve.tensor_scalar(KB[:, :], KB[:, :], -QSCALE, None, ALU.mult).then_inc(sem["kmax_ready"], 1)
                c.rest("kmax")

            def prep_rest(l):
                dve.wait_ge(sem["bv_ready"], c("bv_ready") + 1)
                wait(dve, sem["wide_done"], c("wide_done"))
                dve.tensor_tensor(B1[:, :], ROW[0][:, 8:8 + FB], COLS[:, span(l * 16 + 8, FB)], ALU.add)
                step(dve.tensor_copy(BV[:, :], ROW[0][:, 0:KC]))
                for j in range(KC):
                    ins = dve.tensor_scalar(BVM[:, j * 128:(j + 1) * 128], MASK[:, j * 128:(j + 1) * 128], BV[:, j:j + 1],
                                            None, ALU.mult)
                ins.then_inc(sem["bvm_ready"], 1)
                for k in range(KC):
                    dve.tensor_scalar(WVO[:, k, 0:D], WVO[:, k, 0:D], COLS[:, span(l * 16 + k, 1)], None, ALU.mult)
                    dve.tensor_scalar(W1[:, k, :], W1[:, k, :], COLS[:, span(l * 16 + 4 + k, 1)], None, ALU.mult)
                dve.wait_ge(sem["b2m_ready"], c("b2m_ready") + 1)
                dve.tensor_copy(B2M[:, :, :], ROW[1][:, :].rearrange("p (k n) -> p k n", k=KC)).then_inc(sem["rest_ready"], 1)
                c.rest("prep_rest")

            def context(g):
                wait(dve, sem["xt_done"], c("xt_done"))
                wait(dve, sem["g_acc"], c("g_acc"))
                for i in range(G):
                    t = span(g * G + i, 1)
                    dve.tensor_scalar(XH[:, i, :], X[:, t, :].rearrange("p a d -> p (a d)"), RSTD[:, t], NMR[:, t],
                                      ALU.mult, ALU.add).then_inc(sem["bxh_ready"], 1)
                c.rest("context")

            def fold():
                dve.wait_ge(sem["kexp"], c("kexp"))
                step(dve.tensor_reduce(RS[:, 0, :], KS[:, :, :], axis=AX_X, op=ALU.add))
                step(dve.reciprocal(RS[:, 1, :], RS[:, 0, :]))
                dve.wait_ge(sem["g_closed"], c("g_closed") + 1)
                for m in range(KC):
                    ins = dve.tensor_copy(GS[:, m, :], ACC[m][:, 0:D])
                ins.then_inc(sem["gs_ready"], 1)
                dve.wait_ge(sem["cm_ready"], c("cm_ready") + 1)
                dve.tensor_tensor(CM[:, :], TP[:, 0:D], MASK[:, :], ALU.mult).then_inc(sem["cm_done"], 1)
                dve.wait_ge(sem["m_ready"], c("m_ready") + 1)
                for j in range(KC):
                    ins = dve.scalar_tensor_tensor(MS[:, j, :], ROW[j][:, 0:D], RS[:, 1, j:j + 1], B2M[:, j, :],
                                                   ALU.mult, ALU.add)
                ins.then_inc(sem["ms_done"], 1)
                c.rest("fold")

            def attend(g):
                wait(dve, sem["qt_done"], c("qt_done"))
                dve.tensor_copy(QS[:, :, :], QT[:, :, span(g * GW, GW)]).then_inc(sem["qs_ready"], 1)
                add_rows(g, 0, G)
                c.rest("attend")

            def down(g, h):
                add_rows(g, *HALF[h])
                c.rest(f"down{h}")

            dve.memset(RANK, 0.0)
            dve.wait_ge(sem["consts"], 1)
            dve.wait_ge(sem["e_bucketed"], 1)
            with dve.Fori(0, NB) as b:
                n = b * 4
                dve.tensor_scalar(HIT, BKT, BT[:, span(b, 1)], None, ALU.is_equal).then_inc(sem["e_rank"], 1)
                dve.wait_ge(sem["e_rank"], n + 2)
                dve.tensor_tensor_scan(SCAN, HIT, HIT, 0.0, ALU.add, ALU.bypass).then_inc(sem["e_rank"], 1)
                dve.wait_ge(sem["e_rank"], n + 3)
                dve.tensor_copy(CNT[:, span(b, 1)], SCAN[:, EC - 1:EC])
                dve.tensor_tensor(HIT, HIT, SCAN, ALU.mult).then_inc(sem["e_rank"], 1)
                dve.wait_ge(sem["e_rank"], n + 4)
                dve.tensor_tensor(RANK, RANK, HIT, ALU.add).then_inc(sem["e_rank"], 1)
                dve.wait_ge(sem["e_rank"], n + 5)
            dve.sem_inc(sem["e_counted"], 1)
            dve.wait_ge(sem["e_offset"], 1)
            step(dve.tensor_scalar(TOTI[:, 0:NB], P[6][:, 32:32 + NB], 127.0, None, ALU.add))
            step(dve.tensor_scalar(TOTI[:, 0:NB], TOTI[:, 0:NB], 7, 7, ALU.logical_shift_right, ALU.logical_shift_left))
            step(dve.tensor_copy(TOT[:, 0:NB], TOTI[:, 0:NB]))
            step(dve.tensor_tensor_scan(END[:, 0:NB], TOT[:, 0:NB], TOT[:, 0:NB], 0.0, ALU.add, ALU.bypass))
            step(dve.tensor_tensor(BASE[:, 0:NB], END[:, 0:NB], TOT[:, 0:NB], ALU.subtract))
            step(dve.scalar_tensor_tensor(OFF[:, 0:NB], P[6][:, 0:NB], -1.0, BASE[:, 0:NB], ALU.add, ALU.add))
            dve.sem_inc(sem["e_ends"], 1)
            with dve.Fori(0, NB) as b:
                n = b * 2 + 4 * NB
                dve.tensor_scalar(HIT, BKT, BT[:, span(b, 1)], OFF[:, span(b, 1)], ALU.is_equal, ALU.mult).then_inc(sem["e_rank"], 1)
                dve.wait_ge(sem["e_rank"], n + 2)
                dve.tensor_tensor(RANK, RANK, HIT, ALU.add).then_inc(sem["e_rank"], 1)
                dve.wait_ge(sem["e_rank"], n + 3)
            step(dve.tensor_copy(POS, RANK))
            step(dve.tensor_single_scalar(LANE, POS, 127, ALU.bitwise_and))
            step(dve.tensor_single_scalar(POS, POS, 7, ALU.logical_shift_right))
            dve.scalar_tensor_tensor(POSI[:, :], LANE, float(RC), POS, ALU.mult, ALU.add).then_inc(sem["e_placed"], 1)
            dve.wait_ge(sem["e_past"], 1)
            step(dve.tensor_scalar(ENDC[0:NT, 0:1], P[7][0:NT, 0:1], 1.0 / 128, None, ALU.mult))
            dve.tensor_scalar(PAST[0:NT, :], IOTA[0:NT, 0:NCH], ENDC[0:NT, 0:1], None, ALU.is_ge).then_inc(sem["e_passed"], 1)
            dve.wait_ge(sem["e_blocks"], 1)
            step(dve.tensor_scalar(BLK[:, :], P[7][0:1, 0:NCH], float(NT - 1), None, ALU.min))

            dve.wait_ge(sem["x_in"], 16)
            dve.wait_ge(sem["cols_in"], 16)
            dve.wait_ge(sem["e_records"], 1)
            layers(dve, c, {
                "prep_qk": prep_qk, "prep_rest": prep_rest, "support": support,
                "norm_in": lambda g: norm("norm_in", g, AGG, keep=True),
                "norm_a": lambda g: norm("norm_a", g, X), "norm_c": lambda g: norm("norm_c", g, X, bias=BB2[:, :]),
                "keys": keys, "queries": queries, "turn_q": lambda g: c.rest("turn_q"), "kmax": kmax,
                "context": context, "fold": fold, "attend": attend, "up": lambda l, g, h: c.rest(f"up{h}"),
                "down": down})

            dve.wait_ge(sem["e_back"], 16)
            with c.loop(dve, 0, NCH // UNIT, ["edges"]) as r:
                def hot(i):
                    dve.wait_ge(sem["agg_ready"], c("agg_ready") + max(i - 1, 0))
                    rec = REC3[:, span(r * UNIT + i, 1), :].rearrange("p a r -> p (a r)")
                    dve.tensor_scalar(HOT[:, i % 2, :], IOTA[:, 0:T], rec[:, 1:2], rec[:, 2:3], ALU.is_equal,
                                      ALU.mult).then_inc(sem["hot_ready"], 1)

                def gather_sums(i):
                    t = dve.value_load(BLK[0:1, span(r * UNIT + i, 1)], min_val=0, max_val=NT - 1)
                    a = AGG[:, bass.ds(t, 1), :].rearrange("p a d -> p (a d)")
                    dve.wait_ge(sem["agg_ready"], c("agg_ready") + i + 1)
                    dve.wait_ge(sem["agg_done"], c("agg_done") + i)
                    dve.tensor_tensor(a, ACC[i % 2][0:T, 0:D], a, ALU.add).then_inc(sem["agg_done"], 1)
                hot(0)
                for i in range(1, UNIT):
                    hot(i)
                    gather_sums(i - 1)
                gather_sums(UNIT - 1)
                c.rest("edges")

            dve.memset(BD, 0.0).then_inc(sem["f_bd"], 1)
            dve.wait_ge(sem["f_in"], F_LOADS)
            step(dve.tensor_scalar(TI, TEMP, 0.1, 5.0, ALU.max, ALU.min))
            step(dve.reciprocal(TI, TI))
            for j in range(4):
                ins = dve.tensor_scalar(LBX[:, j, :], ones[:, 0:T], BXC[:, j:j + 1], None, ALU.mult)
            ins.then_inc(sem["f_lbx"], 1)
            dve.wait_ge(sem["f_fold"], 1)

            def heads(a):
                return a.rearrange("p (h s) -> p h s", h=FH)

            def over(a, parts):
                return a.unsqueeze(2).broadcast_to([parts, FH, FG])
            for m in range(KC):
                dve.tensor_tensor(heads(WXS[:, m, :]), heads(ACC[m][:, :]), over(TI, 128), ALU.mult)
            step(dve.tensor_tensor(heads(LBI), heads(ROW[0][0:T, :]), BSL.unsqueeze(1).broadcast_to([T, FH, FG]), ALU.add))
            dve.tensor_tensor(heads(LBI), heads(LBI), over(TI[0:T, :], T), ALU.mult).then_inc(sem["f_ready"], 1)
            dve.wait_ge(sem["f_ready"], 1)
            with c.loop(dve, 0, NG, ["norm_f", "logits"]) as g:
                step(dve.tensor_tensor(tiles_of(X, g), tiles_of(X, g), tiles_of(AGG, g), ALU.add))
                norm("norm_f", g, X)

                def before(i):
                    z = SZ[i % 2]
                    dve.wait_ge(sem["row_ready"], c("row_ready") + i + 1)
                    dve.tensor_tensor(z, ROW[i % 2][0:T, :], LBI, ALU.add).then_inc(sem["row_done"], 1)
                    dve.wait_ge(sem["row_done"], c("row_done") + i + 1)
                    step(dve.tensor_reduce(SMX, heads(z), axis=AX_X, op=ALU.max))
                    dve.tensor_tensor(heads(z), heads(z), over(SMX, T), ALU.subtract).then_inc(sem["sz_ready"], 1)

                def after(i):
                    z = SZ[i % 2]
                    dve.wait_ge(sem["se_ready"], c("se_ready") + i + 1)
                    wait(dve, sem["s_ready"], c("s_ready") + i)
                    step(dve.tensor_reduce(SDEN, heads(z), axis=AX_X, op=ALU.add))
                    step(dve.reciprocal(SDEN, SDEN))
                    dve.tensor_tensor(heads(S[:, span(g * G + i, 1), :].rearrange("p a s -> p (a s)")), heads(z),
                                      over(SDEN, T), ALU.mult).then_inc(sem["s_ready"], 1)
                before(0)
                for i in range(1, G):
                    before(i)
                    after(i - 1)
                after(G - 1)
                c.rest("logits")
            dve.wait_ge(sem["y_ready"], 1)
            for m in range(KC):
                ins = dve.tensor_copy(YT[:, m, :], ACC[m][:, :])
            ins.then_inc(sem["y_ready"], 1)
            dve.wait_ge(sem["n_ready"], 1)
            step(dve.tensor_copy(NRM[:, :], TP[0:FG, 0:FH]))
            dve.tensor_tensor(heads(TK), heads(BFX), over(NRM[:, :], FG), ALU.mult)
            step(dve.tensor_scalar(DEN[:, :], NRM[:, :], 1e-5, None, ALU.add))
            step(dve.reciprocal(DEN[:, :], DEN[:, :]))
            dve.wait_ge(sem["tk_ready"], 1)
            step(dve.tensor_tensor(TK, ROW[0][0:FG, :], TK, ALU.add))
            dve.tensor_tensor(heads(TK), heads(TK), over(DEN[:, :], FG), ALU.mult).then_inc(sem["tk_done"], 1)
            dve.wait_ge(sem["tkt_ready"], 1)
            dve.tensor_copy(TKT, QP[0:FD, :]).then_inc(sem["tkt_done"], 1)
            dve.wait_ge(sem["qkv_ready"], 1)
            dve.tensor_copy(FQT, WIDE[0][0:FD, :])
            dve.tensor_copy(FKT, WIDE[1][0:FD, :])
            dve.tensor_copy(FV, ROW[1][0:FG, :]).then_inc(sem["qkv_done"], 1)
            dve.wait_ge(sem["aw_ready"], 1)
            step(dve.tensor_reduce(AMX[:, :], heads(ROW[0][0:FG, :]), axis=AX_X, op=ALU.max))
            dve.tensor_tensor(heads(AW), heads(ROW[0][0:FG, :]), over(AMX[:, :], FG), ALU.subtract).then_inc(sem["az_ready"], 1)
            dve.wait_ge(sem["ae_ready"], 1)
            step(dve.tensor_reduce(AMX[:, :], heads(AW), axis=AX_X, op=ALU.add))
            step(dve.reciprocal(AMX[:, :], AMX[:, :]))
            dve.tensor_tensor(heads(AW), heads(AW), over(AMX[:, :], FG), ALU.mult).then_inc(sem["aw_done"], 1)
            dve.wait_ge(sem["awt_ready"], 1)
            dve.tensor_copy(AWT, QP[0:FG, :]).then_inc(sem["awt_done"], 1)
            step(dve.memset(OP, 0.0))
            dve.wait_ge(sem["o_ready"], 1)
            for a in range(2):
                ins = dve.tensor_copy(OP[:, a::2, a * FG:(a + 1) * FG], heads(ROW[1][0:FD, :])[:, a::2, :])
            ins.then_inc(sem["o_done"], 1)
            dve.wait_ge(sem["m2_ready"], 1)
            for a in range(2):
                ins = dve.tensor_copy(M2[:, 2 * a:2 * a + 2, :], ACC[a][:, :].rearrange("p (j d) -> p j d", j=2))
            ins.then_inc(sem["m2_done"], 1)
            with c.loop(dve, 0, NG, ["finish"]) as g:
                step(dve.tensor_tensor(tiles_of(X, g), tiles_of(X, g), BOUT.unsqueeze(1).broadcast_to([T, G, D]), ALU.add))
                add_rows(g, 0, G)
                c.rest("finish")


def kernel(**inputs):
    import numpy as np
    import concourse.bacc as bacc
    from concourse import mybir as mb
    from concourse.bass_utils import run_bass_kernel_spmd

    a = {k.removeprefix("L0_"): np.asarray(v) for k, v in inputs.items()}

    def edges(v, fill):
        return np.concatenate([v, np.full(128 * EC - E, fill, v.dtype)]).reshape(128, EC)

    def blocks(w):
        w = w.reshape(*w.shape[:-2], w.shape[-2] // 128, 128, w.shape[-1])
        return np.ascontiguousarray(np.swapaxes(w, -3, -2))

    def columns(v):
        return v.reshape(LAYERS, -1, 128).transpose(2, 0, 1)

    arrays = {
        "x": a["x"], "src": edges(a["src"], N), "dst": edges(a["dst"], 0), "ew": edges(a["edge_weight"], 0),
        "w_gnn": blocks(a["gnn_W"]),
        "w_qk": blocks(np.concatenate([a["mix_Wq"], a["mix_Wk"]], -1)),
        "w_vo": blocks(np.concatenate([a["mix_Wv"], a["mix_Wo"]], -1)),
        "w_1": blocks(a["mix_W1"]), "w_2": blocks(a["mix_W2"]),
        "cols": np.concatenate([columns(a[f"mix_{n}"]) for n in ("ln1_g", "ln1_b", "ln2_g", "ln2_b", "b1")], -1).reshape(128, -1),
        "b_o": a["mix_bo"], "b_2": a["mix_b2"],
        "w_fx": blocks(a["ffn_W_fx"]), "w_xt": blocks(np.ascontiguousarray(a["ffn_W_x"].T)),
        "w_slice": a["ffn_W_slice"], "b_slice": a["ffn_b_slice"][None], "b_fx": a["ffn_b_fx"][None],
        "b_x": a["ffn_b_x"].reshape(4, 128).T, "w_q": a["ffn_W_q"], "w_k": a["ffn_W_k"], "w_v": a["ffn_W_v"],
        "w_out": a["ffn_W_out"].reshape(FH, FD, D).transpose(1, 0, 2), "b_out": a["ffn_b_out"][None],
        "temp": a["ffn_temperature"].reshape(1, FH),
    }
    arrays = {f"in_{k}": np.ascontiguousarray(v) for k, v in arrays.items()}
    nc = bacc.Bacc("TRN2", target_bir_lowering=False, num_devices=1)
    args = [nc.dram_tensor(k, v.shape, mb.dt.from_np(v.dtype), kind="ExternalInput").ap() for k, v in arrays.items()]
    out = nc.dram_tensor("out_0", (N, D), mb.dt.float32, kind="ExternalOutput").ap()
    gps_layer(nc, *args, out)
    r = run_bass_kernel_spmd(nc, [arrays], core_ids=[0])
    return r.results[0]["out_0"]
```

```python
from contextlib import ExitStack, contextmanager

import concourse.bass as bass
from concourse import mybir

F32 = mybir.dt.float32
I32 = mybir.dt.int32
ALU = mybir.AluOpType
ACT = mybir.ActivationFunctionType
AX_X = mybir.AxisListType.X

N = 3125
D = 256
T = 125
NT = N // T
G = 5
NG = NT // G
GW = G * T
KC = D // 128
LAYERS = 4
HEADS, DH = 8, 32
FF = 4 * D
FB = FF // 128
EPS = 1e-5
QSCALE = DH ** -0.25
E = 50000
HU = 4
UNIT = 2 * HU
EC = -(-E // (128 * UNIT)) * UNIT
NCH = -(-(E + NT * 127) // (128 * UNIT)) * UNIT
RC = NCH + HU
SET = UNIT // 2
FH, FD, FG = 8, 64, 64
INNER = FH * FD
HALF = [(0, 3), (3, 2)]
PB = -(-(NT + 1) // (NG - 1))
NB = PB * (NG - 1)
MAGIC = float(0x5F3759DF)

COUNTS = {
    "calc_in": {"xh_ready": G, "dve_step": 15},
    "calc_a": {"xh_ready": G, "dve_step": 15},
    "calc_c": {"xh_ready": G, "dve_step": 16},
    "calc_f": {"x_summed": 1, "xh_ready": G, "dve_step": 15},
    "norm_in": {"xt_ready": G, "xt_done": G},
    "norm_a": {"xt_ready": G, "xt_done": G},
    "norm_c": {"xt_ready": G, "xt_done": G},
    "norm_f": {"xt_ready": G, "xt_done": G},
    "support": {"row_ready": G, "row_done": G, "sup_stored": 16},
    "keys": {"wide_ready": 2 * KC, "wide_done": 2 * KC, "dve_step": 1},
    "queries": {"row_ready": G, "row_done": G, "qz_ready": 1, "dve_step": 1},
    "soften": {"qe_ready": 1, "qn_ready": 1, "dve_step": 2},
    "turn_q": {"qt_ready": G, "qt_done": G},
    "place": {"placed_by": 2 * PB},
    "placed": {"dve_step": 3},
    "kmax": {"kmax_ready": 1, "dve_step": 1},
    "context": {"kexp": KC, "bxh_ready": G, "kt_ready": G, "kt_done": G, "g_acc": G},
    "fold": {"g_closed": 1, "gs_ready": 1, "cm_ready": 1, "cm_done": 1, "m_ready": 1, "ms_done": 1, "dve_step": 2},
    "fetch_q": {"qs_ready": 1},
    "attend": {"row_ready": G, "row_done": G},
    "up0": {"wide_ready": FB, "wide_done": FB},
    "up1": {"wide_ready": FB, "wide_done": FB},
    "down0": {"row_ready": HALF[0][1], "row_done": HALF[0][1]},
    "down1": {"row_ready": HALF[1][1], "row_done": HALF[1][1]},
    "spread_b": {"lb_ready": 1},
    "prep_qk": {"w_qk": 16, "bqk_ready": 1, "qk_ready": 1},
    "load_rest": {"w_rest": 80},
    "prep_biases": {"bv_ready": 1, "bvm_ready": 1, "dve_step": 1},
    "prep_m": {"b2m_ready": 1, "rest_ready": 1},
    "edges_first": {"hot_ready": HU},
    "edges0": {"hot_ready": HU, "agg_ready": HU, "agg_done": HU, "msgs0": 16 * HU},
    "edges1": {"hot_ready": HU, "agg_ready": HU, "agg_done": HU, "msgs1": 16 * HU},
    "slices": {"x_summed": 1, "xh_ready": G, "xt_ready": G, "xt_done": G, "row_ready": G, "row_done": G,
               "sz_ready": G, "se_ready": G, "s_ready": G, "tok": G, "s_summed": G, "dve_step": 15 + 2 * G},
    "slices_last": {"row_ready": G, "row_done": G, "sz_ready": G, "se_ready": G, "s_ready": G, "tok": G, "s_summed": G,
                    "dve_step": 2 * G},
    "finish": {"sc_ready": G, "st_ready": G, "st_done": G, "row_ready": G, "row_done": G, "out_done": 16,
               "dve_step": 1},
}


class Count:

    def __init__(self, start=0):
        self.base, self.own = {}, {sem: start for stage in COUNTS.values() for sem in stage}

    def __call__(self, sem):
        b, o = self.base.get(sem, 0), self.own.get(sem, 0)
        return o if isinstance(b, int) and b == 0 else b + o

    def over(self, *stages):
        for stage in stages:
            for sem, n in COUNTS[stage].items():
                self.own[sem] = self.own.get(sem, 0) + n

    def rest(self, stage):
        for sem, n in COUNTS[stage].items():
            if sem != "dve_step":
                self.own[sem] = self.own.get(sem, 0) + n

    @contextmanager
    def loop(self, eng, lo, hi, stages):
        per = Count()
        per.over(*stages)
        per.own = {sem: n for sem, n in per.own.items() if n}
        base, own = dict(self.base), dict(self.own)
        with eng.Fori(lo, hi) as r:
            turn = r if lo == 0 else r - lo
            for sem, n in per.own.items():
                self.base[sem] = turn * n + self(sem)
                self.own[sem] = 0
            yield r
        for sem in per.own:
            assert self.own[sem] == per.own[sem], (sem, self.own[sem], per.own[sem])
        self.base, self.own = base, own
        for sem, n in per.own.items():
            self.own[sem] = own.get(sem, 0) + n * (hi - lo)


def wait(eng, sem, value):
    if not isinstance(value, int) or value > 1:
        eng.wait_ge(sem, value)


def apart(eng, sem):
    eng.sem_inc(sem, 1)


A_STAGES = ["calc_a", "norm_a", "keys", "queries", "soften", "turn_q"]
FRONT = ["fetch_q", "attend", "calc_c", "norm_c"]
FFN_STAGES = ["up0", "up1", "down0", "down1"]
B_STAGES = ["context"] * NG + ["soften", "prep_biases", "turn_q", "prep_m", "fold"]
TAIL = ["load_rest", "calc_a", "norm_a", "keys", "kmax", "queries"]
LAYER_STAGES = B_STAGES + ["spread_b", "prep_qk"] + (FRONT + FFN_STAGES) * NG + A_STAGES * (NG - 1) + TAIL
LAST_STAGES = B_STAGES + (FRONT + FFN_STAGES) * NG
TURN_E, HEAD_E, TAIL_E = 6, 2, 4
EDGE_TURN = ["edges0", "edges1"] * (TURN_E // 2)
EDGE_LAYER = ["edges_first"] + ["edges0", "edges1"] * ((HEAD_E + NG * TURN_E + TAIL_E) // 2)
assert ((LAYERS - 1) * (HEAD_E + NG * TURN_E) + (LAYERS - 2) * TAIL_E) * HU == NCH


def idle_stages(c):
    idle = {name: lambda *a, name=name: c.over(name) for name in COUNTS}
    return {**idle, "up": lambda l, g, h: c.over(f"up{h}"), "down": lambda g, h: c.over(f"down{h}"),
            "edges": lambda p: c.over(f"edges{p}"), "qk_set": lambda: None, "open": lambda: None}


def layers(eng, c, stage):
    parity = [0]

    def turn(l, g, front, back, with_edges):
        def edges():
            if with_edges:
                stage["edges"](parity[0] % 2)
                parity[0] += 1
        if back:
            stage["calc_a"](g - 1)
        stage["up"](l, g, 0)
        edges()
        if back:
            stage["norm_a"](g - 1)
            stage["keys"](g - 1)
            stage["queries"](g - 1)
        edges()
        stage["up"](l, g, 1)
        if back:
            stage["soften"]()
        if front:
            stage["fetch_q"](g + 1)
        edges()
        stage["down"](g, 0)
        edges()
        if front:
            stage["attend"](g + 1)
            stage["calc_c"](g + 1)
        edges()
        stage["down"](g, 1)
        if back:
            stage["turn_q"](g - 1)
        if front:
            stage["norm_c"](g + 1)
        edges()

    def layer(l, more, with_edges):
        def edges():
            if with_edges:
                stage["edges"](parity[0] % 2)
                parity[0] += 1
        with c.loop(eng, 0, NG - 1, ["context"] + ["place"] * (not with_edges)) as g:
            stage["context"](g)
            if not with_edges:
                stage["place"](g)
        if not with_edges:
            stage["placed"]()
        stage["soften"]()
        stage["prep_biases"](l)
        stage["turn_q"](NG - 1)
        stage["context"](NG - 1)
        stage["prep_m"]()
        if more:
            stage["spread_b"](l + 1)
        stage["fold"]()
        stage["fetch_q"](0)
        if more:
            stage["prep_qk"](l + 1)
        if with_edges:
            stage["edges_first"]()
        edges()
        if more:
            stage["qk_set"]()
        stage["attend"](0)
        stage["calc_c"](0)
        edges()
        stage["norm_c"](0)
        turn(l, 0, True, False, with_edges)
        with c.loop(eng, 1, NG - 1, FFN_STAGES + FRONT + A_STAGES * more + EDGE_TURN * with_edges) as g:
            turn(l, g, True, more, with_edges)
        turn(l, NG - 1, False, more, with_edges)
        if more:
            stage["load_rest"](l + 1)
            stage["calc_a"](NG - 1)
            edges()
            stage["norm_a"](NG - 1)
            edges()
            stage["keys"](NG - 1)
            stage["kmax"]()
            edges()
            stage["queries"](NG - 1)
            edges()
            stage["open"]()

    stage["load_rest"](0)
    stage["spread_b"](0)
    stage["prep_qk"](0)
    stage["qk_set"]()
    stage["calc_in"](0)
    with c.loop(eng, 0, NG - 1, ["norm_in", "calc_in", "support"]) as g:
        stage["norm_in"](g)
        stage["calc_in"](g + 1)
        stage["support"](g)
    stage["norm_in"](NG - 1)
    stage["calc_a"](0)
    stage["support"](NG - 1)
    stage["norm_a"](0)
    stage["calc_a"](1)
    stage["keys"](0)
    stage["queries"](0)
    with c.loop(eng, 0, NG - 2, A_STAGES) as g:
        stage["soften"]()
        stage["norm_a"](g + 1)
        stage["calc_a"](g + 2)
        stage["keys"](g + 1)
        stage["turn_q"](g)
        stage["queries"](g + 1)
    stage["soften"]()
    stage["norm_a"](NG - 1)
    stage["keys"](NG - 1)
    stage["kmax"]()
    stage["turn_q"](NG - 2)
    stage["queries"](NG - 1)
    stage["open"]()
    layer(0, True, False)
    with c.loop(eng, 1, LAYERS - 1, LAYER_STAGES + EDGE_LAYER) as l:
        layer(l, True, True)
    layer(LAYERS - 1, False, True)


def gps_layer(nc, x, src, dst, ew, w_gnn, w_qk, w_vo, w_1, w_2, cols, b_o, b_2, w_fx, w_xt, w_slice,
              b_slice, b_fx, b_x, w_q, w_k, w_v, w_out, b_out, temp, out):
    x_t = x.rearrange("(t p) c -> p t c", p=T)
    out_t = out.rearrange("(t p) c -> p t c", p=T)
    sup_d = nc.dram_tensor("support_rows", (N, D), F32).ap()
    rec_d = nc.dram_tensor("edge_records", (128 * RC, 4), F32).ap()
    sup_t = sup_d.rearrange("(t p) c -> p t c", p=T)

    with ExitStack() as ctx:
        def sb(name, shape, dt=F32):
            return ctx.enter_context(nc.sbuf_tensor(name, shape, dt))

        X = sb("X", [T, NT, D])
        AGG = sb("AGG", [T, NT, D])
        big = sb("big", [128, NT * INNER])
        KX = big[:, 0:KC * N].rearrange("p (k n) -> p k n", k=KC)
        QT = big[:, KC * N:2 * KC * N].rearrange("p (k n) -> p k n", k=KC)
        S = big[0:T, :].rearrange("p (t s) -> p t s", t=NT)
        W1 = sb("W1", [128, KC, FF])
        W2 = sb("W2", [128, FB, D])
        UT = [sb(f"UT{h}", [128, FB, n * T]) for h, (_, n) in enumerate(HALF)]
        WQK = sb("WQK", [128, KC, 2 * D])
        WVO = sb("WVO", [128, KC, 2 * D])
        WG = sb("WG", [128, KC, D])
        COLS = sb("COLS", [128, LAYERS * 16])
        XH = sb("XH", [T, G, D])
        XT = sb("XT", [128, KC, GW])
        QS = sb("QS", [128, KC, GW])
        KE = QS
        QZ = sb("QZ", [T, G, D])
        KT = sb("KT", [T, 2, D])
        GS = sb("GS", [128, KC, D])
        CM = sb("CM", [128, D])
        MS = sb("MS", [128, KC, D])
        B2M = sb("B2M", [128, KC, D])
        BVM = sb("BVM", [128, D])
        LB = sb("LB", [128, KC, T])
        BQ = sb("BQ", [T, D])
        BK = sb("BK", [128, KC])
        BV = sb("BV", [128, KC])
        B1 = sb("B1", [128, FB])
        BB2 = sb("BB2", [T, D])
        BO = sb("BO", [1, D])
        MASK = sb("MASK", [128, D])
        ident = sb("ident", [128, 128])
        ones = sb("ones", [128, 128])
        eighth = sb("eighth", [1, 128])
        ST = sb("ST", [T, G, 6])
        MV = sb("MV", [T, G, 2])
        NW = sb("NW", [T, 3, G])
        RSTD = sb("RSTD", [T, NT])
        NMR = sb("NMR", [T, NT])
        QM = sb("QM", [T, G * HEADS])
        MX = sb("MX", [128, KC, NG])
        KB = sb("KB", [128, KC])
        KS = sb("KS", [128, KC, NG])
        RS = sb("RS", [128, 2, KC])
        REC = sb("REC", [128, RC * 4])
        REC3 = REC[:, :].rearrange("p (c r) -> p c r", r=4)
        MSG = sb("MSG", [128, UNIT, D])
        IDS = sb("IDS", [128, UNIT], I32)
        HOT = sb("HOT", [128, HU, T])
        SLOT = sb("SLOT", [128, 2, SET, 4])
        AT = sb("AT", [128, 2, SET], I32)
        POSI = sb("POSI", [128, EC], I32)
        IOTA = sb("IOTA", [128, 512])
        BLK = sb("BLK", [1, NCH], I32)

        TRI = CM[:, 0:128]
        ENDC = sb("ENDC", [32, 4])
        BT = sb("BT", [128, NB])
        zeros = sb("zeros", [1, INNER])

        u0 = UT[0][:, :, :].rearrange("p a b -> p (a b)")
        u1 = UT[1][:, :, :].rearrange("p a b -> p (a b)")
        SRC, DST, EW = u0[:, 0:EC].bitcast(I32), u0[:, 400:400 + EC].bitcast(I32), u0[:, 800:800 + EC]
        SRCF, LOC, BKT = u0[:, 1200:1200 + EC], u0[:, 1600:1600 + EC], u0[:, 2000:2000 + EC]
        CNT, OFF, TOT = u0[:, 2400:2432], u0[:, 2440:2472], u0[:, 2480:2512]
        END, BASE = u0[:, 2520:2552], u0[:, 2560:2592]
        TOTI = u0[:, 2600:2632].bitcast(I32)
        HIT2, SCAN2 = u1[:, 1200:1200 + EC], u1[:, 1600:1600 + EC]
        HIT, SCAN, RANK = u1[:, 0:EC], u1[:, 400:400 + EC], u1[:, 800:800 + EC]
        POS, LANE = u1[:, 1200:1200 + EC].bitcast(I32), u1[:, 1600:1600 + EC].bitcast(I32)
        PAST = KX[0:32, 0, 0:NCH]
        REC0 = REC[:, 0:EC * 4].rearrange("p (c r) -> p c r", r=4)

        WXT = QS[:, :, :].rearrange("p k n -> p (k n)")[:, 0:4 * D].rearrange("p (j c) -> p j c", j=4)
        WXS = W1[:, :, 0:INNER]
        WFX = W1[:, :, INNER:2 * INNER]
        M2 = W2[:, 0:4, :]
        BOUT = W2[0:T, 4, :]
        wq_ = WQK[:, :, :].rearrange("p k n -> p (k n)")
        LBX = wq_[:, 0:4 * T].rearrange("p (j t) -> p j t", j=4)
        BD, TEMP, TI, BXC = wq_[:, 512:640], wq_[:, 640:648], wq_[:, 648:656], wq_[:, 656:660]
        BSL = wq_[0:T, 664:664 + FG]
        LBI = u1[0:T, 0:INNER]
        SZ = [u1[0:T, 600:600 + INNER], u1[0:T, 1200:1200 + INNER]]
        SMX = QM[:, 0:FH]
        SNEG = [QM[:, (1 + i) * FH:(2 + i) * FH] for i in range(2)]
        SSD = [QM[:, (3 + i) * FH:(4 + i) * FH] for i in range(2)]
        SSUM = GS[0:T, :, :].rearrange("p k n -> p (k n)")
        SC = [QZ[:, 0:2, :].rearrange("p a b -> p (a b)"), QZ[:, 2:4, :].rearrange("p a b -> p (a b)")]
        STT = [u0[:, 0:4 * T].rearrange("p (j t) -> p j t", j=4), u0[:, 512:512 + 4 * T].rearrange("p (j t) -> p j t", j=4)]
        YT = WVO[:, :, :]
        w8 = lambda a: a.rearrange("p (h c) -> p h c", h=FH)
        qk_ = WQK[0:FG, :, :].rearrange("p k n -> p (k n)")
        TK, TKT = qk_[:, 0:INNER], qk_[:, INNER:2 * INNER]
        gx = XT[0:FG, :, :].rearrange("p k n -> p (k n)")
        BFX, FQT = u0[0:FG, 2104:2104 + INNER], gx[:, INNER:2 * INNER]
        qx = QS[0:FG, :, :].rearrange("p k n -> p (k n)")
        FKT, FV = qx[:, 0:INNER], qx[:, INNER:2 * INNER]
        gs_ = GS[0:FG, :, :].rearrange("p k n -> p (k n)")
        AW = gs_[:, 0:INNER]
        ms_ = MS[0:FG, :, :].rearrange("p k n -> p (k n)")
        AWT = ms_[:, 0:INNER]
        OP = u0[0:FG, 1040:1040 + FH * 128].rearrange("p (h a) -> p h a", h=FH)
        WOUT = MSG[0:FG, :, :]
        WQKV = B2M[0:FG, :, :].rearrange("p k n -> p (k n)")[:, 0:3 * FD]
        DEN, AMX = sb("DEN", [FG, FH]), sb("AMX", [FG, FH])
        NRM = sb("NRM", [FG, FH])

        P = [ctx.enter_context(nc.psum_tensor(f"P{i}", [128, 512], F32)) for i in range(8)]
        WIDE, ROW, TURN, ACC = [P[0], P[1]], [P[2], P[3]], [P[4], P[5]], [P[6], P[7]]
        TP, QP = TURN

        def turned(bank):
            return bank[:, 0:256].rearrange("p (k t) -> p k t", k=KC)[:, :, 0:T]

        names = sorted({n for cs in COUNTS.values() for n in cs} | {
            "consts", "x_in", "w_g", "cols_in", "edges_in", "dve_step", "pool_step", "pe_step", "e_records", "e_counted",
            "e_offset", "e_placed", "e_ends", "e_past", "e_passed", "e_blocks", "e_zero", "e_zeroed", "e_back",
            "fold_in", "f_in", "f_bd", "f_lbx", "f_fold", "f_ready", "f_gone", "y_ready", "n_ready", "tk_ready", "tk_done",
            "tkt_ready", "tkt_done", "qkv_ready", "qkv_done", "aw_ready", "az_ready", "ae_ready", "aw_done",
            "awt_ready", "awt_done", "o_ready", "o_done", "m2_ready", "m2_done", "ssum_zero", "slots", "ids_ready",
            "e_bucketed", "e_rank", "dve_waited", "pool_waited"})
        sem = {n: ctx.enter_context(nc.semaphore(n)) for n in names}
        sent = [ctx.enter_context(nc.semaphore(f"sent{i}")) for i in range(2)]
        block = ctx.enter_context(nc.Block())

        def agg_bank(i):
            return ACC[i // 2][0:T, (i % 2) * D:(i % 2 + 1) * D]

        def span(at, n):
            return slice(at, at + n) if isinstance(at, int) else bass.ds(at, n)

        FOLD_LOADS, F_LOADS = 6 * 16, 7 * 16
        SLICES = ["calc_f", "norm_f"] + ["slices"] * (NG - 1) + ["slices_last"]
        MIXER = (["load_rest", "spread_b", "prep_qk"] + ["calc_in", "norm_in", "support"] * NG + A_STAGES * (NG - 1) + TAIL[1:] +
                 LAYER_STAGES * (LAYERS - 1) + LAST_STAGES)

        @block.sync
        def _(sp):
            for n in sorted({n for stage in COUNTS.values() for n in stage} - {"msgs0", "msgs1"}):
                sp.sem_inc(sem[n], 1)
            sp.sem_inc(sem["e_rank"], 1)
            c = Count(1)
            sp.dma_start(SRC, src).then_inc(sem["edges_in"], 16)
            sp.dma_start(DST, dst).then_inc(sem["edges_in"], 16)
            sp.dma_start(EW, ew).then_inc(sem["edges_in"], 16)
            sp.dma_start(AGG[:, :, :], x_t).then_inc(sem["x_in"], 16)
            sp.dma_start(WG[:, :, :], w_gnn).then_inc(sem["w_g"], 16)
            sp.dma_start(COLS[:, :], cols).then_inc(sem["cols_in"], 16)
            sp.wait_ge(sem["e_zero"], 1)
            sp.dma_start(rec_d.rearrange("(p c) r -> p (c r)", p=128), REC[:, :]).then_inc(sem["e_zeroed"], 16)

            def prep_qk(l):
                wait(sp, sem["row_done"], c("row_done"))
                sp.dma_start(WQK[:, :, :], w_qk[span(l, 1)].rearrange("l p k n -> p (l k) n")).then_inc(sem["w_qk"], 16)
                c.over("prep_qk")

            def load_rest(l):
                wait(sp, sem["row_done"], c("row_done"))
                for buf, w in ((WVO, w_vo), (W1, w_1), (W2, w_2)):
                    sp.dma_start(buf[:, :, :], w[span(l, 1)].rearrange("l p k n -> p (l k) n")).then_inc(sem["w_rest"], 16)
                sp.dma_start(BO[:, :], b_o[span(l, 1), :]).then_inc(sem["w_rest"], 16)
                sp.dma_start(BB2[:, :], b_2[span(l, 1), :].broadcast_to([T, D])).then_inc(sem["w_rest"], 16)
                c.over("load_rest")

            def support(g):
                sp.wait_ge(sem["row_done"], c("row_done") + G)
                sp.dma_start(sup_t[:, span(g * G, G), :], QZ[:, :, :]).then_inc(sem["sup_stored"], 16)
                c.over("support")

            layers(sp, c, {**idle_stages(c), "prep_qk": prep_qk, "load_rest": load_rest, "support": support})

            sp.wait_ge(sem["row_ready"], c("row_ready") - G - HALF[1][1])
            for a, b in ((WXT, w_xt), (TEMP, temp.broadcast_to([128, FH])), (BXC, b_x), (BSL, b_slice.broadcast_to([T, FG]))):
                sp.dma_start(a, b).then_inc(sem["fold_in"], 16)
            sp.wait_ge(sem["f_bd"], 1)
            for i in range(2):
                sp.dma_start(BD[FD * i:FD * (i + 1), FG * i:FG * (i + 1)], w_slice).then_inc(sem["fold_in"], 16)
            sp.wait_ge(sem["row_done"], c("row_done"))
            sp.wait_ge(sem["agg_done"], NCH + 1)
            for a, b in ((WFX, w_fx), (BOUT, b_out.broadcast_to([T, D])), (WOUT, w_out), (BFX, b_fx.broadcast_to([FG, INNER])),
                         (WQKV[:, 0:FD], w_q), (WQKV[:, FD:2 * FD], w_k), (WQKV[:, 2 * FD:3 * FD], w_v)):
                sp.dma_start(a, b).then_inc(sem["f_in"], 16)
            c.over(*SLICES)
            with c.loop(sp, 0, NG, ["finish"]) as g:
                sp.wait_ge(sem["row_done"], c("row_done") + G)
                sp.dma_start(out_t[:, span(g * G, G), :], X[:, span(g * G, G), :]).then_inc(sem["out_done"], 16)
                c.over("finish")
            sp.wait_ge(sem["out_done"], 16 * NG + 1)

        @block.gpsimd
        def _(pool):
            done = [0]

            def step(ins):
                done[0] += 1
                ins.then_inc(sem["pool_step"], 1)
                pool.wait_ge(sem["pool_step"], done[0])

            pool.memset(REC[:, :], 0.0).then_inc(sem["e_zero"], 1)
            step(pool.memset(ones[:, :], 1.0))
            step(pool.memset(MASK[:, :], 1.0))
            step(pool.memset(eighth[:, :], 1.0 / HEADS))
            step(pool.iota(IOTA[:, :], pattern=[[1, 512]], base=0, channel_multiplier=0,
                           allow_small_or_imprecise_dtypes=True))
            step(pool.affine_select(out=ident[:, :], in_=ones[:, :], compare_op=ALU.is_equal, fill=0.0,
                                    base=0, pattern=[[-1, 128]], channel_multiplier=1))
            step(pool.affine_select(out=TRI[:, :], in_=ones[:, :], compare_op=ALU.is_gt, fill=0.0,
                                    base=0, pattern=[[1, 128]], channel_multiplier=-1))
            for k in range(KC):
                mk = MASK[:, k * 128:(k + 1) * 128].rearrange("p (h d) -> p h d", d=DH)
                step(pool.affine_select(out=mk, in_=mk, compare_op=ALU.is_ge, fill=0.0, base=0,
                                        pattern=[[-DH, 128 // DH], [0, DH]], channel_multiplier=1))
                step(pool.affine_select(out=mk, in_=mk, compare_op=ALU.is_ge, fill=0.0, base=DH - 1,
                                        pattern=[[DH, 128 // DH], [0, DH]], channel_multiplier=-1))
            pool.memset(zeros[:, :], 0.0).then_inc(sem["consts"], 1)
            pool.wait_ge(sem["edges_in"], 48)
            step(pool.tensor_copy(SRCF, SRC))
            step(pool.tensor_scalar(LOC.bitcast(I32), SRCF, 1.0 / T, -(T - 1) / (2.0 * T), ALU.mult, ALU.add))
            step(pool.tensor_copy(BKT, LOC.bitcast(I32)))
            step(pool.tensor_scalar(BKT, BKT, float(T), None, ALU.mult))
            step(pool.tensor_tensor(LOC, SRCF, BKT, ALU.subtract))
            pool.iota(BT[:, :], pattern=[[T, NB]], base=0, channel_multiplier=0,
                      allow_small_or_imprecise_dtypes=True).then_inc(sem["e_bucketed"], 1)
            pool.wait_ge(sem["e_zeroed"], 16)
            step(pool.tensor_copy(REC0[:, :, 0].bitcast(I32), DST))
            step(pool.tensor_copy(REC0[:, :, 1], LOC))
            pool.tensor_copy(REC0[:, :, 2], EW).then_inc(sem["e_records"], 1)

            pool.wait_ge(sem["e_placed"], 1)
            pool.wait_ge(sem["e_records"], 1)
            def scatter(r):
                for i in range(2):
                    if not isinstance(r, int):
                        pool.wait_ge(sent[i], r * (16 * SET))
                    pool.tensor_copy(AT[:, i, :], POSI[:, span(r * UNIT + i * SET, SET)]).then_inc(sem["slots"], 1)
                    pool.tensor_copy(SLOT[:, i, :, :], REC0[:, span(r * UNIT + i * SET, SET), :]).then_inc(sem["slots"], 1)
                    pool.wait_ge(sem["slots"], r * 4 + 2 * i + 2)
                    apart(pool, sem["pool_waited"])
                    for j in range(SET):
                        pool.indirect_dma_start(rec_d, bass.IndirectOffsetOnAxis(ap=AT[:, i, j:j + 1], axis=0),
                                                SLOT[:, i, j, :], None).then_inc(sent[i], 16)
            scatter(0)
            with pool.Fori(1, EC // UNIT) as r:
                scatter(r)

            for i in range(2):
                pool.wait_ge(sent[i], 16 * EC // 2)
            pool.dma_start(REC[:, :], rec_d.rearrange("(p c) r -> p (c r)", p=128)).then_inc(sem["e_back"], 16)

            pool.wait_ge(sem["e_back"], 16)
            pool.wait_ge(sem["sup_stored"], 16 * NG + 1)

            def gather(r):
                for h in range(2):
                    if not isinstance(r, int):
                        pool.wait_ge(sem["agg_ready"], r * UNIT + (1 + (h + 1) * HU - UNIT))
                    half = slice(h * HU, (h + 1) * HU)
                    pool.tensor_copy(IDS[:, half], REC3[:, span(r * UNIT + h * HU, HU), 0].bitcast(I32)).then_inc(sem["ids_ready"], 1)
                    pool.wait_ge(sem["ids_ready"], r * 2 + h + 1)
                    apart(pool, sem["pool_waited"])
                    for i in range(h * HU, (h + 1) * HU):
                        pool.indirect_dma_start(MSG[:, i, :], None, sup_d,
                                                bass.IndirectOffsetOnAxis(ap=IDS[:, i:i + 1], axis=0)).then_inc(sem[f"msgs{h}"], 16)
            gather(0)
            with pool.Fori(1, NCH // UNIT) as r:
                gather(r)

            c = Count(1)
            c.over(*MIXER)
            pool.memset(BD, 0.0).then_inc(sem["f_bd"], 1)

            def x_sum(g):
                x_ = X[:, span(g * G, G), :]
                pool.tensor_tensor(x_, x_, AGG[:, span(g * G, G), :], ALU.add).then_inc(sem["x_summed"], 1)
            pool.wait_ge(sem["row_done"], c("row_done"))
            pool.wait_ge(sem["agg_done"], NCH + 1)
            x_sum(0)
            pool.memset(SSUM, 0.0).then_inc(sem["ssum_zero"], 1)
            pool.wait_ge(sem["ssum_zero"], 1)
            c.over("calc_f", "norm_f")

            def slices(g, more):
                if more:
                    x_sum(g + 1)
                for i in range(G):
                    pool.wait_ge(sem["s_ready"], c("s_ready") + i + 1)
                    pool.wait_ge(sem["s_summed"], c("s_summed") + i)
                    pool.tensor_tensor(SSUM, SSUM, S[:, span(g * G + i, 1), :].rearrange("p a s -> p (a s)"),
                                       ALU.add).then_inc(sem["s_summed"], 1)
                c.over("slices" if more else "slices_last")
            with c.loop(pool, 0, NG - 1, ["slices"]) as g:
                slices(g, True)
            slices(NG - 1, False)
            with c.loop(pool, 0, NG, ["finish"]) as g:
                for i in range(G):
                    pool.wait_ge(sem["st_ready"], c("st_ready") + max(i - 1, 0))
                    pool.tensor_copy(SC[i % 2], S[:, span(g * G + i, 1), :].rearrange("p a s -> p (a s)")).then_inc(sem["sc_ready"], 1)
                c.over("finish")

        @block.tensor
        def _(pe):
            c = Count(1)

            def row_free(i):
                if i == 0:
                    wait(pe, sem["row_done"], c("row_done"))
                elif i >= 2:
                    pe.wait_ge(sem["row_done"], c("row_done") + i - 1)

            def wide_free(i):
                if i == 0:
                    wait(pe, sem["wide_done"], c("wide_done"))
                elif i >= 2:
                    pe.wait_ge(sem["wide_done"], c("wide_done") + i - 1)

            def turns_free():
                for name in ("xt_done", "qt_done", "kt_done"):
                    wait(pe, sem[name], c(name))

            def norm(name):
                turns_free()
                for i in range(G):
                    pe.wait_ge(sem["xh_ready"], c("xh_ready") - G + i + 1)
                    if i >= 2:
                        pe.wait_ge(sem["xt_done"], c("xt_done") + i - 1)
                    for k in range(KC):
                        mm = pe.transpose(turned(TURN[i % 2])[:, k, :], XH[:, i, k * 128:(k + 1) * 128], ident[0:T, 0:T])
                    mm.then_inc(sem["xt_ready"], 1)
                c.over(name)

            def rows(lhs, rhs):
                for i in range(G):
                    row_free(i)
                    for k in range(KC):
                        mm = pe.matmul(ROW[i % 2][0:T, 0:D], lhs(k, i), rhs(k), start=(k == 0), stop=(k == KC - 1))
                    mm.then_inc(sem["row_ready"], 1)

            def support(g):
                pe.wait_ge(sem["xt_done"], c("xt_done"))
                rows(lambda k, i: XT[:, k, i * T:(i + 1) * T], lambda k: WG[:, k, :])
                c.over("support")

            def prep_qk(l):
                pe.wait_ge(sem["w_qk"], c("w_qk") + 16)
                pe.wait_ge(sem["lb_ready"], c("lb_ready"))
                wait(pe, sem["row_done"], c("row_done"))
                for k in range(KC):
                    pe.matmul(ROW[0][0:T, 0:D], LB[:, k, :], WQK[:, k, 0:D], start=(k == 0), stop=(k == KC - 1))
                for m in range(KC):
                    for k in range(KC):
                        mm = pe.matmul(ROW[1][:, m:m + 1], WQK[:, k, D + m * 128:D + (m + 1) * 128], LB[:, k, 0:1],
                                       start=(k == 0), stop=(k == KC - 1))
                mm.then_inc(sem["bqk_ready"], 1)
                c.over("prep_qk")

            def qk_set():
                pe.wait_ge(sem["qk_ready"], c("qk_ready"))

            def keys(g):
                n = 0
                for off, tiles in HALF:
                    pe.wait_ge(sem["xt_done"], c("xt_done") - G + off + tiles)
                    for m in range(KC):
                        wide_free(n)
                        for k in range(KC):
                            mm = pe.matmul(WIDE[n % 2][:, 0:tiles * T], WQK[:, k, D + m * 128:D + (m + 1) * 128],
                                           XT[:, k, off * T:(off + tiles) * T], start=(k == 0), stop=(k == KC - 1))
                        mm.then_inc(sem["wide_ready"], 1)
                        n += 1
                c.over("keys")

            def queries(g):
                rows(lambda k, i: XT[:, k, i * T:(i + 1) * T], lambda k: WQK[:, k, 0:D])
                c.over("queries")

            def turn_q(g):
                pe.wait_ge(sem["qn_ready"], c("qn_ready"))
                turns_free()
                for i in range(G):
                    if i >= 2:
                        pe.wait_ge(sem["qt_done"], c("qt_done") + i - 1)
                    for k in range(KC):
                        mm = pe.transpose(turned(TURN[i % 2])[:, k, :], QZ[:, i, k * 128:(k + 1) * 128], ident[0:T, 0:T])
                    mm.then_inc(sem["qt_ready"], 1)
                c.over("turn_q")

            def prep_biases(l):
                pe.wait_ge(sem["w_rest"], c("w_rest"))
                wait(pe, sem["row_done"], c("row_done"))
                ps = ROW[0]
                for j in range(KC):
                    for k in range(KC):
                        pe.matmul(ps[:, j:j + 1], WVO[:, k, j * 128:(j + 1) * 128], COLS[:, span(l * 16 + 2 + k, 1)],
                                  start=(k == 0), stop=(k == KC - 1))
                for j in range(FB):
                    for k in range(KC):
                        mm = pe.matmul(ps[:, 8 + j:9 + j], W1[:, k, j * 128:(j + 1) * 128], COLS[:, span(l * 16 + 6 + k, 1)],
                                       start=(k == 0), stop=(k == KC - 1))
                mm.then_inc(sem["bv_ready"], 1)
                c.over("prep_biases")

            def prep_m():
                pe.wait_ge(sem["bvm_ready"], c("bvm_ready"))
                for j in range(KC):
                    pe.matmul(ROW[1][:, j * D:(j + 1) * D], BVM[:, j * 128:(j + 1) * 128], WVO[:, j, D:2 * D],
                              start=True, stop=False)
                    mm = pe.matmul(ROW[1][:, j * D:(j + 1) * D], eighth[:, :], BO[:, :], start=False, stop=True)
                mm.then_inc(sem["b2m_ready"], 1)
                c.over("prep_m")

            def open_():
                wait(pe, sem["agg_done"], c("agg_done"))
                for m in range(KC):
                    pe.matmul(ACC[m][:, 0:D], zeros[:, 0:128], zeros[:, 0:D], start=True, stop=False,
                              skip_group_check=True)

            def context(g):
                def turn(i):
                    pe.wait_ge(sem["kexp"], c("kexp") + KC)
                    if i == 0:
                        turns_free()
                    elif i >= 2:
                        pe.wait_ge(sem["kt_done"], c("kt_done") + i - 1)
                    bank = TURN[i % 2]
                    for k in range(KC):
                        mm = pe.transpose(bank[0:T, k * 128:(k + 1) * 128], KE[:, k, i * T:(i + 1) * T], ident[:, :])
                    mm.then_inc(sem["kt_ready"], 1)

                def add(i):
                    pe.wait_ge(sem["kt_done"], c("kt_done") + i + 1)
                    pe.wait_ge(sem["bxh_ready"], c("bxh_ready") + i + 1)
                    for m in range(KC):
                        mm = pe.matmul(ACC[m][:, 0:D], XH[:, i, m * 128:(m + 1) * 128], KT[:, i % 2, :],
                                       start=False, stop=False, skip_group_check=True)
                    mm.then_inc(sem["g_acc"], 1)
                turn(0)
                for i in range(1, G):
                    turn(i)
                    add(i - 1)
                add(G - 1)
                c.over("context")


            def fold():
                for m in range(KC):
                    mm = pe.matmul(ACC[m][:, 0:D], zeros[:, 0:128], zeros[:, 0:D], start=False, stop=True,
                                   skip_group_check=True)
                mm.then_inc(sem["g_closed"], 1)
                pe.wait_ge(sem["gs_ready"], c("gs_ready") + 1)
                turns_free()
                for j in range(KC):
                    cols_ = slice(j * 128, (j + 1) * 128)
                    for k in range(KC):
                        mm = pe.matmul(TP[:, cols_], WVO[:, k, cols_], GS[:, k, cols_], start=(k == 0), stop=(k == KC - 1))
                mm.then_inc(sem["cm_ready"], 1)
                pe.wait_ge(sem["cm_done"], c("cm_done") + 1)
                pe.wait_ge(sem["rest_ready"], c("rest_ready"))
                for j in range(KC):
                    mm = pe.matmul(ROW[j][:, 0:D], CM[:, j * 128:(j + 1) * 128], WVO[:, j, D:2 * D], start=True, stop=True)
                mm.then_inc(sem["m_ready"], 1)
                pe.wait_ge(sem["ms_done"], c("ms_done") + 1)
                c.over("fold")

            def attend(g):
                pe.wait_ge(sem["qs_ready"], c("qs_ready"))
                rows(lambda k, i: QS[:, k, i * T:(i + 1) * T], lambda k: MS[:, k, :])
                c.over("attend")

            def up(l, g, h):
                off, tiles = HALF[h]
                if h == 0:
                    pe.wait_ge(sem["xt_done"], c("xt_done"))
                for j in range(FB):
                    wide_free(j)
                    for k in range(KC):
                        mm = pe.matmul(WIDE[j % 2][:, 0:tiles * T], W1[:, k, j * 128:(j + 1) * 128],
                                       KX[:, k, span(g * GW + off * T, tiles * T)], start=(k == 0), stop=(k == KC - 1))
                    mm.then_inc(sem["wide_ready"], 1)
                c.over(f"up{h}")

            def down(g, h):
                off, tiles = HALF[h]
                pe.wait_ge(sem["wide_done"], c("wide_done"))
                for i in range(tiles):
                    row_free(i)
                    for j in range(FB):
                        mm = pe.matmul(ROW[i % 2][0:T, 0:D], UT[h][:, j, i * T:(i + 1) * T], W2[:, j, :],
                                       start=(j == 0), stop=(j == FB - 1))
                    mm.then_inc(sem["row_ready"], 1)
                c.over(f"down{h}")

            def edges(p):
                pe.wait_ge(sem["hot_ready"], c("hot_ready"))
                pe.wait_ge(sem[f"msgs{p}"], c(f"msgs{p}") + 16 * HU - 1)
                wait(pe, sem["agg_done"], c("agg_done"))
                for i in range(HU):
                    pe.matmul(agg_bank(i), HOT[:, i, :], MSG[:, p * HU + i, :], start=True,
                              stop=True).then_inc(sem["agg_ready"], 1)
                c.over(f"edges{p}")

            pe.wait_ge(sem["consts"], 1)
            pe.wait_ge(sem["e_counted"], 1)
            pe.matmul(P[6][:, 0:NB], TRI[:, :], CNT[:, 0:NB], start=True, stop=True)
            pe.matmul(P[6][:, 32:32 + NB], ones[:, :], CNT[:, 0:NB], start=True, stop=True).then_inc(sem["e_offset"], 1)
            pe.wait_ge(sem["e_ends"], 1)
            pe.matmul(P[7][0:NT, 0:1], END[0:1, 0:NT], ones[0:1, 0:1], start=True, stop=True).then_inc(sem["e_past"], 1)
            pe.wait_ge(sem["e_passed"], 1)
            pe.matmul(P[7][0:1, 0:NCH], ones[0:NT, 0:1], PAST[0:NT, :], start=True, stop=True).then_inc(sem["e_blocks"], 1)
            pe.wait_ge(sem["w_g"], 16)
            pe.wait_ge(sem["cols_in"], 16)

            layers(pe, c, {
                **idle_stages(c), "prep_qk": prep_qk, "qk_set": qk_set, "support": support,
                "norm_in": lambda g: norm("norm_in"), "norm_a": lambda g: norm("norm_a"),
                "norm_c": lambda g: norm("norm_c"), "keys": keys, "queries": queries, "turn_q": turn_q, "open": open_,
                "context": context, "prep_biases": prep_biases, "prep_m": prep_m, "fold": fold, "attend": attend,
                "up": up, "down": down, "edges": edges})

            pe.wait_ge(sem["fold_in"], FOLD_LOADS)
            pe.wait_ge(sem["agg_done"], NCH + 1)
            wait(pe, sem["row_done"], c("row_done"))
            for j in range(4):
                js = slice(j * 128, (j + 1) * 128)
                for m in range(KC):
                    pe.matmul(ACC[m][:, js], WXT[:, j, m * 128:(m + 1) * 128], BD, start=True, stop=True)
            pe.wait_ge(sem["f_lbx"], 1)
            for j in range(4):
                mm = pe.matmul(ROW[0][0:T, j * 128:(j + 1) * 128], LBX[:, j, :], BD, start=True, stop=True)
            mm.then_inc(sem["f_fold"], 1)
            c.over("calc_f")
            norm("norm_f")
            pe.wait_ge(sem["f_ready"], 1)
            for m in range(KC):
                pe.matmul(ACC[m][:, :], zeros[:, 0:128], zeros[:, :], start=True, stop=False, skip_group_check=True)

            def slices(g, more):
                def logit(i):
                    row_free(i)
                    pe.wait_ge(sem["xt_done"], c("xt_done") - G + i + 1)
                    for k in range(KC):
                        mm = pe.matmul(ROW[i % 2][0:T, :], XT[:, k, i * T:(i + 1) * T], WXS[:, k, :],
                                       start=(k == 0), stop=(k == KC - 1))
                    mm.then_inc(sem["row_ready"], 1)

                def token(i):
                    pe.wait_ge(sem["s_ready"], c("s_ready") + i + 1)
                    for m in range(KC):
                        mm = pe.matmul(ACC[m][:, :], XH[:, i, m * 128:(m + 1) * 128],
                                       S[:, span(g * G + i, 1), :].rearrange("p a s -> p (a s)"),
                                       start=False, stop=False, skip_group_check=True)
                    mm.then_inc(sem["tok"], 1)

                def turn(i):
                    if more:
                        if i == 0:
                            wait(pe, sem["xt_done"], c("xt_done"))
                        elif i >= 2:
                            pe.wait_ge(sem["xt_done"], c("xt_done") + i - 1)
                        pe.wait_ge(sem["xh_ready"], c("xh_ready") + i + 1)
                        for k in range(KC):
                            mm = pe.transpose(turned(TURN[i % 2])[:, k, :], XH[:, i, k * 128:(k + 1) * 128], ident[0:T, 0:T])
                        mm.then_inc(sem["xt_ready"], 1)
                logit(0)
                logit(1)
                token(0)
                for i in range(2, G):
                    logit(i)
                    token(i - 1)
                    turn(i - 2)
                token(G - 1)
                turn(G - 2)
                turn(G - 1)
                c.over("slices" if more else "slices_last")
            with c.loop(pe, 0, NG - 1, ["slices"]) as g:
                slices(g, True)
            slices(NG - 1, False)
            for m in range(KC):
                mm = pe.matmul(ACC[m][:, :], zeros[:, 0:128], zeros[:, :], start=False, stop=True, skip_group_check=True)
            mm.then_inc(sem["y_ready"], 1)
            pe.wait_ge(sem["f_in"], F_LOADS)
            pe.wait_ge(sem["s_summed"], NT + 1)
            wait(pe, sem["row_done"], c("row_done"))
            for h in range(FH):
                mm = pe.matmul(TP[0:FG, h:h + 1], SSUM[:, h * FG:(h + 1) * FG], ones[0:T, 0:1], start=True, stop=True)
            mm.then_inc(sem["n_ready"], 1)
            pe.wait_ge(sem["y_ready"], 2)
            for h in range(FH):
                for k in range(KC):
                    mm = pe.matmul(ROW[0][0:FG, h * FD:(h + 1) * FD], YT[:, k, h * FG:(h + 1) * FG],
                                   WFX[:, k, h * FD:(h + 1) * FD], start=(k == 0), stop=(k == KC - 1))
            mm.then_inc(sem["tk_ready"], 1)
            pe.wait_ge(sem["tk_done"], 1)
            for h in range(FH):
                mm = pe.transpose(QP[0:FD, h * FG:(h + 1) * FG], TK[:, h * FD:(h + 1) * FD], ident[0:FG, 0:FG])
            mm.then_inc(sem["tkt_ready"], 1)
            pe.wait_ge(sem["tkt_done"], 1)
            pe.matmul(WIDE[0][0:FD, :], WQKV[:, 0:FD], TKT, start=True, stop=True)
            pe.matmul(WIDE[1][0:FD, :], WQKV[:, FD:2 * FD], TKT, start=True, stop=True)
            for h in range(FH):
                mm = pe.matmul(ROW[1][0:FG, h * FD:(h + 1) * FD], TKT[:, h * FG:(h + 1) * FG], WQKV[:, 2 * FD:3 * FD],
                               start=True, stop=True)
            mm.then_inc(sem["qkv_ready"], 1)
            pe.wait_ge(sem["qkv_done"], 1)
            for h in range(FH):
                hs = slice(h * FG, (h + 1) * FG)
                mm = pe.matmul(ROW[0][0:FG, hs], FQT[:, hs], FKT[:, hs], start=True, stop=True)
            mm.then_inc(sem["aw_ready"], 1)
            pe.wait_ge(sem["aw_done"], 1)
            for h in range(FH):
                hs = slice(h * FG, (h + 1) * FG)
                mm = pe.transpose(QP[0:FG, hs], AW[:, hs], ident[0:FG, 0:FG])
            mm.then_inc(sem["awt_ready"], 1)
            pe.wait_ge(sem["awt_done"], 1)
            for h in range(FH):
                hs = slice(h * FG, (h + 1) * FG)
                mm = pe.matmul(ROW[1][0:FD, hs], FV[:, h * FD:(h + 1) * FD], AWT[:, hs], start=True, stop=True)
            mm.then_inc(sem["o_ready"], 1)
            pe.wait_ge(sem["o_done"], 1)
            for j in range(4):
                for a in range(2):
                    mm = pe.matmul(ACC[j // 2][:, (j % 2) * D:(j % 2 + 1) * D], OP[:, 2 * j + a, :], WOUT[:, 2 * j + a, :],
                                   start=(a == 0), stop=(a == 1))
            mm.then_inc(sem["m2_ready"], 1)
            pe.wait_ge(sem["m2_done"], 1)
            with c.loop(pe, 0, NG, ["finish"]) as g:
                def turn(i):
                    pe.wait_ge(sem["sc_ready"], c("sc_ready") + i + 1)
                    pe.wait_ge(sem["st_done"], c("st_done") + i)
                    for j in range(4):
                        mm = pe.transpose(TP[:, j * T:(j + 1) * T], SC[i % 2][:, j * 128:(j + 1) * 128], ident[0:T, 0:T])
                    mm.then_inc(sem["st_ready"], 1)

                def put(i):
                    pe.wait_ge(sem["st_done"], c("st_done") + i + 1)
                    row_free(i)
                    for j in range(4):
                        mm = pe.matmul(ROW[i % 2][0:T, 0:D], STT[i % 2][:, j, :], M2[:, j, :], start=(j == 0), stop=(j == 3))
                    mm.then_inc(sem["row_ready"], 1)
                turn(0)
                for i in range(1, G):
                    turn(i)
                    put(i - 1)
                put(G - 1)
                c.over("finish")

        @block.scalar
        def _(act):
            c = Count(1)

            def norm(name, g, out_, readers):
                for sem_ in readers:
                    wait(act, sem[sem_], c(sem_))
                for i in range(G):
                    act.wait_ge(sem["xt_ready"], c("xt_ready") + i + 1)
                    act.activation(out_(g, i), turned(TURN[i % 2]), ACT.Copy).then_inc(sem["xt_done"], 1)
                c.over(name)

            def support(g):
                wait(act, sem["sup_stored"], c("sup_stored"))
                for i in range(G):
                    act.wait_ge(sem["row_ready"], c("row_ready") + i + 1)
                    act.activation(QZ[:, i, :], ROW[i % 2][0:T, 0:D], ACT.Copy).then_inc(sem["row_done"], 1)
                c.over("support")

            def to_xt(g, i):
                return XT[:, :, i * T:(i + 1) * T]

            def to_kx(g, i):
                return KX[:, :, span(g * GW + i * T, T)]

            def keys(g):
                n = 0
                for off, tiles in HALF:
                    for m in range(KC):
                        act.wait_ge(sem["wide_ready"], c("wide_ready") + n + 1)
                        act.activation(KX[:, m, span(g * GW + off * T, tiles * T)], WIDE[n % 2][:, 0:tiles * T],
                                       ACT.Identity, bias=BK[:, m:m + 1]).then_inc(sem["wide_done"], 1)
                        n += 1
                c.over("keys")

            def soften():
                act.wait_ge(sem["qz_ready"], c("qz_ready"))
                act.activation(QZ[:, :, :], QZ[:, :, :], ACT.Exp, scale=QSCALE).then_inc(sem["qe_ready"], 1)
                c.over("soften")

            def fetch_q(g):
                act.wait_ge(sem["qt_done"], c("qt_done"))
                act.wait_ge(sem["row_ready"], c("row_ready"))
                act.wait_ge(sem["kt_ready"], c("kt_ready"))
                act.activation(QS[:, :, :], QT[:, :, span(g * GW, GW)], ACT.Copy).then_inc(sem["qs_ready"], 1)
                c.over("fetch_q")

            def turn_q(g):
                wait(act, sem["qs_ready"], c("qs_ready"))
                for i in range(G):
                    act.wait_ge(sem["qt_ready"], c("qt_ready") + i + 1)
                    act.activation(QT[:, :, span(g * GW + i * T, T)], turned(TURN[i % 2]), ACT.Copy).then_inc(sem["qt_done"], 1)
                c.over("turn_q")

            def context(g):
                act.wait_ge(sem["kmax_ready"], c("kmax_ready"))
                wait(act, sem["kt_ready"], c("kt_ready"))
                for k in range(KC):
                    act.activation(KE[:, k, :], KX[:, k, span(g * GW, GW)], ACT.Exp, bias=KB[:, k:k + 1], scale=QSCALE,
                                   accum_out=KS[:, k, span(g, 1)]).then_inc(sem["kexp"], 1)
                for i in range(G):
                    act.wait_ge(sem["kt_ready"], c("kt_ready") + i + 1)
                    if i != 1:
                        wait(act, sem["g_acc"], c("g_acc") + max(i - 1, 0))
                    act.activation(KT[:, i % 2, :], TURN[i % 2][0:T, 0:D], ACT.Copy).then_inc(sem["kt_done"], 1)
                c.over("context")

            def up(l, g, h):
                off, tiles = HALF[h]
                for j in range(FB):
                    act.wait_ge(sem["wide_ready"], c("wide_ready") + j + 1)
                    act.activation(UT[h][:, j, :], WIDE[j % 2][:, 0:tiles * T], ACT.Gelu,
                                   bias=B1[:, j:j + 1]).then_inc(sem["wide_done"], 1)
                c.over(f"up{h}")

            layers(act, c, {
                **idle_stages(c), "support": support, "norm_in": lambda g: norm("norm_in", g, to_xt, ["row_ready"]),
                "norm_a": lambda g: norm("norm_a", g, to_xt, ["row_ready", "wide_ready"]),
                "norm_c": lambda g: norm("norm_c", g, to_kx, ["kt_ready"]),
                "keys": keys, "soften": soften, "turn_q": turn_q, "context": context, "fetch_q": fetch_q, "up": up})

            c.over("calc_f")
            norm("norm_f", 0, to_xt, ["row_ready"])

            def slices(g, more):
                def exp(i):
                    act.wait_ge(sem["sz_ready"], c("sz_ready") + i + 1)
                    for h in range(FH):
                        z = SZ[i % 2][:, h * FG:(h + 1) * FG]
                        ins = act.activation(z, z, ACT.Exp, bias=SNEG[i % 2][:, h:h + 1], accum_out=SSD[i % 2][:, h:h + 1])
                    ins.then_inc(sem["se_ready"], 1)

                def turned_tile(i):
                    if more:
                        act.wait_ge(sem["row_ready"], c("row_ready") + i + 1)
                        act.wait_ge(sem["xt_ready"], c("xt_ready") + i + 1)
                        act.activation(to_xt(g, i), turned(TURN[i % 2]), ACT.Copy).then_inc(sem["xt_done"], 1)
                for i in range(G):
                    exp(i)
                    if i >= 2:
                        turned_tile(i - 2)
                turned_tile(G - 2)
                turned_tile(G - 1)
                c.over("slices" if more else "slices_last")
            with c.loop(act, 0, NG - 1, ["slices"]) as g:
                slices(g, True)
            slices(NG - 1, False)
            act.wait_ge(sem["az_ready"], 1)
            act.activation(AW, AW, ACT.Exp, scale=FD ** -0.5).then_inc(sem["ae_ready"], 1)
            with c.loop(act, 0, NG, ["finish"]) as g:
                for i in range(G):
                    act.wait_ge(sem["st_ready"], c("st_ready") + i + 1)
                    wait(act, sem["row_ready"], c("row_ready") + max(i - 1, 0))
                    act.activation(STT[i % 2], TP[:, 0:4 * T].rearrange("p (j t) -> p j t", j=4),
                                   ACT.Copy).then_inc(sem["st_done"], 1)
                c.over("finish")

        @block.vector
        def _(dve):
            c = Count(1)

            def step(ins):
                ins.then_inc(sem["dve_step"], 1)
                c.own["dve_step"] += 1
                dve.wait_ge(sem["dve_step"], c("dve_step"))

            def tiles_of(buf, g):
                return buf[:, span(g * G, G), :]

            def stats(g, src_):
                for i in range(G):
                    ins = dve.bn_stats(ST[:, i, :], src_[:, span(g * G + i, 1), :].rearrange("p a d -> p (a d)"))
                step(ins)
                apart(dve, sem["dve_waited"])
                for i in range(G):
                    ins = dve.bn_aggr(MV[:, i, :], ST[:, i, :])
                step(ins)
                rs, nm = RSTD[:, span(g * G, G)], NMR[:, span(g * G, G)]
                v, y, z = NW[:, 0, :], NW[:, 1, :], NW[:, 2, :]
                step(dve.tensor_scalar_add(v, MV[:, :, 1], EPS))
                step(dve.tensor_single_scalar(z.bitcast(I32), v.bitcast(I32), 1, ALU.logical_shift_right))
                step(dve.tensor_scalar(y.bitcast(I32), z.bitcast(I32), -1.0, MAGIC, ALU.mult, ALU.add))
                for n in range(3):
                    step(dve.scalar_tensor_tensor(z, y, -0.5, y, ALU.mult, ALU.mult))
                    step(dve.tensor_tensor(z, z, v, ALU.mult))
                    step(dve.scalar_tensor_tensor(rs if n == 2 else y, z, 1.5, y, ALU.add, ALU.mult))
                step(dve.scalar_tensor_tensor(nm, MV[:, :, 0], -1.0, rs, ALU.mult, ALU.mult))

            def calc(name, g, src_, keep=False, bias=None):
                wait(dve, sem["row_done"], c("row_done"))
                apart(dve, sem["dve_waited"])
                stats(g, src_)
                wait(dve, sem["xt_ready"], c("xt_ready"))
                wait(dve, sem["g_acc"], c("g_acc"))
                for i in range(G):
                    t = span(g * G + i, 1)
                    dve.tensor_scalar(XH[:, i, :], src_[:, t, :].rearrange("p a d -> p (a d)"), RSTD[:, t], NMR[:, t],
                                      ALU.mult, ALU.add).then_inc(sem["xh_ready"], 1)
                    if keep:
                        dve.tensor_scalar(X[:, t, :].rearrange("p a d -> p (a d)"), src_[:, t, :].rearrange("p a d -> p (a d)"),
                                          RSTD[:, t], NMR[:, t], ALU.mult, ALU.add)
                if bias is not None:
                    dve.wait_ge(sem["xh_ready"], c("xh_ready") + G)
                    step(dve.tensor_tensor(tiles_of(X, g), tiles_of(X, g), bias.unsqueeze(1).broadcast_to([T, G, D]), ALU.add))
                    apart(dve, sem["dve_waited"])
                c.rest(name)

            def add_rows(g, off, tiles):
                for i in range(tiles):
                    t = span(g * G + off + i, 1)
                    x_ = X[:, t, :].rearrange("p a d -> p (a d)")
                    dve.wait_ge(sem["row_ready"], c("row_ready") + i + 1)
                    dve.tensor_tensor(x_, ROW[i % 2][0:T, 0:D], x_, ALU.add).then_inc(sem["row_done"], 1)

            def spread_b(l):
                for k in range(KC):
                    ins = dve.tensor_scalar(LB[:, k, :], ones[:, 0:T], COLS[:, span(l * 16 + 2 + k, 1)], None, ALU.mult)
                ins.then_inc(sem["lb_ready"], 1)
                c.rest("spread_b")

            def prep_qk(l):
                dve.wait_ge(sem["bqk_ready"], c("bqk_ready") + 1)
                wait(dve, sem["wide_done"], c("wide_done"))
                dve.tensor_copy(BQ[:, :], ROW[0][0:T, 0:D])
                dve.tensor_copy(BK[:, :], ROW[1][:, 0:KC])
                for k in range(KC):
                    ins = dve.tensor_scalar(WQK[:, k, :], WQK[:, k, :], COLS[:, span(l * 16 + k, 1)], None, ALU.mult)
                ins.then_inc(sem["qk_ready"], 1)
                c.rest("prep_qk")

            def keys(g):
                dve.wait_ge(sem["wide_done"], c("wide_done") + 2 * KC)
                step(dve.tensor_reduce(MX[:, :, span(g, 1)], KX[:, :, span(g * GW, GW)], axis=AX_X, op=ALU.max))
                c.rest("keys")

            def queries(g):
                wait(dve, sem["qt_ready"], c("qt_ready"))
                wait(dve, sem["sup_stored"], c("sup_stored"))
                for i in range(G):
                    dve.wait_ge(sem["row_ready"], c("row_ready") + i + 1)
                    dve.tensor_tensor(QZ[:, i, :], ROW[i % 2][0:T, 0:D], BQ[:, :], ALU.add).then_inc(sem["row_done"], 1)
                z = QZ[:, :, :].rearrange("p g (h d) -> p (g h) d", d=DH)
                m = QM[:, :].unsqueeze(2).broadcast_to([T, G * HEADS, DH])
                dve.wait_ge(sem["row_done"], c("row_done") + G)
                step(dve.tensor_reduce(QM[:, :], z, axis=AX_X, op=ALU.max))
                dve.tensor_tensor(z, z, m, ALU.subtract).then_inc(sem["qz_ready"], 1)
                c.rest("queries")

            def soften():
                z = QZ[:, :, :].rearrange("p g (h d) -> p (g h) d", d=DH)
                m = QM[:, :].unsqueeze(2).broadcast_to([T, G * HEADS, DH])
                dve.wait_ge(sem["qe_ready"], c("qe_ready") + 1)
                step(dve.tensor_reduce(QM[:, :], z, axis=AX_X, op=ALU.add))
                step(dve.reciprocal(QM[:, :], QM[:, :]))
                dve.tensor_tensor(z, z, m, ALU.mult).then_inc(sem["qn_ready"], 1)
                c.rest("soften")

            def kmax():
                wait(dve, sem["kexp"], c("kexp"))
                step(dve.tensor_reduce(KB[:, :], MX[:, :, :], axis=AX_X, op=ALU.max))
                dve.tensor_scalar(KB[:, :], KB[:, :], -QSCALE, None, ALU.mult).then_inc(sem["kmax_ready"], 1)
                c.rest("kmax")

            def prep_biases(l):
                dve.wait_ge(sem["bv_ready"], c("bv_ready") + 1)
                wait(dve, sem["wide_done"], c("wide_done"))
                dve.tensor_tensor(B1[:, :], ROW[0][:, 8:8 + FB], COLS[:, span(l * 16 + 8, FB)], ALU.add)
                step(dve.tensor_copy(BV[:, :], ROW[0][:, 0:KC]))
                for j in range(KC):
                    ins = dve.tensor_scalar(BVM[:, j * 128:(j + 1) * 128], MASK[:, j * 128:(j + 1) * 128], BV[:, j:j + 1],
                                            None, ALU.mult)
                ins.then_inc(sem["bvm_ready"], 1)
                for k in range(KC):
                    dve.tensor_scalar(WVO[:, k, 0:D], WVO[:, k, 0:D], COLS[:, span(l * 16 + k, 1)], None, ALU.mult)
                    dve.tensor_scalar(W1[:, k, :], W1[:, k, :], COLS[:, span(l * 16 + 4 + k, 1)], None, ALU.mult)
                c.rest("prep_biases")

            def prep_m():
                dve.wait_ge(sem["b2m_ready"], c("b2m_ready") + 1)
                dve.tensor_copy(B2M[:, :, :], ROW[1][:, :].rearrange("p (k n) -> p k n", k=KC)).then_inc(sem["rest_ready"], 1)
                c.rest("prep_m")

            def context(g):
                wait(dve, sem["xt_ready"], c("xt_ready"))
                wait(dve, sem["g_acc"], c("g_acc"))
                for i in range(G):
                    t = span(g * G + i, 1)
                    dve.tensor_scalar(XH[:, i, :], X[:, t, :].rearrange("p a d -> p (a d)"), RSTD[:, t], NMR[:, t],
                                      ALU.mult, ALU.add).then_inc(sem["bxh_ready"], 1)
                c.rest("context")

            def fold():
                dve.wait_ge(sem["kexp"], c("kexp"))
                step(dve.tensor_reduce(RS[:, 0, :], KS[:, :, :], axis=AX_X, op=ALU.add))
                step(dve.reciprocal(RS[:, 1, :], RS[:, 0, :]))
                dve.wait_ge(sem["g_closed"], c("g_closed") + 1)
                for m in range(KC):
                    ins = dve.tensor_copy(GS[:, m, :], ACC[m][:, 0:D])
                ins.then_inc(sem["gs_ready"], 1)
                dve.wait_ge(sem["cm_ready"], c("cm_ready") + 1)
                dve.tensor_tensor(CM[:, :], TP[:, 0:D], MASK[:, :], ALU.mult).then_inc(sem["cm_done"], 1)
                dve.wait_ge(sem["m_ready"], c("m_ready") + 1)
                for j in range(KC):
                    ins = dve.scalar_tensor_tensor(MS[:, j, :], ROW[j][:, 0:D], RS[:, 1, j:j + 1], B2M[:, j, :],
                                                   ALU.mult, ALU.add)
                ins.then_inc(sem["ms_done"], 1)
                c.rest("fold")

            def attend(g):
                add_rows(g, 0, G)
                c.rest("attend")

            def down(g, h):
                add_rows(g, *HALF[h])
                c.rest(f"down{h}")

            def hot(chunk, i):
                rec = REC3[:, span(chunk, 1), :].rearrange("p a r -> p (a r)")
                dve.tensor_scalar(HOT[:, i, :], IOTA[:, 0:T], rec[:, 1:2], rec[:, 2:3], ALU.is_equal,
                                  ALU.mult).then_inc(sem["hot_ready"], 1)

            def edges_first():
                dve.wait_ge(sem["e_back"], 16)
                for i in range(HU):
                    hot(c("agg_ready") + (i - 1), i)
                c.rest("edges_first")

            def edges(p):
                chunk = [c("agg_ready") + (i - 1) for i in range(HU)]
                tile = [dve.value_load(BLK[0:1, span(chunk[i], 1)], min_val=0, max_val=NT - 1) for i in range(HU)]
                for i in range(HU):
                    a = AGG[:, bass.ds(tile[i], 1), :].rearrange("p a d -> p (a d)")
                    dve.wait_ge(sem["agg_ready"], c("agg_ready") + (i // 2 + 1) * 2)
                    wait(dve, sem["agg_done"], c("agg_done") + i)
                    dve.tensor_tensor(a, agg_bank(i), a, ALU.add).then_inc(sem["agg_done"], 1)
                    hot(chunk[i] + HU, i)
                c.rest(f"edges{p}")

            def place(g):
                def hit(j):
                    b = g * PB + j
                    dve.tensor_scalar([HIT, SCAN][j % 2], BKT, BT[:, span(b, 1)], OFF[:, span(b, 1)], ALU.is_equal,
                                      ALU.mult).then_inc(sem["placed_by"], 1)
                wait(dve, sem["placed_by"], c("placed_by"))
                hit(0)
                for j in range(PB):
                    dve.wait_ge(sem["placed_by"], c("placed_by") + 2 * j + 1)
                    if j + 1 < PB:
                        hit(j + 1)
                    dve.tensor_tensor(RANK, RANK, [HIT, SCAN][j % 2], ALU.add).then_inc(sem["placed_by"], 1)
                c.rest("place")

            def placed():
                dve.wait_ge(sem["placed_by"], c("placed_by"))
                step(dve.tensor_copy(POS, RANK))
                step(dve.tensor_single_scalar(LANE, POS, 127, ALU.bitwise_and))
                step(dve.tensor_single_scalar(POS, POS, 7, ALU.logical_shift_right))
                dve.scalar_tensor_tensor(POSI[:, :], LANE, float(RC), POS, ALU.mult, ALU.add).then_inc(sem["e_placed"], 1)
                c.rest("placed")

            dve.memset(RANK, 0.0)
            dve.wait_ge(sem["consts"], 1)
            dve.wait_ge(sem["e_bucketed"], 1)
            with dve.Fori(0, NB // 2) as r:
                n = r * 8
                two = ((r * 2, HIT, SCAN), (r * 2 + 1, HIT2, SCAN2))
                for b, hit, _ in two:
                    dve.tensor_scalar(hit, BKT, BT[:, span(b, 1)], None, ALU.is_equal).then_inc(sem["e_rank"], 1)
                for i, (_, hit, scan) in enumerate(two):
                    dve.wait_ge(sem["e_rank"], n + 2 + i)
                    dve.tensor_tensor_scan(scan, hit, hit, 0.0, ALU.add, ALU.bypass).then_inc(sem["e_rank"], 1)
                for i, (b, hit, scan) in enumerate(two):
                    dve.wait_ge(sem["e_rank"], n + 4 + i)
                    dve.tensor_copy(CNT[:, span(b, 1)], scan[:, EC - 1:EC])
                    dve.tensor_tensor(hit, hit, scan, ALU.mult).then_inc(sem["e_rank"], 1)
                for i, (_, hit, _) in enumerate(two):
                    dve.wait_ge(sem["e_rank"], n + 6 + 2 * i)
                    dve.tensor_tensor(RANK, RANK, hit, ALU.add).then_inc(sem["e_rank"], 1)
                dve.wait_ge(sem["e_rank"], n + 9)
            dve.sem_inc(sem["e_counted"], 1)
            dve.wait_ge(sem["e_offset"], 1)
            step(dve.tensor_scalar(TOTI[:, 0:NB], P[6][:, 32:32 + NB], 127.0, None, ALU.add))
            step(dve.tensor_scalar(TOTI[:, 0:NB], TOTI[:, 0:NB], 7, 7, ALU.logical_shift_right, ALU.logical_shift_left))
            step(dve.tensor_copy(TOT[:, 0:NB], TOTI[:, 0:NB]))
            step(dve.tensor_tensor_scan(END[:, 0:NB], TOT[:, 0:NB], TOT[:, 0:NB], 0.0, ALU.add, ALU.bypass))
            step(dve.tensor_tensor(BASE[:, 0:NB], END[:, 0:NB], TOT[:, 0:NB], ALU.subtract))
            step(dve.scalar_tensor_tensor(OFF[:, 0:NB], P[6][:, 0:NB], -1.0, BASE[:, 0:NB], ALU.add, ALU.add))
            dve.sem_inc(sem["e_ends"], 1)
            dve.wait_ge(sem["e_past"], 1)
            step(dve.tensor_scalar(ENDC[0:NT, 0:1], P[7][0:NT, 0:1], 1.0 / 128, None, ALU.mult))
            dve.tensor_scalar(PAST[0:NT, :], IOTA[0:NT, 0:NCH], ENDC[0:NT, 0:1], None, ALU.is_ge).then_inc(sem["e_passed"], 1)
            dve.wait_ge(sem["e_blocks"], 1)
            step(dve.tensor_scalar(BLK[:, :], P[7][0:1, 0:NCH], float(NT - 1), None, ALU.min))

            dve.wait_ge(sem["x_in"], 16)
            dve.wait_ge(sem["cols_in"], 16)
            dve.wait_ge(sem["e_records"], 1)
            layers(dve, c, {
                **idle_stages(c), "spread_b": spread_b, "prep_qk": prep_qk, "prep_biases": prep_biases, "prep_m": prep_m,
                "place": place, "placed": placed,
                "calc_in": lambda g: calc("calc_in", g, AGG, keep=True), "calc_a": lambda g: calc("calc_a", g, X),
                "calc_c": lambda g: calc("calc_c", g, X, bias=BB2[:, :]),
                "keys": keys, "queries": queries, "soften": soften, "kmax": kmax, "context": context, "fold": fold,
                "attend": attend, "down": down, "edges_first": edges_first, "edges": edges})

            dve.wait_ge(sem["fold_in"], FOLD_LOADS)
            step(dve.tensor_scalar(TI, TEMP, 0.1, 5.0, ALU.max, ALU.min))
            step(dve.reciprocal(TI, TI))
            for j in range(4):
                ins = dve.tensor_scalar(LBX[:, j, :], ones[:, 0:T], BXC[:, j:j + 1], None, ALU.mult)
            ins.then_inc(sem["f_lbx"], 1)
            dve.wait_ge(sem["x_summed"], c("x_summed") + 1)
            calc("calc_f", 0, X)
            c.over("norm_f")
            dve.wait_ge(sem["f_fold"], 1)

            def heads(a):
                return a.rearrange("p (h s) -> p h s", h=FH)

            def over(a, parts):
                return a.unsqueeze(2).broadcast_to([parts, FH, FG])
            for m in range(KC):
                dve.tensor_tensor(heads(WXS[:, m, :]), heads(ACC[m][:, :]), over(TI, 128), ALU.mult)
            step(dve.tensor_tensor(heads(LBI), heads(ROW[0][0:T, :]), BSL.unsqueeze(1).broadcast_to([T, FH, FG]), ALU.add))
            dve.tensor_tensor(heads(LBI), heads(LBI), over(TI[0:T, :], T), ALU.mult).then_inc(sem["f_ready"], 1)
            dve.wait_ge(sem["f_ready"], 1)

            def slices(g, more):
                def before(i):
                    z = SZ[i % 2]
                    dve.wait_ge(sem["row_ready"], c("row_ready") + i + 1)
                    wait(dve, sem["s_ready"], c("s_ready") + max(i - 1, 0))
                    dve.tensor_tensor(z, ROW[i % 2][0:T, :], LBI, ALU.add).then_inc(sem["row_done"], 1)
                    dve.wait_ge(sem["row_done"], c("row_done") + i + 1)
                    step(dve.tensor_reduce(SMX, heads(z), axis=AX_X, op=ALU.max))
                    dve.tensor_scalar(SNEG[i % 2], SMX, -1.0, None, ALU.mult).then_inc(sem["sz_ready"], 1)

                def after(i):
                    z = SZ[i % 2]
                    dve.wait_ge(sem["se_ready"], c("se_ready") + i + 1)
                    step(dve.reciprocal(SSD[i % 2], SSD[i % 2]))
                    dve.tensor_tensor(heads(S[:, span(g * G + i, 1), :].rearrange("p a s -> p (a s)")), heads(z),
                                      over(SSD[i % 2], T), ALU.mult).then_inc(sem["s_ready"], 1)

                def next_stats():
                    if more:
                        dve.wait_ge(sem["x_summed"], c("x_summed") + 1)
                        apart(dve, sem["dve_waited"])
                        stats(g + 1, X)

                def next_tile(i):
                    if more:
                        t = span((g + 1) * G + i, 1)
                        dve.wait_ge(sem["tok"], c("tok") + i + 1)
                        dve.tensor_scalar(XH[:, i, :], X[:, t, :].rearrange("p a d -> p (a d)"), RSTD[:, t], NMR[:, t],
                                          ALU.mult, ALU.add).then_inc(sem["xh_ready"], 1)
                before(0)
                before(1)
                after(0)
                before(2)
                after(1)
                next_stats()
                next_tile(0)
                for i in range(3, G):
                    before(i)
                    after(i - 1)
                    next_tile(i - 2)
                after(G - 1)
                next_tile(G - 2)
                next_tile(G - 1)
                c.rest("slices" if more else "slices_last")
            with c.loop(dve, 0, NG - 1, ["slices"]) as g:
                slices(g, True)
            slices(NG - 1, False)
            dve.wait_ge(sem["y_ready"], 1)
            for m in range(KC):
                ins = dve.tensor_copy(YT[:, m, :], ACC[m][:, :])
            ins.then_inc(sem["y_ready"], 1)
            dve.wait_ge(sem["n_ready"], 1)
            step(dve.tensor_copy(NRM[:, :], TP[0:FG, 0:FH]))
            dve.tensor_tensor(heads(TK), heads(BFX), over(NRM[:, :], FG), ALU.mult)
            step(dve.tensor_scalar(DEN[:, :], NRM[:, :], 1e-5, None, ALU.add))
            step(dve.reciprocal(DEN[:, :], DEN[:, :]))
            dve.wait_ge(sem["tk_ready"], 1)
            step(dve.tensor_tensor(TK, ROW[0][0:FG, :], TK, ALU.add))
            dve.tensor_tensor(heads(TK), heads(TK), over(DEN[:, :], FG), ALU.mult).then_inc(sem["tk_done"], 1)
            dve.wait_ge(sem["tkt_ready"], 1)
            dve.tensor_copy(TKT, QP[0:FD, :]).then_inc(sem["tkt_done"], 1)
            dve.wait_ge(sem["qkv_ready"], 1)
            dve.tensor_copy(FQT, WIDE[0][0:FD, :])
            dve.tensor_copy(FKT, WIDE[1][0:FD, :])
            dve.tensor_copy(FV, ROW[1][0:FG, :]).then_inc(sem["qkv_done"], 1)
            dve.wait_ge(sem["aw_ready"], 1)
            step(dve.tensor_reduce(AMX[:, :], heads(ROW[0][0:FG, :]), axis=AX_X, op=ALU.max))
            dve.tensor_tensor(heads(AW), heads(ROW[0][0:FG, :]), over(AMX[:, :], FG), ALU.subtract).then_inc(sem["az_ready"], 1)
            dve.wait_ge(sem["ae_ready"], 1)
            step(dve.tensor_reduce(AMX[:, :], heads(AW), axis=AX_X, op=ALU.add))
            step(dve.reciprocal(AMX[:, :], AMX[:, :]))
            dve.tensor_tensor(heads(AW), heads(AW), over(AMX[:, :], FG), ALU.mult).then_inc(sem["aw_done"], 1)
            dve.wait_ge(sem["awt_ready"], 1)
            dve.tensor_copy(AWT, QP[0:FG, :]).then_inc(sem["awt_done"], 1)
            step(dve.memset(OP, 0.0))
            dve.wait_ge(sem["o_ready"], 1)
            for a in range(2):
                ins = dve.tensor_copy(OP[:, a::2, a * FG:(a + 1) * FG], heads(ROW[1][0:FD, :])[:, a::2, :])
            ins.then_inc(sem["o_done"], 1)
            dve.wait_ge(sem["m2_ready"], 1)
            for a in range(2):
                ins = dve.tensor_copy(M2[:, 2 * a:2 * a + 2, :], ACC[a][:, :].rearrange("p (j d) -> p j d", j=2))
            ins.then_inc(sem["m2_done"], 1)
            with c.loop(dve, 0, NG, ["finish"]) as g:
                step(dve.tensor_tensor(tiles_of(X, g), tiles_of(X, g), BOUT.unsqueeze(1).broadcast_to([T, G, D]), ALU.add))
                add_rows(g, 0, G)
                c.rest("finish")


def kernel(**inputs):
    import numpy as np
    import concourse.bacc as bacc
    from concourse import mybir as mb
    from concourse.bass_utils import run_bass_kernel_spmd

    a = {k.removeprefix("L0_"): np.asarray(v) for k, v in inputs.items()}

    def edges(v, fill):
        return np.concatenate([v, np.full(128 * EC - E, fill, v.dtype)]).reshape(128, EC)

    def blocks(w):
        w = w.reshape(*w.shape[:-2], w.shape[-2] // 128, 128, w.shape[-1])
        return np.ascontiguousarray(np.swapaxes(w, -3, -2))

    def columns(v):
        return v.reshape(LAYERS, -1, 128).transpose(2, 0, 1)

    arrays = {
        "x": a["x"], "src": edges(a["src"], N), "dst": edges(a["dst"], 0), "ew": edges(a["edge_weight"], 0),
        "w_gnn": blocks(a["gnn_W"]),
        "w_qk": blocks(np.concatenate([a["mix_Wq"], a["mix_Wk"]], -1)),
        "w_vo": blocks(np.concatenate([a["mix_Wv"], a["mix_Wo"]], -1)),
        "w_1": blocks(a["mix_W1"]), "w_2": blocks(a["mix_W2"]),
        "cols": np.concatenate([columns(a[f"mix_{n}"]) for n in ("ln1_g", "ln1_b", "ln2_g", "ln2_b", "b1")], -1).reshape(128, -1),
        "b_o": a["mix_bo"], "b_2": a["mix_b2"],
        "w_fx": blocks(a["ffn_W_fx"]), "w_xt": blocks(np.ascontiguousarray(a["ffn_W_x"].T)),
        "w_slice": a["ffn_W_slice"], "b_slice": a["ffn_b_slice"][None], "b_fx": a["ffn_b_fx"][None],
        "b_x": a["ffn_b_x"].reshape(4, 128).T, "w_q": a["ffn_W_q"], "w_k": a["ffn_W_k"], "w_v": a["ffn_W_v"],
        "w_out": a["ffn_W_out"].reshape(FH, FD, D).transpose(1, 0, 2), "b_out": a["ffn_b_out"][None],
        "temp": a["ffn_temperature"].reshape(1, FH),
    }
    arrays = {f"in_{k}": np.ascontiguousarray(v) for k, v in arrays.items()}
    nc = bacc.Bacc("TRN2", target_bir_lowering=False, num_devices=1)
    args = [nc.dram_tensor(k, v.shape, mb.dt.from_np(v.dtype), kind="ExternalInput").ap() for k, v in arrays.items()]
    out = nc.dram_tensor("out_0", (N, D), mb.dt.float32, kind="ExternalOutput").ap()
    gps_layer(nc, *args, out)
    r = run_bass_kernel_spmd(nc, [arrays], core_ids=[0])
    return r.results[0]["out_0"]
```

```python
from contextlib import ExitStack, contextmanager

import concourse.bass as bass
from concourse import mybir

F32 = mybir.dt.float32
I32 = mybir.dt.int32
F16 = mybir.dt.float16
ALU = mybir.AluOpType
ACT = mybir.ActivationFunctionType
AX_X = mybir.AxisListType.X

N = 3125
D = 256
T = 125
NT = N // T
G = 5
NG = NT // G
GW = G * T
KC = D // 128
LAYERS = 4
HEADS, DH = 8, 32
FF = 4 * D
FB = FF // 128
EPS = 1e-5
QSCALE = DH ** -0.25
E = 50000
HU = 4
UNIT = 2 * HU
EC = -(-E // (128 * UNIT)) * UNIT
NCH = -(-(E + NT * 127) // (128 * UNIT)) * UNIT
RC = NCH + HU
SET = UNIT // 2
FH, FD, FG = 8, 64, 64
INNER = FH * FD
HALF = [(0, 3), (3, 2)]
NB = NT + 1 + (NT + 1) % 2


def pairs(tiles):
    return [(i, min(2, tiles - i)) for i in range(0, tiles, 2)]


NP = len(pairs(G))
MAGIC = float(0x5F3759DF)
UP = {"0a": (0, 0, FB // 2), "0b": (0, FB // 2, FB), "1": (1, 0, FB)}

COUNTS = {
    "calc_in": {"xh_ready": G, "dve_step": 15},
    "calc_a": {"xh_ready": G, "dve_step": 15},
    "calc_c": {"xh_ready": G, "dve_step": 16},
    "calc_f": {"x_summed": 1, "xh_ready": G, "dve_step": 15},
    "norm_in": {"xt_ready": NP, "xt_done": NP},
    "norm_a": {"xt_ready": NP, "xt_done": NP},
    "norm_c": {"xt_ready": NP, "xt_done": NP},
    "norm_f": {"xt_ready": G, "xt_done": G},
    "support": {"row_ready": NP, "row_done": NP, "sup_stored": 16},
    "keys": {"wide_ready": 2 * KC, "wide_done": 2 * KC, "dve_step": 1},
    "queries": {"row_ready": NP, "row_done": NP, "qz_ready": 1, "dve_step": 1},
    "soften": {"qe_ready": 1, "qn_ready": 1, "dve_step": 2},
    "turn_q": {"qt_ready": NP, "qt_done": NP},
    "kmax": {"kmax_ready": 1, "dve_step": 1},
    "context": {"kexp": KC, "bxh_ready": G, "kt_ready": G, "kt_done": G, "g_acc": G},
    "fold": {"g_closed": 1, "gs_ready": 1, "cm_ready": 1, "cm_done": 1, "m_ready": 1, "ms_done": 1, "dve_step": 2},
    "fetch_q": {"qs_ready": 1},
    "attend": {"row_ready": NP, "row_done": NP},
    "up0a": {"wide_ready": FB // 2, "wide_done": FB // 2},
    "up0b": {"wide_ready": FB // 2, "wide_done": FB // 2},
    "up1": {"wide_ready": FB, "wide_done": FB},
    "down0": {"row_ready": len(pairs(HALF[0][1])), "row_done": len(pairs(HALF[0][1]))},
    "down1": {"row_ready": len(pairs(HALF[1][1])), "row_done": len(pairs(HALF[1][1]))},
    "spread_b": {"lb_ready": 1},
    "prep_qk": {"w_qk": 16, "bqk_ready": 1, "qk_ready": 1},
    "load_rest": {"w_rest": 80},
    "prep_biases": {"bv_ready": 1, "bvm_ready": 1, "dve_step": 1},
    "prep_m": {"b2m_ready": 1, "rest_ready": 1},
    "edges_first": {"hot_ready": HU},
    "edges0": {"hot_ready": HU, "agg_ready": HU, "agg_done": HU, "msgs0": 16 * HU},
    "edges1": {"hot_ready": HU, "agg_ready": HU, "agg_done": HU, "msgs1": 16 * HU},
    "slices": {"x_summed": 1, "xh_ready": G, "xt_ready": G, "xt_done": G, "row_ready": G, "row_done": G,
               "sz_ready": G, "se_ready": G, "s_ready": G, "tok": G, "s_summed": G, "dve_step": 15 + 2 * G},
    "slices_last": {"row_ready": G, "row_done": G, "sz_ready": G, "se_ready": G, "s_ready": G, "tok": G, "s_summed": G,
                    "dve_step": 2 * G},
    "finish": {"sc_ready": G, "st_ready": G, "st_done": G, "row_ready": G, "row_done": G, "out_done": 16,
               "dve_step": 1},
}


class Count:

    def __init__(self, start=0):
        self.base, self.own = {}, {sem: start for stage in COUNTS.values() for sem in stage}

    def __call__(self, sem):
        b, o = self.base.get(sem, 0), self.own.get(sem, 0)
        return o if isinstance(b, int) and b == 0 else b + o

    def over(self, *stages):
        for stage in stages:
            for sem, n in COUNTS[stage].items():
                self.own[sem] = self.own.get(sem, 0) + n

    def rest(self, stage):
        for sem, n in COUNTS[stage].items():
            if sem != "dve_step":
                self.own[sem] = self.own.get(sem, 0) + n

    @contextmanager
    def loop(self, eng, lo, hi, stages):
        per = Count()
        per.over(*stages)
        per.own = {sem: n for sem, n in per.own.items() if n}
        base, own = dict(self.base), dict(self.own)
        with eng.Fori(lo, hi) as r:
            turn = r if lo == 0 else r - lo
            for sem, n in per.own.items():
                self.base[sem] = turn * n + self(sem)
                self.own[sem] = 0
            yield r
        for sem in per.own:
            assert self.own[sem] == per.own[sem], (sem, self.own[sem], per.own[sem])
        self.base, self.own = base, own
        for sem, n in per.own.items():
            self.own[sem] = own.get(sem, 0) + n * (hi - lo)


def wait(eng, sem, value):
    if not isinstance(value, int) or value > 1:
        eng.wait_ge(sem, value)


def apart(eng, sem):
    eng.sem_inc(sem, 1)


A_STAGES = ["calc_a", "norm_a", "keys", "queries", "soften", "turn_q"]
FRONT = ["fetch_q", "attend", "calc_c", "norm_c"]
FFN_STAGES = ["up0a", "up0b", "up1", "down0", "down1"]
B_STAGES = ["context"] * NG + ["soften", "prep_biases", "turn_q", "prep_m", "fold"]
TAIL = ["load_rest", "calc_a", "norm_a", "keys", "kmax", "queries"]
LAYER_STAGES = B_STAGES + ["spread_b", "prep_qk"] + (FRONT + FFN_STAGES) * NG + A_STAGES * (NG - 1) + TAIL
LAST_STAGES = B_STAGES + (FRONT + FFN_STAGES) * NG
TURN_E, HEAD_E, TAIL_E = 6, 2, 4
EDGE_TURN = ["edges0", "edges1"] * (TURN_E // 2)
EDGE_LAYER = ["edges_first"] + ["edges0", "edges1"] * ((HEAD_E + NG * TURN_E + TAIL_E) // 2)
assert ((LAYERS - 1) * (HEAD_E + NG * TURN_E) + (LAYERS - 2) * TAIL_E) * HU == NCH


def idle_stages(c):
    idle = {name: lambda *a, name=name: c.over(name) for name in COUNTS}
    return {**idle, "up": lambda g, part: c.over(f"up{part}"), "down": lambda g, h: c.over(f"down{h}"),
            "edges": lambda p: c.over(f"edges{p}"), "qk_set": lambda: None, "sorted": lambda: None, "open": lambda: None}


def layers(eng, c, stage):
    half = [0]

    def add_edges():
        stage["edges"](half[0])
        half[0] = 1 - half[0]

    def turn(g, front, back, with_edges):
        def edges():
            if with_edges:
                add_edges()
        if back:
            stage["calc_a"](g - 1)
        stage["up"](g, "0a")
        edges()
        stage["up"](g, "0b")
        edges()
        if back:
            stage["norm_a"](g - 1)
            stage["keys"](g - 1)
            stage["queries"](g - 1)
        edges()
        stage["up"](g, "1")
        if back:
            stage["soften"]()
        if front:
            stage["fetch_q"](g + 1)
        edges()
        stage["down"](g, 0)
        edges()
        if front:
            stage["attend"](g + 1)
            stage["calc_c"](g + 1)
        stage["down"](g, 1)
        edges()
        if back:
            stage["turn_q"](g - 1)
        if front:
            stage["norm_c"](g + 1)

    def layer(l, more, with_edges):
        def edges():
            if with_edges:
                add_edges()
        with c.loop(eng, 0, NG - 1, ["context"]) as g:
            stage["context"](g)
        stage["soften"]()
        stage["prep_biases"](l)
        stage["turn_q"](NG - 1)
        stage["context"](NG - 1)
        stage["prep_m"]()
        if more:
            stage["spread_b"](l + 1)
        stage["fold"]()
        stage["fetch_q"](0)
        if more:
            stage["prep_qk"](l + 1)
        if with_edges:
            stage["edges_first"]()
        edges()
        if more:
            stage["qk_set"]()
        if not with_edges:
            stage["sorted"]()
        stage["attend"](0)
        stage["calc_c"](0)
        edges()
        stage["norm_c"](0)
        turn(0, True, False, with_edges)
        with c.loop(eng, 1, NG - 1, FFN_STAGES + FRONT + A_STAGES * more + EDGE_TURN * with_edges) as g:
            turn(g, True, more, with_edges)
        turn(NG - 1, False, more, with_edges)
        if more:
            stage["load_rest"](l + 1)
            stage["calc_a"](NG - 1)
            edges()
            stage["norm_a"](NG - 1)
            edges()
            stage["keys"](NG - 1)
            stage["kmax"]()
            edges()
            stage["queries"](NG - 1)
            edges()
            stage["open"]()

    stage["load_rest"](0)
    stage["spread_b"](0)
    stage["prep_qk"](0)
    stage["qk_set"]()
    stage["calc_in"](0)
    with c.loop(eng, 0, NG - 1, ["norm_in", "calc_in", "support"]) as g:
        stage["norm_in"](g)
        stage["calc_in"](g + 1)
        stage["support"](g)
    stage["norm_in"](NG - 1)
    stage["calc_a"](0)
    stage["support"](NG - 1)
    stage["norm_a"](0)
    stage["calc_a"](1)
    stage["keys"](0)
    stage["queries"](0)
    with c.loop(eng, 0, NG - 2, A_STAGES) as g:
        stage["soften"]()
        stage["norm_a"](g + 1)
        stage["calc_a"](g + 2)
        stage["keys"](g + 1)
        stage["turn_q"](g)
        stage["queries"](g + 1)
    stage["soften"]()
    stage["norm_a"](NG - 1)
    stage["keys"](NG - 1)
    stage["kmax"]()
    stage["turn_q"](NG - 2)
    stage["queries"](NG - 1)
    stage["open"]()
    layer(0, True, False)
    with c.loop(eng, 1, LAYERS - 1, LAYER_STAGES + EDGE_LAYER) as l:
        layer(l, True, True)
    layer(LAYERS - 1, False, True)


def gps_layer(nc, x, src, dst, ew, w_gnn, w_qk, w_vo, w_1, w_2, cols, b_o, b_2, w_fx, w_xt, w_slice,
              b_slice, b_fx, b_x, w_q, w_k, w_v, w_out, b_out, temp, out):
    x_t = x.rearrange("(t p) c -> p t c", p=T)
    out_t = out.rearrange("(t p) c -> p t c", p=T)
    sup_d = nc.dram_tensor("support_rows", (N, D), F32).ap()
    rec_d = nc.dram_tensor("edge_records", (128 * RC, 4), F32).ap()
    sup_t = sup_d.rearrange("(t p) c -> p t c", p=T)

    with ExitStack() as ctx:
        def sb(name, shape, dt=F32):
            return ctx.enter_context(nc.sbuf_tensor(name, shape, dt))

        X = sb("X", [T, NT, D])
        AGG = sb("AGG", [T, NT, D])
        big = sb("big", [128, NT * INNER])
        KX = big[:, 0:KC * N].rearrange("p (k n) -> p k n", k=KC)
        QT = big[:, KC * N:2 * KC * N].rearrange("p (k n) -> p k n", k=KC)
        S = big[0:T, :].rearrange("p (t s) -> p t s", t=NT)
        W1 = sb("W1", [128, KC, FF])
        W2 = sb("W2", [128, FB, D])
        UT = [sb(f"UT{h}", [128, FB, n * T]) for h, (_, n) in enumerate(HALF)]
        WQK = sb("WQK", [128, KC, 2 * D])
        WVO = sb("WVO", [128, KC, 2 * D])
        WG = sb("WG", [128, KC, D])
        COLS = sb("COLS", [128, LAYERS * 16])
        XH = sb("XH", [T, G, D])
        XT = sb("XT", [128, KC, GW])
        QS = sb("QS", [128, KC, GW])
        KE = QS
        QZ = sb("QZ", [T, G, D])
        KT = sb("KT", [T, 2, D])
        GS = sb("GS", [128, KC, D])
        CM = sb("CM", [128, D])
        MS = sb("MS", [128, KC, D])
        B2M = sb("B2M", [128, KC, D])
        BVM = sb("BVM", [128, D])
        LB = sb("LB", [128, KC, T])
        BQ = sb("BQ", [T, D])
        BK = sb("BK", [128, KC])
        BV = sb("BV", [128, KC])
        B1 = sb("B1", [128, FB])
        BB2 = sb("BB2", [T, D])
        BO = sb("BO", [1, D])
        MASK = sb("MASK", [128, D])
        ident = sb("ident", [128, 128])
        ones = sb("ones", [128, 128])
        eighth = sb("eighth", [1, 128])
        ST = sb("ST", [T, G, 6])
        MV = sb("MV", [T, G, 2])
        NW = sb("NW", [T, 3, G])
        RSTD = sb("RSTD", [T, NT])
        NMR = sb("NMR", [T, NT])
        QM = sb("QM", [T, G * HEADS])
        MX = sb("MX", [128, KC, NG])
        KB = sb("KB", [128, KC])
        KS = sb("KS", [128, KC, NG])
        RS = sb("RS", [128, 2, KC])
        REC = sb("REC", [128, RC * 4])
        REC3 = REC[:, :].rearrange("p (c r) -> p c r", r=4)
        MSG = sb("MSG", [128, UNIT, D])
        IDS = sb("IDS", [128, UNIT], I32)
        HOT = sb("HOT", [128, HU, T])
        SLOT = sb("SLOT", [128, 2, SET, 4])
        IOTA = sb("IOTA", [128, 512])
        BLK = sb("BLK", [1, NCH], I32)

        TRI = CM[:, 0:128]
        ENDC = sb("ENDC", [32, 4])
        BT = sb("BT", [128, NB])
        zeros = sb("zeros", [1, INNER])

        u0 = UT[0][:, :, :].rearrange("p a b -> p (a b)")
        u1 = UT[1][:, :, :].rearrange("p a b -> p (a b)")
        SRC, DST, EW = u0[:, 0:EC].bitcast(I32), u0[:, 400:400 + EC].bitcast(I32), u0[:, 800:800 + EC]
        SRCF, LOC, BKT = u0[:, 1200:1200 + EC], u0[:, 1600:1600 + EC], u0[:, 2000:2000 + EC]
        CNT, OFF, TOT = u0[:, 2400:2432], u0[:, 2440:2472], u0[:, 2480:2512]
        END, BASE = u0[:, 2520:2552], u0[:, 2560:2592]
        TOTI = u0[:, 2600:2632].bitcast(I32)
        HIT, SCAN, HIT2, SCAN2, RANK = [u1[:, 200 * i:200 * i + 200].bitcast(F16)[:, 0:EC] for i in range(5)]
        PLACE, BEGIN, EQ, AHEAD = u1[:, 1000:1000 + EC], u1[:, 1400:1400 + EC], u1[:, 1800:1802], u1[:, 1802:1804]
        CHUNK = u1[:, 0:EC]
        BKT16 = u0[:, 2640:2640 + EC // 2].bitcast(F16)
        PAST = KX[0:32, 0, 0:NCH]
        REC0 = REC[:, 0:EC * 4].rearrange("p (c r) -> p c r", r=4)
        POSI = REC0[:, :, 3].bitcast(I32)

        WXT = QS[:, :, :].rearrange("p k n -> p (k n)")[:, 0:4 * D].rearrange("p (j c) -> p j c", j=4)
        WXS = W1[:, :, 0:INNER]
        WFX = W1[:, :, INNER:2 * INNER]
        M2 = W2[:, 0:4, :]
        BOUT = W2[0:T, 4, :]
        wq_ = WQK[:, :, :].rearrange("p k n -> p (k n)")
        LBX = wq_[:, 0:4 * T].rearrange("p (j t) -> p j t", j=4)
        BD, TEMP, TI, BXC = wq_[:, 512:640], wq_[:, 640:648], wq_[:, 648:656], wq_[:, 656:660]
        BSL = wq_[0:T, 664:664 + FG]
        LBI = u1[0:T, 0:INNER]
        SZ = [u1[0:T, 600:600 + INNER], u1[0:T, 1200:1200 + INNER]]
        SMX = QM[:, 0:FH]
        SNEG = [QM[:, (1 + i) * FH:(2 + i) * FH] for i in range(2)]
        SSD = [QM[:, (3 + i) * FH:(4 + i) * FH] for i in range(2)]
        SSUM = GS[0:T, :, :].rearrange("p k n -> p (k n)")
        SC = [QZ[:, 0:2, :].rearrange("p a b -> p (a b)"), QZ[:, 2:4, :].rearrange("p a b -> p (a b)")]
        STT = [u0[:, 0:4 * T].rearrange("p (j t) -> p j t", j=4), u0[:, 512:512 + 4 * T].rearrange("p (j t) -> p j t", j=4)]
        YT = WVO[:, :, :]
        qk_ = WQK[0:FG, :, :].rearrange("p k n -> p (k n)")
        TK, TKT = qk_[:, 0:INNER], qk_[:, INNER:2 * INNER]
        gx = XT[0:FG, :, :].rearrange("p k n -> p (k n)")
        BFX, FQT = u0[0:FG, 2104:2104 + INNER], gx[:, INNER:2 * INNER]
        qx = QS[0:FG, :, :].rearrange("p k n -> p (k n)")
        FKT, FV = qx[:, 0:INNER], qx[:, INNER:2 * INNER]
        gs_ = GS[0:FG, :, :].rearrange("p k n -> p (k n)")
        AW = gs_[:, 0:INNER]
        ms_ = MS[0:FG, :, :].rearrange("p k n -> p (k n)")
        AWT = ms_[:, 0:INNER]
        OP = u0[0:FG, 1040:1040 + FH * 128].rearrange("p (h a) -> p h a", h=FH)
        WOUT = MSG[0:FG, :, :]
        WQKV = B2M[0:FG, :, :].rearrange("p k n -> p (k n)")[:, 0:3 * FD]
        DEN, AMX = sb("DEN", [FG, FH]), sb("AMX", [FG, FH])
        NRM = sb("NRM", [FG, FH])

        P = [ctx.enter_context(nc.psum_tensor(f"P{i}", [128, 512], F32)) for i in range(8)]
        WIDE, ROW, TURN, ACC = [P[0], P[1]], [P[2], P[3]], [P[4], P[5]], [P[6], P[7]]
        TP, QP = TURN

        FIRST = {"support": 0, "queries": 0, "down0": 1, "attend": 1, "down1": 0}

        def pair_bank(stage, n):
            return ROW[(FIRST[stage] + n) % 2]

        def two_rows(bank, tiles):
            return bank[0:T, 0:tiles * D].rearrange("p (t d) -> p t d", t=tiles)

        def turned(bank, tiles=1):
            return bank[:, 0:KC * tiles * T].rearrange("p (k t) -> p k t", k=KC)

        names = sorted({n for cs in COUNTS.values() for n in cs} | {
            "consts", "x_in", "w_g", "cols_in", "edges_in", "dve_step", "pool_step", "e_counted",
            "e_offset", "e_placed", "e_ends", "e_past", "e_passed", "e_blocks", "e_zero", "e_zeroed", "e_back",
            "fold_in", "f_in", "f_bd", "f_lbx", "f_fold", "f_ready", "y_ready", "n_ready", "tk_ready", "tk_done",
            "tkt_ready", "tkt_done", "qkv_ready", "qkv_done", "aw_ready", "az_ready", "ae_ready", "aw_done",
            "awt_ready", "awt_done", "o_ready", "o_done", "m2_ready", "m2_done", "ssum_zero", "slots", "ids_ready",
            "e_bucketed", "e_short", "e_rank", "e_place", "dve_waited", "pool_waited"})
        sem = {n: ctx.enter_context(nc.semaphore(n)) for n in names}
        sent = [ctx.enter_context(nc.semaphore(f"sent{i}")) for i in range(2)]
        block = ctx.enter_context(nc.Block())

        def agg_bank(i):
            return ACC[i // 2][0:T, (i % 2) * D:(i % 2 + 1) * D]

        def span(at, n):
            return slice(at, at + n) if isinstance(at, int) else bass.ds(at, n)

        FOLD_LOADS, F_LOADS = 6 * 16, 7 * 16
        SINGLE = [(i, 1) for i in range(G)]
        SLICES = ["calc_f", "norm_f"] + ["slices"] * (NG - 1) + ["slices_last"]
        MIXER = (["load_rest", "spread_b", "prep_qk"] + ["calc_in", "norm_in", "support"] * NG + A_STAGES * (NG - 1) + TAIL[1:] +
                 LAYER_STAGES * (LAYERS - 1) + LAST_STAGES)

        @block.sync
        def _(sp):
            for n in sorted({n for stage in COUNTS.values() for n in stage} - {"msgs0", "msgs1"}):
                sp.sem_inc(sem[n], 1)
            sp.sem_inc(sem["e_rank"], 1)
            sp.sem_inc(sem["e_place"], 1)
            c = Count(1)
            sp.dma_start(SRC, src).then_inc(sem["edges_in"], 16)
            sp.dma_start(DST, dst).then_inc(sem["edges_in"], 16)
            sp.dma_start(EW, ew).then_inc(sem["edges_in"], 16)
            sp.dma_start(AGG[:, :, :], x_t).then_inc(sem["x_in"], 16)
            sp.dma_start(WG[:, :, :], w_gnn).then_inc(sem["w_g"], 16)
            sp.dma_start(COLS[:, :], cols).then_inc(sem["cols_in"], 16)
            sp.wait_ge(sem["e_zero"], 1)
            sp.dma_start(rec_d.rearrange("(p c) r -> p (c r)", p=128), REC[:, :]).then_inc(sem["e_zeroed"], 16)

            def prep_qk(l):
                wait(sp, sem["row_done"], c("row_done"))
                sp.dma_start(WQK[:, :, :], w_qk[span(l, 1)].rearrange("l p k n -> p (l k) n")).then_inc(sem["w_qk"], 16)
                c.over("prep_qk")

            def load_rest(l):
                wait(sp, sem["row_done"], c("row_done"))
                for buf, w in ((WVO, w_vo), (W1, w_1), (W2, w_2)):
                    sp.dma_start(buf[:, :, :], w[span(l, 1)].rearrange("l p k n -> p (l k) n")).then_inc(sem["w_rest"], 16)
                sp.dma_start(BO[:, :], b_o[span(l, 1), :]).then_inc(sem["w_rest"], 16)
                sp.dma_start(BB2[:, :], b_2[span(l, 1), :].broadcast_to([T, D])).then_inc(sem["w_rest"], 16)
                c.over("load_rest")

            def support(g):
                sp.wait_ge(sem["row_done"], c("row_done") + NP)
                sp.dma_start(sup_t[:, span(g * G, G), :], QZ[:, :, :]).then_inc(sem["sup_stored"], 16)
                c.over("support")

            layers(sp, c, {**idle_stages(c), "prep_qk": prep_qk, "load_rest": load_rest, "support": support})

            rows_after = COUNTS["down0"]["row_ready"] + 2 * COUNTS["down1"]["row_ready"]
            sp.wait_ge(sem["row_ready"], c("row_ready") - rows_after)
            for a, b in ((WXT, w_xt), (TEMP, temp.broadcast_to([128, FH])), (BXC, b_x), (BSL, b_slice.broadcast_to([T, FG]))):
                sp.dma_start(a, b).then_inc(sem["fold_in"], 16)
            sp.wait_ge(sem["f_bd"], 1)
            for i in range(2):
                sp.dma_start(BD[FD * i:FD * (i + 1), FG * i:FG * (i + 1)], w_slice).then_inc(sem["fold_in"], 16)
            sp.wait_ge(sem["row_done"], c("row_done"))
            sp.wait_ge(sem["agg_done"], NCH + 1)
            for a, b in ((WFX, w_fx), (BOUT, b_out.broadcast_to([T, D])), (WOUT, w_out), (BFX, b_fx.broadcast_to([FG, INNER])),
                         (WQKV[:, 0:FD], w_q), (WQKV[:, FD:2 * FD], w_k), (WQKV[:, 2 * FD:3 * FD], w_v)):
                sp.dma_start(a, b).then_inc(sem["f_in"], 16)
            c.over(*SLICES)
            with c.loop(sp, 0, NG, ["finish"]) as g:
                sp.wait_ge(sem["row_done"], c("row_done") + G)
                sp.dma_start(out_t[:, span(g * G, G), :], X[:, span(g * G, G), :]).then_inc(sem["out_done"], 16)
                c.over("finish")
            sp.wait_ge(sem["out_done"], 16 * NG + 1)

        @block.gpsimd
        def _(pool):
            done = [0]

            def step(ins):
                done[0] += 1
                ins.then_inc(sem["pool_step"], 1)
                pool.wait_ge(sem["pool_step"], done[0])

            pool.memset(REC[:, :], 0.0).then_inc(sem["e_zero"], 1)
            step(pool.memset(ones[:, :], 1.0))
            step(pool.memset(MASK[:, :], 1.0))
            step(pool.memset(eighth[:, :], 1.0 / HEADS))
            step(pool.iota(IOTA[:, :], pattern=[[1, 512]], base=0, channel_multiplier=0,
                           allow_small_or_imprecise_dtypes=True))
            step(pool.affine_select(out=ident[:, :], in_=ones[:, :], compare_op=ALU.is_equal, fill=0.0,
                                    base=0, pattern=[[-1, 128]], channel_multiplier=1))
            step(pool.affine_select(out=TRI[:, :], in_=ones[:, :], compare_op=ALU.is_gt, fill=0.0,
                                    base=0, pattern=[[1, 128]], channel_multiplier=-1))
            for k in range(KC):
                mk = MASK[:, k * 128:(k + 1) * 128].rearrange("p (h d) -> p h d", d=DH)
                step(pool.affine_select(out=mk, in_=mk, compare_op=ALU.is_ge, fill=0.0, base=0,
                                        pattern=[[-DH, 128 // DH], [0, DH]], channel_multiplier=1))
                step(pool.affine_select(out=mk, in_=mk, compare_op=ALU.is_ge, fill=0.0, base=DH - 1,
                                        pattern=[[DH, 128 // DH], [0, DH]], channel_multiplier=-1))
            pool.memset(zeros[:, :], 0.0).then_inc(sem["consts"], 1)
            pool.wait_ge(sem["edges_in"], 48)
            step(pool.tensor_copy(SRCF, SRC))
            step(pool.tensor_scalar(LOC.bitcast(I32), SRCF, 1.0 / T, -(T - 1) / (2.0 * T), ALU.mult, ALU.add))
            step(pool.tensor_copy(BKT, LOC.bitcast(I32)))
            pool.iota(BT[:, :], pattern=[[1, NB]], base=0, channel_multiplier=0,
                      allow_small_or_imprecise_dtypes=True).then_inc(sem["e_bucketed"], 1)
            step(pool.tensor_scalar(BEGIN, BKT, float(T), None, ALU.mult))
            step(pool.tensor_tensor(LOC, SRCF, BEGIN, ALU.subtract))
            pool.wait_ge(sem["e_zeroed"], 16)
            step(pool.tensor_copy(REC0[:, :, 0].bitcast(I32), DST))
            step(pool.tensor_copy(REC0[:, :, 1], LOC))
            step(pool.tensor_copy(REC0[:, :, 2], EW))

            pool.wait_ge(sem["e_ends"], 1)
            step(pool.tensor_copy(PLACE, RANK))
            with pool.Fori(0, NB // 2) as r:
                n = r * 6
                pool.tensor_copy(EQ, BT[:, span(r * 2, 2)]).then_inc(sem["e_place"], 1)
                pool.tensor_copy(AHEAD, OFF[:, span(r * 2, 2)]).then_inc(sem["e_place"], 1)
                pool.wait_ge(sem["e_place"], n + 3)
                apart(pool, sem["pool_waited"])
                for i, begin in enumerate((BEGIN, SRCF)):
                    pool.tensor_scalar(begin, BKT, EQ[:, i:i + 1], AHEAD[:, i:i + 1], ALU.is_equal,
                                       ALU.mult).then_inc(sem["e_place"], 1)
                for i, begin in enumerate((BEGIN, SRCF)):
                    pool.wait_ge(sem["e_place"], n + 4 + 2 * i)
                    pool.tensor_tensor(PLACE, PLACE, begin, ALU.add).then_inc(sem["e_place"], 1)
                pool.wait_ge(sem["e_place"], n + 7)
                apart(pool, sem["pool_waited"])
            step(pool.tensor_scalar(POSI, PLACE, 1.0 / 128, -127.0 / 256, ALU.mult, ALU.add))
            step(pool.tensor_copy(CHUNK, POSI))
            step(pool.tensor_scalar(BEGIN, CHUNK, -128.0, None, ALU.mult))
            step(pool.tensor_tensor(BEGIN, BEGIN, PLACE, ALU.add))
            step(pool.tensor_scalar(BEGIN, BEGIN, float(RC), None, ALU.mult))
            step(pool.tensor_tensor(BEGIN, BEGIN, CHUNK, ALU.add))
            step(pool.tensor_copy(POSI, BEGIN))
            pool.sem_inc(sem["e_placed"], 1)

            def scatter(r):
                for i in range(2):
                    if not isinstance(r, int):
                        pool.wait_ge(sent[i], r * (16 * SET))
                    pool.tensor_copy(SLOT[:, i, :, :], REC0[:, span(r * UNIT + i * SET, SET), :]).then_inc(sem["slots"], 1)
                    pool.wait_ge(sem["slots"], r * 2 + i + 1)
                    apart(pool, sem["pool_waited"])
                    for j in range(SET):
                        pool.indirect_dma_start(rec_d, bass.IndirectOffsetOnAxis(ap=SLOT[:, i, j, 3:4].bitcast(I32), axis=0),
                                                SLOT[:, i, j, :], None).then_inc(sent[i], 16)
            scatter(0)
            with pool.Fori(1, EC // UNIT) as r:
                scatter(r)

            for i in range(2):
                pool.wait_ge(sent[i], 16 * EC // 2)
            pool.dma_start(REC[:, :], rec_d.rearrange("(p c) r -> p (c r)", p=128)).then_inc(sem["e_back"], 16)

            pool.wait_ge(sem["e_back"], 16)
            pool.wait_ge(sem["sup_stored"], 16 * NG + 1)

            def gather(r):
                for h in range(2):
                    if not isinstance(r, int):
                        pool.wait_ge(sem["agg_ready"], r * UNIT + (1 + (h + 1) * HU - UNIT))
                    half = slice(h * HU, (h + 1) * HU)
                    pool.tensor_copy(IDS[:, half], REC3[:, span(r * UNIT + h * HU, HU), 0].bitcast(I32)).then_inc(sem["ids_ready"], 1)
                    pool.wait_ge(sem["ids_ready"], r * 2 + h + 1)
                    apart(pool, sem["pool_waited"])
                    for i in range(h * HU, (h + 1) * HU):
                        pool.indirect_dma_start(MSG[:, i, :], None, sup_d,
                                                bass.IndirectOffsetOnAxis(ap=IDS[:, i:i + 1], axis=0)).then_inc(sem[f"msgs{h}"], 16)
            gather(0)
            with pool.Fori(1, NCH // UNIT) as r:
                gather(r)

            c = Count(1)
            c.over(*MIXER)
            pool.memset(BD, 0.0).then_inc(sem["f_bd"], 1)

            def x_sum(g):
                x_ = X[:, span(g * G, G), :]
                pool.tensor_tensor(x_, x_, AGG[:, span(g * G, G), :], ALU.add).then_inc(sem["x_summed"], 1)
            pool.wait_ge(sem["row_done"], c("row_done"))
            pool.wait_ge(sem["agg_done"], NCH + 1)
            x_sum(0)
            pool.memset(SSUM, 0.0).then_inc(sem["ssum_zero"], 1)
            pool.wait_ge(sem["ssum_zero"], 1)
            c.over("calc_f", "norm_f")

            def slices(g, more):
                if more:
                    x_sum(g + 1)
                for i in range(G):
                    pool.wait_ge(sem["s_ready"], c("s_ready") + i + 1)
                    pool.wait_ge(sem["s_summed"], c("s_summed") + i)
                    pool.tensor_tensor(SSUM, SSUM, S[:, span(g * G + i, 1), :].rearrange("p a s -> p (a s)"),
                                       ALU.add).then_inc(sem["s_summed"], 1)
                c.over("slices" if more else "slices_last")
            with c.loop(pool, 0, NG - 1, ["slices"]) as g:
                slices(g, True)
            slices(NG - 1, False)
            with c.loop(pool, 0, NG, ["finish"]) as g:
                for i in range(G):
                    pool.wait_ge(sem["st_ready"], c("st_ready") + max(i - 1, 0))
                    pool.tensor_copy(SC[i % 2], S[:, span(g * G + i, 1), :].rearrange("p a s -> p (a s)")).then_inc(sem["sc_ready"], 1)
                c.over("finish")

        @block.tensor
        def _(pe):
            c = Count(1)

            def row_free(i):
                if i == 0:
                    wait(pe, sem["row_done"], c("row_done"))
                elif i >= 2:
                    pe.wait_ge(sem["row_done"], c("row_done") + i - 1)

            def wide_free(i):
                wait(pe, sem["wide_done"], c("wide_done") + i - 1)

            def turns_free():
                for name in ("xt_done", "qt_done", "kt_done"):
                    wait(pe, sem[name], c(name))

            def turn_tiles(chunks, src, ready, done):
                turns_free()
                for n, (first, tiles) in enumerate(chunks):
                    if src is XH:
                        pe.wait_ge(sem["xh_ready"], c("xh_ready") - G + first + tiles)
                    if n >= 2:
                        pe.wait_ge(sem[done], c(done) + n - 1)
                    bank = turned(TURN[n % 2], tiles)
                    for i in range(tiles):
                        for k in range(KC):
                            mm = pe.transpose(bank[:, k, i * T:(i + 1) * T], src[:, first + i, k * 128:(k + 1) * 128],
                                              ident[0:T, 0:T])
                    mm.then_inc(sem[ready], 1)

            def norm(name, chunks=pairs(G)):
                turn_tiles(chunks, XH, "xt_ready", "xt_done")
                c.over(name)

            last = [None]

            def pair_free(stage, n):
                if n == 0 and last[0] != (FIRST[stage] + 1) % 2:
                    wait(pe, sem["row_done"], c("row_done"))
                else:
                    wait(pe, sem["row_done"], c("row_done") + n - 1)
                last[0] = (FIRST[stage] + n) % 2

            def rows(stage, lhs, rhs):
                for n, (off, tiles) in enumerate(pairs(G)):
                    pair_free(stage, n)
                    for i in range(tiles):
                        for k in range(KC):
                            mm = pe.matmul(pair_bank(stage, n)[0:T, i * D:(i + 1) * D], lhs(k, off + i), rhs(k),
                                           start=(k == 0), stop=(k == KC - 1))
                    mm.then_inc(sem["row_ready"], 1)

            def support(g):
                pe.wait_ge(sem["xt_done"], c("xt_done"))
                last[0] = None
                rows("support", lambda k, i: XT[:, k, i * T:(i + 1) * T], lambda k: WG[:, k, :])
                c.over("support")

            def prep_qk(l):
                pe.wait_ge(sem["w_qk"], c("w_qk") + 16)
                pe.wait_ge(sem["lb_ready"], c("lb_ready"))
                wait(pe, sem["row_done"], c("row_done"))
                for k in range(KC):
                    pe.matmul(ROW[0][0:T, 0:D], LB[:, k, :], WQK[:, k, 0:D], start=(k == 0), stop=(k == KC - 1))
                for m in range(KC):
                    for k in range(KC):
                        mm = pe.matmul(ROW[1][:, m:m + 1], WQK[:, k, D + m * 128:D + (m + 1) * 128], LB[:, k, 0:1],
                                       start=(k == 0), stop=(k == KC - 1))
                mm.then_inc(sem["bqk_ready"], 1)
                c.over("prep_qk")

            def qk_set():
                pe.wait_ge(sem["qk_ready"], c("qk_ready"))

            def keys(g):
                n = 0
                for off, tiles in HALF:
                    pe.wait_ge(sem["xt_done"], c("xt_done") - NP + len(pairs(off + tiles)))
                    for m in range(KC):
                        wide_free(n)
                        for k in range(KC):
                            mm = pe.matmul(WIDE[n % 2][:, 0:tiles * T], WQK[:, k, D + m * 128:D + (m + 1) * 128],
                                           XT[:, k, off * T:(off + tiles) * T], start=(k == 0), stop=(k == KC - 1))
                        mm.then_inc(sem["wide_ready"], 1)
                        n += 1
                c.over("keys")

            def queries(g):
                last[0] = None
                rows("queries", lambda k, i: XT[:, k, i * T:(i + 1) * T], lambda k: WQK[:, k, 0:D])
                c.over("queries")

            def turn_q(g):
                pe.wait_ge(sem["qn_ready"], c("qn_ready"))
                turn_tiles(pairs(G), QZ, "qt_ready", "qt_done")
                c.over("turn_q")

            def prep_biases(l):
                pe.wait_ge(sem["w_rest"], c("w_rest"))
                wait(pe, sem["row_done"], c("row_done"))
                ps = ROW[0]
                for j in range(KC):
                    for k in range(KC):
                        pe.matmul(ps[:, j:j + 1], WVO[:, k, j * 128:(j + 1) * 128], COLS[:, span(l * 16 + 2 + k, 1)],
                                  start=(k == 0), stop=(k == KC - 1))
                for j in range(FB):
                    for k in range(KC):
                        mm = pe.matmul(ps[:, 8 + j:9 + j], W1[:, k, j * 128:(j + 1) * 128], COLS[:, span(l * 16 + 6 + k, 1)],
                                       start=(k == 0), stop=(k == KC - 1))
                mm.then_inc(sem["bv_ready"], 1)
                c.over("prep_biases")

            def prep_m():
                pe.wait_ge(sem["bvm_ready"], c("bvm_ready"))
                for j in range(KC):
                    pe.matmul(ROW[1][:, j * D:(j + 1) * D], BVM[:, j * 128:(j + 1) * 128], WVO[:, j, D:2 * D],
                              start=True, stop=False)
                    mm = pe.matmul(ROW[1][:, j * D:(j + 1) * D], eighth[:, :], BO[:, :], start=False, stop=True)
                mm.then_inc(sem["b2m_ready"], 1)
                c.over("prep_m")

            def open_():
                wait(pe, sem["agg_done"], c("agg_done"))
                for m in range(KC):
                    pe.matmul(ACC[m][:, 0:D], zeros[:, 0:128], zeros[:, 0:D], start=True, stop=False,
                              skip_group_check=True)

            def context(g):
                def turn(i):
                    pe.wait_ge(sem["kexp"], c("kexp") + KC)
                    if i == 0:
                        turns_free()
                    elif i >= 2:
                        pe.wait_ge(sem["kt_done"], c("kt_done") + i - 1)
                    bank = TURN[i % 2]
                    for k in range(KC):
                        mm = pe.transpose(bank[0:T, k * 128:(k + 1) * 128], KE[:, k, i * T:(i + 1) * T], ident[:, :])
                    mm.then_inc(sem["kt_ready"], 1)

                def add(i):
                    pe.wait_ge(sem["kt_done"], c("kt_done") + i + 1)
                    pe.wait_ge(sem["bxh_ready"], c("bxh_ready") + i + 1)
                    for m in range(KC):
                        mm = pe.matmul(ACC[m][:, 0:D], XH[:, i, m * 128:(m + 1) * 128], KT[:, i % 2, :],
                                       start=False, stop=False, skip_group_check=True)
                    mm.then_inc(sem["g_acc"], 1)
                turn(0)
                for i in range(1, G):
                    turn(i)
                    add(i - 1)
                add(G - 1)
                c.over("context")


            def fold():
                last[0] = None
                for m in range(KC):
                    mm = pe.matmul(ACC[m][:, 0:D], zeros[:, 0:128], zeros[:, 0:D], start=False, stop=True,
                                   skip_group_check=True)
                mm.then_inc(sem["g_closed"], 1)
                pe.wait_ge(sem["gs_ready"], c("gs_ready") + 1)
                turns_free()
                for j in range(KC):
                    cols_ = slice(j * 128, (j + 1) * 128)
                    for k in range(KC):
                        mm = pe.matmul(TP[:, cols_], WVO[:, k, cols_], GS[:, k, cols_], start=(k == 0), stop=(k == KC - 1))
                mm.then_inc(sem["cm_ready"], 1)
                pe.wait_ge(sem["cm_done"], c("cm_done") + 1)
                pe.wait_ge(sem["rest_ready"], c("rest_ready"))
                for j in range(KC):
                    mm = pe.matmul(ROW[j][:, 0:D], CM[:, j * 128:(j + 1) * 128], WVO[:, j, D:2 * D], start=True, stop=True)
                mm.then_inc(sem["m_ready"], 1)
                pe.wait_ge(sem["ms_done"], c("ms_done") + 1)
                c.over("fold")

            def attend(g):
                pe.wait_ge(sem["qs_ready"], c("qs_ready"))
                rows("attend", lambda k, i: QS[:, k, i * T:(i + 1) * T], lambda k: MS[:, k, :])
                c.over("attend")

            def up(g, part):
                h, first, end = UP[part]
                off, tiles = HALF[h]
                last[0] = None
                if part == "0a":
                    pe.wait_ge(sem["xt_done"], c("xt_done") - NP + len(pairs(tiles)))
                else:
                    pe.wait_ge(sem["xt_done"], c("xt_done"))
                for j in range(first, end):
                    wide_free(j - first)
                    for k in range(KC):
                        mm = pe.matmul(WIDE[j % 2][:, 0:tiles * T], W1[:, k, j * 128:(j + 1) * 128],
                                       KX[:, k, span(g * GW + off * T, tiles * T)], start=(k == 0), stop=(k == KC - 1))
                    mm.then_inc(sem["wide_ready"], 1)
                c.over(f"up{part}")

            def down(g, h):
                off, tiles = HALF[h]
                pe.wait_ge(sem["wide_done"], c("wide_done") - (FB if h == 0 else 0))
                for n, (first, tiles_) in enumerate(pairs(tiles)):
                    pair_free(f"down{h}", n)
                    for i in range(tiles_):
                        at = slice((first + i) * T, (first + i + 1) * T)
                        for j in range(FB):
                            mm = pe.matmul(pair_bank(f"down{h}", n)[0:T, i * D:(i + 1) * D], UT[h][:, j, at], W2[:, j, :],
                                           start=(j == 0), stop=(j == FB - 1))
                    mm.then_inc(sem["row_ready"], 1)
                c.over(f"down{h}")

            def edges(p):
                pe.wait_ge(sem["hot_ready"], c("hot_ready"))
                pe.wait_ge(sem[f"msgs{p}"], c(f"msgs{p}") + 16 * HU - 1)
                wait(pe, sem["agg_done"], c("agg_done"))
                for i in range(HU):
                    pe.matmul(agg_bank(i), HOT[:, i, :], MSG[:, p * HU + i, :], start=True,
                              stop=True).then_inc(sem["agg_ready"], 1)
                c.over(f"edges{p}")

            pe.wait_ge(sem["consts"], 1)
            pe.wait_ge(sem["e_counted"], 1)
            pe.matmul(P[6][:, 0:NB], TRI[:, :], CNT[:, 0:NB], start=True, stop=True)
            pe.matmul(P[6][:, 32:32 + NB], ones[:, :], CNT[:, 0:NB], start=True, stop=True).then_inc(sem["e_offset"], 1)
            pe.wait_ge(sem["e_ends"], 1)
            pe.matmul(P[7][0:NT, 0:1], END[0:1, 0:NT], ones[0:1, 0:1], start=True, stop=True).then_inc(sem["e_past"], 1)
            pe.wait_ge(sem["e_passed"], 1)
            pe.matmul(P[7][0:1, 0:NCH], ones[0:NT, 0:1], PAST[0:NT, :], start=True, stop=True).then_inc(sem["e_blocks"], 1)
            pe.wait_ge(sem["w_g"], 16)
            pe.wait_ge(sem["cols_in"], 16)

            layers(pe, c, {
                **idle_stages(c), "prep_qk": prep_qk, "qk_set": qk_set, "support": support,
                "norm_in": lambda g: norm("norm_in"), "norm_a": lambda g: norm("norm_a"),
                "norm_c": lambda g: norm("norm_c"), "keys": keys, "queries": queries, "turn_q": turn_q, "open": open_,
                "context": context, "prep_biases": prep_biases, "prep_m": prep_m, "fold": fold, "attend": attend,
                "up": up, "down": down, "edges": edges})

            pe.wait_ge(sem["fold_in"], FOLD_LOADS)
            pe.wait_ge(sem["agg_done"], NCH + 1)
            wait(pe, sem["row_done"], c("row_done"))
            for j in range(4):
                js = slice(j * 128, (j + 1) * 128)
                for m in range(KC):
                    pe.matmul(ACC[m][:, js], WXT[:, j, m * 128:(m + 1) * 128], BD, start=True, stop=True)
            pe.wait_ge(sem["f_lbx"], 1)
            for j in range(4):
                mm = pe.matmul(ROW[0][0:T, j * 128:(j + 1) * 128], LBX[:, j, :], BD, start=True, stop=True)
            mm.then_inc(sem["f_fold"], 1)
            c.over("calc_f")
            norm("norm_f", SINGLE)
            pe.wait_ge(sem["f_ready"], 1)
            for m in range(KC):
                pe.matmul(ACC[m][:, :], zeros[:, 0:128], zeros[:, :], start=True, stop=False, skip_group_check=True)

            def slices(g, more):
                def logit(i):
                    row_free(i)
                    pe.wait_ge(sem["xt_done"], c("xt_done") - G + i + 1)
                    for k in range(KC):
                        mm = pe.matmul(ROW[i % 2][0:T, :], XT[:, k, i * T:(i + 1) * T], WXS[:, k, :],
                                       start=(k == 0), stop=(k == KC - 1))
                    mm.then_inc(sem["row_ready"], 1)

                def token(i):
                    pe.wait_ge(sem["s_ready"], c("s_ready") + i + 1)
                    for m in range(KC):
                        mm = pe.matmul(ACC[m][:, :], XH[:, i, m * 128:(m + 1) * 128],
                                       S[:, span(g * G + i, 1), :].rearrange("p a s -> p (a s)"),
                                       start=False, stop=False, skip_group_check=True)
                    mm.then_inc(sem["tok"], 1)

                def turn(i):
                    if more:
                        if i == 0:
                            wait(pe, sem["xt_done"], c("xt_done"))
                        elif i >= 2:
                            pe.wait_ge(sem["xt_done"], c("xt_done") + i - 1)
                        pe.wait_ge(sem["xh_ready"], c("xh_ready") + i + 1)
                        for k in range(KC):
                            mm = pe.transpose(turned(TURN[i % 2])[:, k, :], XH[:, i, k * 128:(k + 1) * 128], ident[0:T, 0:T])
                        mm.then_inc(sem["xt_ready"], 1)
                logit(0)
                logit(1)
                for i in range(2, G):
                    logit(i)
                    token(i - 2)
                    if i >= 3:
                        turn(i - 3)
                for i in range(G - 2, G):
                    token(i)
                    turn(i - 1)
                turn(G - 1)
                c.over("slices" if more else "slices_last")
            with c.loop(pe, 0, NG - 1, ["slices"]) as g:
                slices(g, True)
            slices(NG - 1, False)
            for m in range(KC):
                mm = pe.matmul(ACC[m][:, :], zeros[:, 0:128], zeros[:, :], start=False, stop=True, skip_group_check=True)
            mm.then_inc(sem["y_ready"], 1)
            pe.wait_ge(sem["f_in"], F_LOADS)
            pe.wait_ge(sem["s_summed"], NT + 1)
            wait(pe, sem["row_done"], c("row_done"))
            for h in range(FH):
                mm = pe.matmul(TP[0:FG, h:h + 1], SSUM[:, h * FG:(h + 1) * FG], ones[0:T, 0:1], start=True, stop=True)
            mm.then_inc(sem["n_ready"], 1)
            pe.wait_ge(sem["y_ready"], 2)
            for h in range(FH):
                for k in range(KC):
                    mm = pe.matmul(ROW[0][0:FG, h * FD:(h + 1) * FD], YT[:, k, h * FG:(h + 1) * FG],
                                   WFX[:, k, h * FD:(h + 1) * FD], start=(k == 0), stop=(k == KC - 1))
            mm.then_inc(sem["tk_ready"], 1)
            pe.wait_ge(sem["tk_done"], 1)
            for h in range(FH):
                mm = pe.transpose(QP[0:FD, h * FG:(h + 1) * FG], TK[:, h * FD:(h + 1) * FD], ident[0:FG, 0:FG])
            mm.then_inc(sem["tkt_ready"], 1)
            pe.wait_ge(sem["tkt_done"], 1)
            pe.matmul(WIDE[0][0:FD, :], WQKV[:, 0:FD], TKT, start=True, stop=True)
            pe.matmul(WIDE[1][0:FD, :], WQKV[:, FD:2 * FD], TKT, start=True, stop=True)
            for h in range(FH):
                mm = pe.matmul(ROW[1][0:FG, h * FD:(h + 1) * FD], TKT[:, h * FG:(h + 1) * FG], WQKV[:, 2 * FD:3 * FD],
                               start=True, stop=True)
            mm.then_inc(sem["qkv_ready"], 1)
            pe.wait_ge(sem["qkv_done"], 1)
            for h in range(FH):
                hs = slice(h * FG, (h + 1) * FG)
                mm = pe.matmul(ROW[0][0:FG, hs], FQT[:, hs], FKT[:, hs], start=True, stop=True)
            mm.then_inc(sem["aw_ready"], 1)
            pe.wait_ge(sem["aw_done"], 1)
            for h in range(FH):
                hs = slice(h * FG, (h + 1) * FG)
                mm = pe.transpose(QP[0:FG, hs], AW[:, hs], ident[0:FG, 0:FG])
            mm.then_inc(sem["awt_ready"], 1)
            pe.wait_ge(sem["awt_done"], 1)
            for h in range(FH):
                hs = slice(h * FG, (h + 1) * FG)
                mm = pe.matmul(ROW[1][0:FD, hs], FV[:, h * FD:(h + 1) * FD], AWT[:, hs], start=True, stop=True)
            mm.then_inc(sem["o_ready"], 1)
            pe.wait_ge(sem["o_done"], 1)
            for j in range(4):
                for a in range(2):
                    mm = pe.matmul(ACC[j // 2][:, (j % 2) * D:(j % 2 + 1) * D], OP[:, 2 * j + a, :], WOUT[:, 2 * j + a, :],
                                   start=(a == 0), stop=(a == 1))
            mm.then_inc(sem["m2_ready"], 1)
            pe.wait_ge(sem["m2_done"], 1)
            with c.loop(pe, 0, NG, ["finish"]) as g:
                def turn(i):
                    pe.wait_ge(sem["sc_ready"], c("sc_ready") + i + 1)
                    pe.wait_ge(sem["st_done"], c("st_done") + i)
                    for j in range(4):
                        mm = pe.transpose(TP[:, j * T:(j + 1) * T], SC[i % 2][:, j * 128:(j + 1) * 128], ident[0:T, 0:T])
                    mm.then_inc(sem["st_ready"], 1)

                def put(i):
                    pe.wait_ge(sem["st_done"], c("st_done") + i + 1)
                    row_free(i)
                    for j in range(4):
                        mm = pe.matmul(ROW[i % 2][0:T, 0:D], STT[i % 2][:, j, :], M2[:, j, :], start=(j == 0), stop=(j == 3))
                    mm.then_inc(sem["row_ready"], 1)
                turn(0)
                for i in range(1, G):
                    turn(i)
                    put(i - 1)
                put(G - 1)
                c.over("finish")

        @block.scalar
        def _(act):
            c = Count(1)

            def norm(name, g, out_, readers, chunks=pairs(G)):
                for sem_ in readers:
                    wait(act, sem[sem_], c(sem_))
                for n, (first, tiles) in enumerate(chunks):
                    act.wait_ge(sem["xt_ready"], c("xt_ready") + n + 1)
                    act.activation(out_(g, first, tiles), turned(TURN[n % 2], tiles), ACT.Copy).then_inc(sem["xt_done"], 1)
                c.over(name)

            def support(g):
                wait(act, sem["sup_stored"], c("sup_stored"))
                for n, (first, tiles) in enumerate(pairs(G)):
                    act.wait_ge(sem["row_ready"], c("row_ready") + n + 1)
                    act.activation(QZ[:, first:first + tiles, :], two_rows(pair_bank("support", n), tiles),
                                   ACT.Copy).then_inc(sem["row_done"], 1)
                c.over("support")

            def to_xt(g, i, tiles=1):
                return XT[:, :, i * T:(i + tiles) * T]

            def to_kx(g, i, tiles):
                return KX[:, :, span(g * GW + i * T, tiles * T)]

            def keys(g):
                n = 0
                for off, tiles in HALF:
                    for m in range(KC):
                        act.wait_ge(sem["wide_ready"], c("wide_ready") + n + 1)
                        act.activation(KX[:, m, span(g * GW + off * T, tiles * T)], WIDE[n % 2][:, 0:tiles * T],
                                       ACT.Identity, bias=BK[:, m:m + 1]).then_inc(sem["wide_done"], 1)
                        n += 1
                c.over("keys")

            def soften():
                act.wait_ge(sem["qz_ready"], c("qz_ready"))
                act.activation(QZ[:, :, :], QZ[:, :, :], ACT.Exp, scale=QSCALE).then_inc(sem["qe_ready"], 1)
                c.over("soften")

            def fetch_q(g):
                act.wait_ge(sem["qt_done"], c("qt_done"))
                act.wait_ge(sem["row_ready"], c("row_ready"))
                act.wait_ge(sem["kt_ready"], c("kt_ready"))
                act.activation(QS[:, :, :], QT[:, :, span(g * GW, GW)], ACT.Copy).then_inc(sem["qs_ready"], 1)
                c.over("fetch_q")

            def turn_q(g):
                wait(act, sem["qs_ready"], c("qs_ready"))
                for n, (first, tiles) in enumerate(pairs(G)):
                    act.wait_ge(sem["qt_ready"], c("qt_ready") + n + 1)
                    act.activation(QT[:, :, span(g * GW + first * T, tiles * T)], turned(TURN[n % 2], tiles),
                                   ACT.Copy).then_inc(sem["qt_done"], 1)
                c.over("turn_q")

            def context(g):
                act.wait_ge(sem["kmax_ready"], c("kmax_ready"))
                wait(act, sem["kt_ready"], c("kt_ready"))
                for k in range(KC):
                    act.activation(KE[:, k, :], KX[:, k, span(g * GW, GW)], ACT.Exp, bias=KB[:, k:k + 1], scale=QSCALE,
                                   accum_out=KS[:, k, span(g, 1)]).then_inc(sem["kexp"], 1)
                for i in range(G):
                    act.wait_ge(sem["kt_ready"], c("kt_ready") + i + 1)
                    if i != 1:
                        wait(act, sem["g_acc"], c("g_acc") + max(i - 1, 0))
                    act.activation(KT[:, i % 2, :], TURN[i % 2][0:T, 0:D], ACT.Copy).then_inc(sem["kt_done"], 1)
                c.over("context")

            def up(g, part):
                h, first, end = UP[part]
                off, tiles = HALF[h]
                for j in range(first, end):
                    act.wait_ge(sem["wide_ready"], c("wide_ready") + j - first + 1)
                    act.activation(UT[h][:, j, :], WIDE[j % 2][:, 0:tiles * T], ACT.Gelu,
                                   bias=B1[:, j:j + 1]).then_inc(sem["wide_done"], 1)
                c.over(f"up{part}")

            def sorted_():
                act.wait_ge(sem["e_placed"], 1)

            layers(act, c, {
                **idle_stages(c), "sorted": sorted_, "support": support, "norm_in": lambda g: norm("norm_in", g, to_xt, ["row_ready"]),
                "norm_a": lambda g: norm("norm_a", g, to_xt, ["row_ready", "wide_ready"]),
                "norm_c": lambda g: norm("norm_c", g, to_kx, ["kt_ready"]),
                "keys": keys, "soften": soften, "turn_q": turn_q, "context": context, "fetch_q": fetch_q, "up": up})

            c.over("calc_f")
            norm("norm_f", 0, to_xt, ["row_ready"], SINGLE)

            def slices(g, more):
                def exp(i):
                    act.wait_ge(sem["sz_ready"], c("sz_ready") + i + 1)
                    for h in range(FH):
                        z = SZ[i % 2][:, h * FG:(h + 1) * FG]
                        ins = act.activation(z, z, ACT.Exp, bias=SNEG[i % 2][:, h:h + 1], accum_out=SSD[i % 2][:, h:h + 1])
                    ins.then_inc(sem["se_ready"], 1)

                def turned_tile(i):
                    if more:
                        act.wait_ge(sem["row_ready"], c("row_ready") + i + 1)
                        act.wait_ge(sem["xt_ready"], c("xt_ready") + i + 1)
                        act.activation(to_xt(g, i), turned(TURN[i % 2]), ACT.Copy).then_inc(sem["xt_done"], 1)
                for i in range(G):
                    exp(i)
                    if i >= 3:
                        turned_tile(i - 3)
                for i in range(G - 3, G):
                    turned_tile(i)
                c.over("slices" if more else "slices_last")
            with c.loop(act, 0, NG - 1, ["slices"]) as g:
                slices(g, True)
            slices(NG - 1, False)
            act.wait_ge(sem["az_ready"], 1)
            act.activation(AW, AW, ACT.Exp, scale=FD ** -0.5).then_inc(sem["ae_ready"], 1)
            with c.loop(act, 0, NG, ["finish"]) as g:
                for i in range(G):
                    act.wait_ge(sem["st_ready"], c("st_ready") + i + 1)
                    wait(act, sem["row_ready"], c("row_ready") + max(i - 1, 0))
                    act.activation(STT[i % 2], TP[:, 0:4 * T].rearrange("p (j t) -> p j t", j=4),
                                   ACT.Copy).then_inc(sem["st_done"], 1)
                c.over("finish")

        @block.vector
        def _(dve):
            c = Count(1)

            def step(ins):
                ins.then_inc(sem["dve_step"], 1)
                c.own["dve_step"] += 1
                dve.wait_ge(sem["dve_step"], c("dve_step"))

            def tiles_of(buf, g):
                return buf[:, span(g * G, G), :]

            def stats(g, src_):
                for i in range(G):
                    ins = dve.bn_stats(ST[:, i, :], src_[:, span(g * G + i, 1), :].rearrange("p a d -> p (a d)"))
                step(ins)
                apart(dve, sem["dve_waited"])
                for i in range(G):
                    ins = dve.bn_aggr(MV[:, i, :], ST[:, i, :])
                step(ins)
                rs, nm = RSTD[:, span(g * G, G)], NMR[:, span(g * G, G)]
                v, y, z = NW[:, 0, :], NW[:, 1, :], NW[:, 2, :]
                step(dve.tensor_scalar_add(v, MV[:, :, 1], EPS))
                step(dve.tensor_single_scalar(z.bitcast(I32), v.bitcast(I32), 1, ALU.logical_shift_right))
                step(dve.tensor_scalar(y.bitcast(I32), z.bitcast(I32), -1.0, MAGIC, ALU.mult, ALU.add))
                for n in range(3):
                    step(dve.scalar_tensor_tensor(z, y, -0.5, y, ALU.mult, ALU.mult))
                    step(dve.tensor_tensor(z, z, v, ALU.mult))
                    step(dve.scalar_tensor_tensor(rs if n == 2 else y, z, 1.5, y, ALU.add, ALU.mult))
                step(dve.scalar_tensor_tensor(nm, MV[:, :, 0], -1.0, rs, ALU.mult, ALU.mult))

            def calc(name, g, src_, keep=False, bias=None):
                wait(dve, sem["row_done"], c("row_done"))
                apart(dve, sem["dve_waited"])
                stats(g, src_)
                wait(dve, sem["xt_ready"], c("xt_ready"))
                wait(dve, sem["g_acc"], c("g_acc"))
                for i in range(G):
                    t = span(g * G + i, 1)
                    dve.tensor_scalar(XH[:, i, :], src_[:, t, :].rearrange("p a d -> p (a d)"), RSTD[:, t], NMR[:, t],
                                      ALU.mult, ALU.add).then_inc(sem["xh_ready"], 1)
                    if keep:
                        dve.tensor_scalar(X[:, t, :].rearrange("p a d -> p (a d)"), src_[:, t, :].rearrange("p a d -> p (a d)"),
                                          RSTD[:, t], NMR[:, t], ALU.mult, ALU.add)
                if bias is not None:
                    dve.wait_ge(sem["xh_ready"], c("xh_ready") + G)
                    step(dve.tensor_tensor(tiles_of(X, g), tiles_of(X, g), bias.unsqueeze(1).broadcast_to([T, G, D]), ALU.add))
                    apart(dve, sem["dve_waited"])
                c.rest(name)

            def add_rows(stage, g, off, tiles):
                for n, (first, tiles_) in enumerate(pairs(tiles)):
                    x_ = X[:, span(g * G + off + first, tiles_), :]
                    dve.wait_ge(sem["row_ready"], c("row_ready") + n + 1)
                    dve.tensor_tensor(x_, two_rows(pair_bank(stage, n), tiles_), x_, ALU.add).then_inc(sem["row_done"], 1)

            def spread_b(l):
                for k in range(KC):
                    ins = dve.tensor_scalar(LB[:, k, :], ones[:, 0:T], COLS[:, span(l * 16 + 2 + k, 1)], None, ALU.mult)
                ins.then_inc(sem["lb_ready"], 1)
                c.rest("spread_b")

            def prep_qk(l):
                dve.wait_ge(sem["bqk_ready"], c("bqk_ready") + 1)
                wait(dve, sem["wide_done"], c("wide_done"))
                dve.tensor_copy(BQ[:, :], ROW[0][0:T, 0:D])
                dve.tensor_copy(BK[:, :], ROW[1][:, 0:KC])
                for k in range(KC):
                    ins = dve.tensor_scalar(WQK[:, k, :], WQK[:, k, :], COLS[:, span(l * 16 + k, 1)], None, ALU.mult)
                ins.then_inc(sem["qk_ready"], 1)
                c.rest("prep_qk")

            def keys(g):
                dve.wait_ge(sem["wide_done"], c("wide_done") + 2 * KC)
                step(dve.tensor_reduce(MX[:, :, span(g, 1)], KX[:, :, span(g * GW, GW)], axis=AX_X, op=ALU.max))
                c.rest("keys")

            def queries(g):
                wait(dve, sem["qt_ready"], c("qt_ready"))
                wait(dve, sem["sup_stored"], c("sup_stored"))
                for n, (first, tiles) in enumerate(pairs(G)):
                    dve.wait_ge(sem["row_ready"], c("row_ready") + n + 1)
                    dve.tensor_tensor(QZ[:, first:first + tiles, :], two_rows(pair_bank("queries", n), tiles),
                                      BQ[:, :].unsqueeze(1).broadcast_to([T, tiles, D]), ALU.add).then_inc(sem["row_done"], 1)
                z = QZ[:, :, :].rearrange("p g (h d) -> p (g h) d", d=DH)
                m = QM[:, :].unsqueeze(2).broadcast_to([T, G * HEADS, DH])
                dve.wait_ge(sem["row_done"], c("row_done") + NP)
                step(dve.tensor_reduce(QM[:, :], z, axis=AX_X, op=ALU.max))
                dve.tensor_tensor(z, z, m, ALU.subtract).then_inc(sem["qz_ready"], 1)
                c.rest("queries")

            def soften():
                z = QZ[:, :, :].rearrange("p g (h d) -> p (g h) d", d=DH)
                m = QM[:, :].unsqueeze(2).broadcast_to([T, G * HEADS, DH])
                dve.wait_ge(sem["qe_ready"], c("qe_ready") + 1)
                step(dve.tensor_reduce(QM[:, :], z, axis=AX_X, op=ALU.add))
                step(dve.reciprocal(QM[:, :], QM[:, :]))
                dve.tensor_tensor(z, z, m, ALU.mult).then_inc(sem["qn_ready"], 1)
                c.rest("soften")

            def kmax():
                wait(dve, sem["kexp"], c("kexp"))
                step(dve.tensor_reduce(KB[:, :], MX[:, :, :], axis=AX_X, op=ALU.max))
                dve.tensor_scalar(KB[:, :], KB[:, :], -QSCALE, None, ALU.mult).then_inc(sem["kmax_ready"], 1)
                c.rest("kmax")

            def prep_biases(l):
                dve.wait_ge(sem["bv_ready"], c("bv_ready") + 1)
                wait(dve, sem["wide_done"], c("wide_done"))
                dve.tensor_tensor(B1[:, :], ROW[0][:, 8:8 + FB], COLS[:, span(l * 16 + 8, FB)], ALU.add)
                step(dve.tensor_copy(BV[:, :], ROW[0][:, 0:KC]))
                for j in range(KC):
                    ins = dve.tensor_scalar(BVM[:, j * 128:(j + 1) * 128], MASK[:, j * 128:(j + 1) * 128], BV[:, j:j + 1],
                                            None, ALU.mult)
                ins.then_inc(sem["bvm_ready"], 1)
                for k in range(KC):
                    dve.tensor_scalar(WVO[:, k, 0:D], WVO[:, k, 0:D], COLS[:, span(l * 16 + k, 1)], None, ALU.mult)
                    dve.tensor_scalar(W1[:, k, :], W1[:, k, :], COLS[:, span(l * 16 + 4 + k, 1)], None, ALU.mult)
                c.rest("prep_biases")

            def prep_m():
                dve.wait_ge(sem["b2m_ready"], c("b2m_ready") + 1)
                dve.tensor_copy(B2M[:, :, :], ROW[1][:, :].rearrange("p (k n) -> p k n", k=KC)).then_inc(sem["rest_ready"], 1)
                c.rest("prep_m")

            def context(g):
                wait(dve, sem["xt_ready"], c("xt_ready"))
                wait(dve, sem["g_acc"], c("g_acc"))
                for i in range(G):
                    t = span(g * G + i, 1)
                    dve.tensor_scalar(XH[:, i, :], X[:, t, :].rearrange("p a d -> p (a d)"), RSTD[:, t], NMR[:, t],
                                      ALU.mult, ALU.add).then_inc(sem["bxh_ready"], 1)
                c.rest("context")

            def fold():
                dve.wait_ge(sem["kexp"], c("kexp"))
                step(dve.tensor_reduce(RS[:, 0, :], KS[:, :, :], axis=AX_X, op=ALU.add))
                step(dve.reciprocal(RS[:, 1, :], RS[:, 0, :]))
                dve.wait_ge(sem["g_closed"], c("g_closed") + 1)
                for m in range(KC):
                    ins = dve.tensor_copy(GS[:, m, :], ACC[m][:, 0:D])
                ins.then_inc(sem["gs_ready"], 1)
                dve.wait_ge(sem["cm_ready"], c("cm_ready") + 1)
                dve.tensor_tensor(CM[:, :], TP[:, 0:D], MASK[:, :], ALU.mult).then_inc(sem["cm_done"], 1)
                dve.wait_ge(sem["m_ready"], c("m_ready") + 1)
                for j in range(KC):
                    ins = dve.scalar_tensor_tensor(MS[:, j, :], ROW[j][:, 0:D], RS[:, 1, j:j + 1], B2M[:, j, :],
                                                   ALU.mult, ALU.add)
                ins.then_inc(sem["ms_done"], 1)
                c.rest("fold")

            def attend(g):
                add_rows("attend", g, 0, G)
                c.rest("attend")

            def down(g, h):
                add_rows(f"down{h}", g, *HALF[h])
                c.rest(f"down{h}")

            def hot(chunk, i):
                rec = REC3[:, span(chunk, 1), :].rearrange("p a r -> p (a r)")
                dve.tensor_scalar(HOT[:, i, :], IOTA[:, 0:T], rec[:, 1:2], rec[:, 2:3], ALU.is_equal,
                                  ALU.mult).then_inc(sem["hot_ready"], 1)

            def edges_first():
                dve.wait_ge(sem["e_back"], 16)
                for i in range(HU):
                    hot(c("agg_ready") + (i - 1), i)
                c.rest("edges_first")

            def edges(p):
                chunk = [c("agg_ready") + (i - 1) for i in range(HU)]
                tile = [dve.value_load(BLK[0:1, span(chunk[i], 1)], min_val=0, max_val=NT - 1) for i in range(HU)]
                for i in range(HU):
                    a = AGG[:, bass.ds(tile[i], 1), :].rearrange("p a d -> p (a d)")
                    dve.wait_ge(sem["agg_ready"], c("agg_ready") + (i // 2 + 1) * 2)
                    wait(dve, sem["agg_done"], c("agg_done") + i)
                    dve.tensor_tensor(a, agg_bank(i), a, ALU.add).then_inc(sem["agg_done"], 1)
                    hot(chunk[i] + HU, i)
                c.rest(f"edges{p}")

            dve.memset(RANK, 0.0)
            dve.wait_ge(sem["consts"], 1)
            dve.wait_ge(sem["e_bucketed"], 1)
            dve.tensor_copy(BKT16, BKT).then_inc(sem["e_short"], 1)
            dve.wait_ge(sem["e_short"], 1)
            with dve.Fori(0, NB // 2) as r:
                n = r * 8
                two = ((r * 2, HIT, SCAN), (r * 2 + 1, HIT2, SCAN2))
                for b, hit, _ in two:
                    dve.tensor_scalar(hit, BKT16, BT[:, span(b, 1)], None, ALU.is_equal).then_inc(sem["e_rank"], 1)
                for i, (_, hit, scan) in enumerate(two):
                    dve.wait_ge(sem["e_rank"], n + 2 + i)
                    dve.tensor_tensor_scan(scan, hit, hit, 0.0, ALU.add, ALU.bypass).then_inc(sem["e_rank"], 1)
                for i, (b, hit, scan) in enumerate(two):
                    dve.wait_ge(sem["e_rank"], n + 4 + i)
                    dve.tensor_copy(CNT[:, span(b, 1)], scan[:, EC - 1:EC])
                    dve.tensor_tensor(hit, hit, scan, ALU.mult).then_inc(sem["e_rank"], 1)
                for i, (_, hit, _) in enumerate(two):
                    dve.wait_ge(sem["e_rank"], n + 6 + 2 * i)
                    dve.tensor_tensor(RANK, RANK, hit, ALU.add).then_inc(sem["e_rank"], 1)
                dve.wait_ge(sem["e_rank"], n + 9)
            dve.sem_inc(sem["e_counted"], 1)
            dve.wait_ge(sem["e_offset"], 1)
            step(dve.tensor_scalar(TOTI[:, 0:NB], P[6][:, 32:32 + NB], 127.0, None, ALU.add))
            step(dve.tensor_scalar(TOTI[:, 0:NB], TOTI[:, 0:NB], 7, 7, ALU.logical_shift_right, ALU.logical_shift_left))
            step(dve.tensor_copy(TOT[:, 0:NB], TOTI[:, 0:NB]))
            step(dve.tensor_tensor_scan(END[:, 0:NB], TOT[:, 0:NB], TOT[:, 0:NB], 0.0, ALU.add, ALU.bypass))
            step(dve.tensor_tensor(BASE[:, 0:NB], END[:, 0:NB], TOT[:, 0:NB], ALU.subtract))
            step(dve.scalar_tensor_tensor(OFF[:, 0:NB], P[6][:, 0:NB], -1.0, BASE[:, 0:NB], ALU.add, ALU.add))
            dve.sem_inc(sem["e_ends"], 1)
            dve.wait_ge(sem["e_past"], 1)
            step(dve.tensor_scalar(ENDC[0:NT, 0:1], P[7][0:NT, 0:1], 1.0 / 128, None, ALU.mult))
            dve.tensor_scalar(PAST[0:NT, :], IOTA[0:NT, 0:NCH], ENDC[0:NT, 0:1], None, ALU.is_ge).then_inc(sem["e_passed"], 1)
            dve.wait_ge(sem["e_blocks"], 1)
            step(dve.tensor_scalar(BLK[:, :], P[7][0:1, 0:NCH], float(NT - 1), None, ALU.min))

            dve.wait_ge(sem["x_in"], 16)
            dve.wait_ge(sem["cols_in"], 16)
            layers(dve, c, {
                **idle_stages(c), "spread_b": spread_b, "prep_qk": prep_qk, "prep_biases": prep_biases, "prep_m": prep_m,
                "calc_in": lambda g: calc("calc_in", g, AGG, keep=True), "calc_a": lambda g: calc("calc_a", g, X),
                "calc_c": lambda g: calc("calc_c", g, X, bias=BB2[:, :]),
                "keys": keys, "queries": queries, "soften": soften, "kmax": kmax, "context": context, "fold": fold,
                "attend": attend, "down": down, "edges_first": edges_first, "edges": edges})

            dve.wait_ge(sem["fold_in"], FOLD_LOADS)
            step(dve.tensor_scalar(TI, TEMP, 0.1, 5.0, ALU.max, ALU.min))
            step(dve.reciprocal(TI, TI))
            for j in range(4):
                ins = dve.tensor_scalar(LBX[:, j, :], ones[:, 0:T], BXC[:, j:j + 1], None, ALU.mult)
            ins.then_inc(sem["f_lbx"], 1)
            dve.wait_ge(sem["x_summed"], c("x_summed") + 1)
            calc("calc_f", 0, X)
            c.over("norm_f")
            dve.wait_ge(sem["f_fold"], 1)

            def heads(a):
                return a.rearrange("p (h s) -> p h s", h=FH)

            def over(a, parts):
                return a.unsqueeze(2).broadcast_to([parts, FH, FG])
            for m in range(KC):
                dve.tensor_tensor(heads(WXS[:, m, :]), heads(ACC[m][:, :]), over(TI, 128), ALU.mult)
            step(dve.tensor_tensor(heads(LBI), heads(ROW[0][0:T, :]), BSL.unsqueeze(1).broadcast_to([T, FH, FG]), ALU.add))
            dve.tensor_tensor(heads(LBI), heads(LBI), over(TI[0:T, :], T), ALU.mult).then_inc(sem["f_ready"], 1)
            dve.wait_ge(sem["f_ready"], 1)

            def slices(g, more):
                def before(i):
                    z = SZ[i % 2]
                    dve.wait_ge(sem["row_ready"], c("row_ready") + i + 1)
                    wait(dve, sem["s_ready"], c("s_ready") + max(i - 1, 0))
                    dve.tensor_tensor(z, ROW[i % 2][0:T, :], LBI, ALU.add).then_inc(sem["row_done"], 1)
                    dve.wait_ge(sem["row_done"], c("row_done") + i + 1)
                    step(dve.tensor_reduce(SMX, heads(z), axis=AX_X, op=ALU.max))
                    dve.tensor_scalar(SNEG[i % 2], SMX, -1.0, None, ALU.mult).then_inc(sem["sz_ready"], 1)

                def after(i):
                    z = SZ[i % 2]
                    dve.wait_ge(sem["se_ready"], c("se_ready") + i + 1)
                    step(dve.reciprocal(SSD[i % 2], SSD[i % 2]))
                    dve.tensor_tensor(heads(S[:, span(g * G + i, 1), :].rearrange("p a s -> p (a s)")), heads(z),
                                      over(SSD[i % 2], T), ALU.mult).then_inc(sem["s_ready"], 1)

                def next_stats():
                    if more:
                        dve.wait_ge(sem["x_summed"], c("x_summed") + 1)
                        apart(dve, sem["dve_waited"])
                        stats(g + 1, X)

                def next_tile(i):
                    if more:
                        t = span((g + 1) * G + i, 1)
                        dve.wait_ge(sem["tok"], c("tok") + i + 1)
                        dve.tensor_scalar(XH[:, i, :], X[:, t, :].rearrange("p a d -> p (a d)"), RSTD[:, t], NMR[:, t],
                                          ALU.mult, ALU.add).then_inc(sem["xh_ready"], 1)
                before(0)
                before(1)
                after(0)
                before(2)
                after(1)
                next_stats()
                next_tile(0)
                for i in range(3, G):
                    before(i)
                    after(i - 1)
                    next_tile(i - 2)
                after(G - 1)
                next_tile(G - 2)
                next_tile(G - 1)
                c.rest("slices" if more else "slices_last")
            with c.loop(dve, 0, NG - 1, ["slices"]) as g:
                slices(g, True)
            slices(NG - 1, False)
            dve.wait_ge(sem["y_ready"], 1)
            for m in range(KC):
                ins = dve.tensor_copy(YT[:, m, :], ACC[m][:, :])
            ins.then_inc(sem["y_ready"], 1)
            dve.wait_ge(sem["n_ready"], 1)
            step(dve.tensor_copy(NRM[:, :], TP[0:FG, 0:FH]))
            dve.tensor_tensor(heads(TK), heads(BFX), over(NRM[:, :], FG), ALU.mult)
            step(dve.tensor_scalar(DEN[:, :], NRM[:, :], 1e-5, None, ALU.add))
            step(dve.reciprocal(DEN[:, :], DEN[:, :]))
            dve.wait_ge(sem["tk_ready"], 1)
            step(dve.tensor_tensor(TK, ROW[0][0:FG, :], TK, ALU.add))
            dve.tensor_tensor(heads(TK), heads(TK), over(DEN[:, :], FG), ALU.mult).then_inc(sem["tk_done"], 1)
            dve.wait_ge(sem["tkt_ready"], 1)
            dve.tensor_copy(TKT, QP[0:FD, :]).then_inc(sem["tkt_done"], 1)
            dve.wait_ge(sem["qkv_ready"], 1)
            dve.tensor_copy(FQT, WIDE[0][0:FD, :])
            dve.tensor_copy(FKT, WIDE[1][0:FD, :])
            dve.tensor_copy(FV, ROW[1][0:FG, :]).then_inc(sem["qkv_done"], 1)
            dve.wait_ge(sem["aw_ready"], 1)
            step(dve.tensor_reduce(AMX[:, :], heads(ROW[0][0:FG, :]), axis=AX_X, op=ALU.max))
            dve.tensor_tensor(heads(AW), heads(ROW[0][0:FG, :]), over(AMX[:, :], FG), ALU.subtract).then_inc(sem["az_ready"], 1)
            dve.wait_ge(sem["ae_ready"], 1)
            step(dve.tensor_reduce(AMX[:, :], heads(AW), axis=AX_X, op=ALU.add))
            step(dve.reciprocal(AMX[:, :], AMX[:, :]))
            dve.tensor_tensor(heads(AW), heads(AW), over(AMX[:, :], FG), ALU.mult).then_inc(sem["aw_done"], 1)
            dve.wait_ge(sem["awt_ready"], 1)
            dve.tensor_copy(AWT, QP[0:FG, :]).then_inc(sem["awt_done"], 1)
            step(dve.memset(OP, 0.0))
            dve.wait_ge(sem["o_ready"], 1)
            for a in range(2):
                ins = dve.tensor_copy(OP[:, a::2, a * FG:(a + 1) * FG], heads(ROW[1][0:FD, :])[:, a::2, :])
            ins.then_inc(sem["o_done"], 1)
            dve.wait_ge(sem["m2_ready"], 1)
            for a in range(2):
                ins = dve.tensor_copy(M2[:, 2 * a:2 * a + 2, :], ACC[a][:, :].rearrange("p (j d) -> p j d", j=2))
            ins.then_inc(sem["m2_done"], 1)
            with c.loop(dve, 0, NG, ["finish"]) as g:
                step(dve.tensor_tensor(tiles_of(X, g), tiles_of(X, g), BOUT.unsqueeze(1).broadcast_to([T, G, D]), ALU.add))
                for i in range(G):
                    x_ = X[:, span(g * G + i, 1), :].rearrange("p a d -> p (a d)")
                    dve.wait_ge(sem["row_ready"], c("row_ready") + i + 1)
                    dve.tensor_tensor(x_, ROW[i % 2][0:T, 0:D], x_, ALU.add).then_inc(sem["row_done"], 1)
                c.rest("finish")


def kernel(**inputs):
    import numpy as np
    import concourse.bacc as bacc
    from concourse import mybir as mb
    from concourse.bass_utils import run_bass_kernel_spmd

    a = {k.removeprefix("L0_"): np.asarray(v) for k, v in inputs.items()}

    def edges(v, fill):
        return np.concatenate([v, np.full(128 * EC - E, fill, v.dtype)]).reshape(128, EC)

    def blocks(w):
        w = w.reshape(*w.shape[:-2], w.shape[-2] // 128, 128, w.shape[-1])
        return np.ascontiguousarray(np.swapaxes(w, -3, -2))

    def columns(v):
        return v.reshape(LAYERS, -1, 128).transpose(2, 0, 1)

    arrays = {
        "x": a["x"], "src": edges(a["src"], N), "dst": edges(a["dst"], 0), "ew": edges(a["edge_weight"], 0),
        "w_gnn": blocks(a["gnn_W"]),
        "w_qk": blocks(np.concatenate([a["mix_Wq"], a["mix_Wk"]], -1)),
        "w_vo": blocks(np.concatenate([a["mix_Wv"], a["mix_Wo"]], -1)),
        "w_1": blocks(a["mix_W1"]), "w_2": blocks(a["mix_W2"]),
        "cols": np.concatenate([columns(a[f"mix_{n}"]) for n in ("ln1_g", "ln1_b", "ln2_g", "ln2_b", "b1")], -1).reshape(128, -1),
        "b_o": a["mix_bo"], "b_2": a["mix_b2"],
        "w_fx": blocks(a["ffn_W_fx"]), "w_xt": blocks(np.ascontiguousarray(a["ffn_W_x"].T)),
        "w_slice": a["ffn_W_slice"], "b_slice": a["ffn_b_slice"][None], "b_fx": a["ffn_b_fx"][None],
        "b_x": a["ffn_b_x"].reshape(4, 128).T, "w_q": a["ffn_W_q"], "w_k": a["ffn_W_k"], "w_v": a["ffn_W_v"],
        "w_out": a["ffn_W_out"].reshape(FH, FD, D).transpose(1, 0, 2), "b_out": a["ffn_b_out"][None],
        "temp": a["ffn_temperature"].reshape(1, FH),
    }
    arrays = {f"in_{k}": np.ascontiguousarray(v) for k, v in arrays.items()}
    nc = bacc.Bacc("TRN2", target_bir_lowering=False, num_devices=1)
    args = [nc.dram_tensor(k, v.shape, mb.dt.from_np(v.dtype), kind="ExternalInput").ap() for k, v in arrays.items()]
    out = nc.dram_tensor("out_0", (N, D), mb.dt.float32, kind="ExternalOutput").ap()
    gps_layer(nc, *args, out)
    r = run_bass_kernel_spmd(nc, [arrays], core_ids=[0])
    return r.results[0]["out_0"]
```
